# Optimizing a Trainium2 kernel written in Bass

```python
import numpy as np
import jax
import jax.numpy as jnp

def _softmax(x, axis=-1):
    return jax.nn.softmax(x, axis=axis)

def _gelu(x):
    return jax.nn.gelu(x, approximate=True)

def _silu(x):
    return jax.nn.silu(x)

def _sigmoid(x):
    return jax.nn.sigmoid(x)

def _layernorm(x, axis=-1, eps=1e-05):
    m = jnp.mean(x, axis=axis, keepdims=True)
    v = jnp.var(x, axis=axis, keepdims=True)
    return (x - m) / jnp.sqrt(v + eps)

def _scatter_add(tgt, idx, src, axis=0):
    return tgt.at[idx].add(src)

def _segment_sum(src, seg, n):
    return jax.ops.segment_sum(src, seg, n)
kernel_name = 'mk_decoder_preln_d1_seqx_r4_0b03f2'

def setup_inputs(seed: int=0):
    np.random.seed(seed)
    _w = jnp.asarray

    def _rec_inputs():
        import jax
        import jax.numpy as jnp
        _rk = jax.random.key(seed)
        x = -0.000125 + 0.9999 * jax.random.normal(jax.random.fold_in(_rk, 1), (4, 512, 512), jnp.float32)
        _lenS = 512 - jax.random.randint(jax.random.fold_in(_rk, 7), (4,), 0, max(1, 512 // 4) + 1, jnp.int32)
        _lenS2 = 512 - jax.random.randint(jax.random.fold_in(_rk, 8), (4,), 0, max(1, 512 // 4) + 1, jnp.int32)
        fside_BxS2xS2_0 = -3.05549e-07 + 0.0199987 * jax.random.normal(jax.random.fold_in(_rk, 11), (4, 512, 512), jnp.float32)
        _ctx_1024P = jax.random.normal(jax.random.fold_in(_rk, 12), (4, 16, 256), jnp.float32)
        _ctx_1024c = jax.random.dirichlet(jax.random.fold_in(_rk, 512), 0.3 * jnp.ones((16,), jnp.float32), (4, 512))
        _ctx_1024t = jnp.einsum('bsk,bkd->bsd', _ctx_1024c, _ctx_1024P)
        _ctx_1024t = _ctx_1024t * jax.lax.rsqrt(jnp.mean(jnp.square(_ctx_1024t)) + 1e-12) * 0.953939
        ctx_1024 = 6.82029e-06 + 0.0200006 * (_ctx_1024t + 0.3 * jax.random.normal(jax.random.fold_in(_rk, 612), (4, 512, 256), jnp.float32))
        return (x, fside_BxS2xS2_0, ctx_1024)
    x, fside_BxS2xS2_0, ctx_1024 = _rec_inputs()

    def _L0_attn_setup():
        import jax, jax.numpy as jnp
        import numpy as np
        L = 2
        H = 512
        HEADS = 8
        HEAD = H // HEADS
        FF = 2048
        B = 4
        S = 256
        EPS = 1e-05
        GAMMAS = jnp.asarray(1.0 - np.exp(np.linspace(np.log(1.0 / 32), np.log(1.0 / 128), HEADS)), dtype=jnp.float32)

        def decay_mask(seq_len):
            n = jnp.arange(seq_len)
            diff = n[:, None] - n[None, :]
            mask = (diff >= 0).astype(jnp.float32)
            D = mask[None] * GAMMAS[:, None, None] ** jnp.maximum(diff, 0)[None].astype(jnp.float32)
            return D

        def layer_norm(x, g, b):
            mu = jnp.mean(x, axis=-1, keepdims=True)
            var = jnp.var(x, axis=-1, keepdims=True)
            return (x - mu) * jax.lax.rsqrt(var + EPS) * g + b

        def group_norm(y, g, b):
            yh = y.reshape(y.shape[0], y.shape[1], HEADS, HEAD)
            mu = jnp.mean(yh, axis=-1, keepdims=True)
            var = jnp.var(yh, axis=-1, keepdims=True)
            yh = (yh - mu) * jax.lax.rsqrt(var + EPS)
            return yh.reshape(y.shape) * g + b

        def msr(x, Wq, Wk, Wv, Wg, Wo, gg, gb, D):
            b, s, _ = x.shape
            q = (x @ Wq).reshape(b, s, HEADS, HEAD)
            k = (x @ Wk).reshape(b, s, HEADS, HEAD)
            v = (x @ Wv).reshape(b, s, HEADS, HEAD)
            scores = jnp.einsum('bnhd,bmhd->bhnm', q, k) * D
            y = jnp.einsum('bhnm,bmhd->bnhd', scores, v).reshape(b, s, H)
            y = group_norm(y, gg, gb)
            return jax.nn.silu(x @ Wg) * y @ Wo
        key = jax.random.key(seed)
        ks = jax.random.split(key, 8)
        g = lambda k, shp, sc: jax.random.normal(k, shp, dtype=jnp.float32) * sc
        return {'x': g(ks[0], (B, S, H), 1.0), 'Wq': g(ks[1], (L, H, H), H ** (-0.5)), 'Wk': g(ks[2], (L, H, H), H ** (-0.5)), 'Wv': g(ks[3], (L, H, H), H ** (-0.5)), 'Wg': g(ks[4], (L, H, H), H ** (-0.5)), 'Wo': g(ks[5], (L, H, H), H ** (-0.5)), 'gn_gamma': jnp.ones((L, H), jnp.float32), 'gn_beta': jnp.zeros((L, H), jnp.float32), 'W1': g(ks[6], (L, H, FF), H ** (-0.5)), 'b1': jnp.zeros((L, FF), jnp.float32), 'W2': g(ks[7], (L, FF, H), FF ** (-0.5)), 'b2': jnp.zeros((L, H), jnp.float32), 'ln_gamma': jnp.ones((H,), jnp.float32), 'ln_beta': jnp.zeros((H,), jnp.float32)}
    _L0_attn_all = _L0_attn_setup()
    _L0_attn_in = {k: v for k, v in _L0_attn_all.items() if k in ('Wq', 'Wk', 'Wv', 'Wg', 'Wo', 'gn_gamma', 'gn_beta', 'W1', 'b1', 'W2', 'b2', 'ln_gamma', 'ln_beta')}
    del _L0_attn_all

    def _L0_xattn_setup():
        import jax, jax.numpy as jnp
        import numpy as np
        EPS = 1e-06
        QMAX = 127.0

        def _smooth_quant_linear(x, w):
            amax_x = jnp.max(jnp.abs(x), axis=0)
            amax_w = jnp.max(jnp.abs(w), axis=0)
            s = jnp.sqrt(jnp.maximum(amax_x, EPS) / jnp.maximum(amax_w, EPS))
            s = jnp.maximum(s, EPS)
            xs = x / s
            ws = w * s
            x_scale = jnp.maximum(jnp.max(jnp.abs(xs), axis=-1, keepdims=True), EPS) / QMAX
            w_scale = jnp.maximum(jnp.max(jnp.abs(ws), axis=-1, keepdims=True), EPS) / QMAX
            x_q = jnp.clip(jnp.round(xs / x_scale), -QMAX, QMAX)
            w_q = jnp.clip(jnp.round(ws / w_scale), -QMAX, QMAX)
            return x_q @ w_q.T * x_scale * w_scale.T

        def _expert_forward(xe, guw, dw):
            h = _smooth_quant_linear(xe, guw)
            gate, up = jnp.split(h, 2, axis=-1)
            a = jax.nn.silu(gate) * up
            return _smooth_quant_linear(a, dw)
        key = jax.random.key(seed)
        k1, k2, k3 = jax.random.split(key, 3)
        E, T, D, I = (8, 512, 512, 256)
        x = jax.random.normal(k1, (E, T, D), dtype=jnp.float32)
        gate_up_weight = jax.random.normal(k2, (E, 2 * I, D), dtype=jnp.float32) * 0.02
        down_weight = jax.random.normal(k3, (E, D, I), dtype=jnp.float32) * 0.02
        return {'x': x, 'gate_up_weight': gate_up_weight, 'down_weight': down_weight}
    _L0_xattn_all = _L0_xattn_setup()
    _L0_xattn_in = {k: v for k, v in _L0_xattn_all.items() if k in ()}
    del _L0_xattn_all

    def _L0_ffn_setup():
        import jax, jax.numpy as jnp
        import numpy as np
        HIDDEN = 512
        INTER = 2048
        MOE_INTER = 256
        N_ROUTED = 8
        NUM_LOCAL = 8
        TOP_K = 2
        B, S = (4, 512)

        def _mlp(x, gw, uw, dw):
            g = x @ gw.T
            u = x @ uw.T
            return g * jax.nn.sigmoid(g) * u @ dw.T
        key = jax.random.key(seed)
        ks = jax.random.split(key, 8)
        std = 0.02
        return {'hidden_states': jax.random.normal(ks[0], (B, S, HIDDEN), jnp.float32), 'router_weight': jax.random.normal(ks[1], (N_ROUTED, HIDDEN), jnp.float32) * std, 'sh_gate': jax.random.normal(ks[2], (INTER, HIDDEN), jnp.float32) * std, 'sh_up': jax.random.normal(ks[3], (INTER, HIDDEN), jnp.float32) * std, 'sh_down': jax.random.normal(ks[4], (HIDDEN, INTER), jnp.float32) * std, 'r_gate': jax.random.normal(ks[5], (MOE_INTER, HIDDEN), jnp.float32) * std, 'r_up': jax.random.normal(ks[6], (MOE_INTER, HIDDEN), jnp.float32) * std, 'r_down': jax.random.normal(ks[7], (HIDDEN, MOE_INTER), jnp.float32) * std}
    _L0_ffn_all = _L0_ffn_setup()
    _L0_ffn_in = {k: v for k, v in _L0_ffn_all.items() if k in ('router_weight', 'sh_gate', 'sh_up', 'sh_down', 'r_gate', 'r_up', 'r_down')}
    del _L0_ffn_all
    return {'x': x, 'fside_BxS2xS2_0': fside_BxS2xS2_0, 'ctx_1024': ctx_1024, 'L0_attn_Wq': _L0_attn_in['Wq'], 'L0_attn_Wk': _L0_attn_in['Wk'], 'L0_attn_Wv': _L0_attn_in['Wv'], 'L0_attn_Wg': _L0_attn_in['Wg'], 'L0_attn_Wo': _L0_attn_in['Wo'], 'L0_attn_gn_gamma': _L0_attn_in['gn_gamma'], 'L0_attn_gn_beta': _L0_attn_in['gn_beta'], 'L0_attn_W1': _L0_attn_in['W1'], 'L0_attn_b1': _L0_attn_in['b1'], 'L0_attn_W2': _L0_attn_in['W2'], 'L0_attn_b2': _L0_attn_in['b2'], 'L0_attn_ln_gamma': _L0_attn_in['ln_gamma'], 'L0_attn_ln_beta': _L0_attn_in['ln_beta'], 'L0_ffn_router_weight': _L0_ffn_in['router_weight'], 'L0_ffn_sh_gate': _L0_ffn_in['sh_gate'], 'L0_ffn_sh_up': _L0_ffn_in['sh_up'], 'L0_ffn_sh_down': _L0_ffn_in['sh_down'], 'L0_ffn_r_gate': _L0_ffn_in['r_gate'], 'L0_ffn_r_up': _L0_ffn_in['r_up'], 'L0_ffn_r_down': _L0_ffn_in['r_down']}

def reference(x, fside_BxS2xS2_0, ctx_1024, L0_attn_Wq, L0_attn_Wk, L0_attn_Wv, L0_attn_Wg, L0_attn_Wo, L0_attn_gn_gamma, L0_attn_gn_beta, L0_attn_W1, L0_attn_b1, L0_attn_W2, L0_attn_b2, L0_attn_ln_gamma, L0_attn_ln_beta, L0_ffn_router_weight, L0_ffn_sh_gate, L0_ffn_sh_up, L0_ffn_sh_down, L0_ffn_r_gate, L0_ffn_r_up, L0_ffn_r_down):
    import jax
    import jax.numpy as jnp

    def _L0_attn_ref(x, Wq, Wk, Wv, Wg, Wo, gn_gamma, gn_beta, W1, b1, W2, b2, ln_gamma, ln_beta):
        import jax, jax.numpy as jnp
        import numpy as np
        L = 2
        H = 512
        HEADS = 8
        HEAD = H // HEADS
        FF = 2048
        B = 4
        S = 256
        EPS = 1e-05
        GAMMAS = jnp.asarray(1.0 - np.exp(np.linspace(np.log(1.0 / 32), np.log(1.0 / 128), HEADS)), dtype=jnp.float32)

        def decay_mask(seq_len):
            n = jnp.arange(seq_len)
            diff = n[:, None] - n[None, :]
            mask = (diff >= 0).astype(jnp.float32)
            D = mask[None] * GAMMAS[:, None, None] ** jnp.maximum(diff, 0)[None].astype(jnp.float32)
            return D

        def layer_norm(x, g, b):
            mu = jnp.mean(x, axis=-1, keepdims=True)
            var = jnp.var(x, axis=-1, keepdims=True)
            return (x - mu) * jax.lax.rsqrt(var + EPS) * g + b

        def group_norm(y, g, b):
            yh = y.reshape(y.shape[0], y.shape[1], HEADS, HEAD)
            mu = jnp.mean(yh, axis=-1, keepdims=True)
            var = jnp.var(yh, axis=-1, keepdims=True)
            yh = (yh - mu) * jax.lax.rsqrt(var + EPS)
            return yh.reshape(y.shape) * g + b

        def msr(x, Wq, Wk, Wv, Wg, Wo, gg, gb, D):
            b, s, _ = x.shape
            q = (x @ Wq).reshape(b, s, HEADS, HEAD)
            k = (x @ Wk).reshape(b, s, HEADS, HEAD)
            v = (x @ Wv).reshape(b, s, HEADS, HEAD)
            scores = jnp.einsum('bnhd,bmhd->bhnm', q, k) * D
            y = jnp.einsum('bhnm,bmhd->bnhd', scores, v).reshape(b, s, H)
            y = group_norm(y, gg, gb)
            return jax.nn.silu(x @ Wg) * y @ Wo
        D = decay_mask(x.shape[1])
        for i in range(L):
            xn = layer_norm(x, ln_gamma, ln_beta)
            ret = msr(xn, Wq[i], Wk[i], Wv[i], Wg[i], Wo[i], gn_gamma[i], gn_beta[i], D) + x
            rn = layer_norm(ret, ln_gamma, ln_beta)
            ffn = jax.nn.gelu(rn @ W1[i] + b1[i]) @ W2[i] + b2[i]
            x = ffn + ret
        return x

    def _L0_xattn_ref(x, gate_up_weight, down_weight):
        import jax, jax.numpy as jnp
        import numpy as np
        EPS = 1e-06
        QMAX = 127.0

        def _smooth_quant_linear(x, w):
            amax_x = jnp.max(jnp.abs(x), axis=0)
            amax_w = jnp.max(jnp.abs(w), axis=0)
            s = jnp.sqrt(jnp.maximum(amax_x, EPS) / jnp.maximum(amax_w, EPS))
            s = jnp.maximum(s, EPS)
            xs = x / s
            ws = w * s
            x_scale = jnp.maximum(jnp.max(jnp.abs(xs), axis=-1, keepdims=True), EPS) / QMAX
            w_scale = jnp.maximum(jnp.max(jnp.abs(ws), axis=-1, keepdims=True), EPS) / QMAX
            x_q = jnp.clip(jnp.round(xs / x_scale), -QMAX, QMAX)
            w_q = jnp.clip(jnp.round(ws / w_scale), -QMAX, QMAX)
            return x_q @ w_q.T * x_scale * w_scale.T

        def _expert_forward(xe, guw, dw):
            h = _smooth_quant_linear(xe, guw)
            gate, up = jnp.split(h, 2, axis=-1)
            a = jax.nn.silu(gate) * up
            return _smooth_quant_linear(a, dw)
        return jax.vmap(_expert_forward)(x, gate_up_weight, down_weight)

    def _L0_ffn_ref(hidden_states, router_weight, sh_gate, sh_up, sh_down, r_gate, r_up, r_down):
        import jax, jax.numpy as jnp
        import numpy as np
        HIDDEN = 512
        INTER = 2048
        MOE_INTER = 256
        N_ROUTED = 8
        NUM_LOCAL = 8
        TOP_K = 2
        B, S = (4, 512)

        def _mlp(x, gw, uw, dw):
            g = x @ gw.T
            u = x @ uw.T
            return g * jax.nn.sigmoid(g) * u @ dw.T
        Bsz, Seq, H = hidden_states.shape
        x = hidden_states.reshape(-1, H)
        logits = x.astype(jnp.float32) @ router_weight.astype(jnp.float32).T
        topk_vals, topk_idx = jax.lax.top_k(logits, TOP_K)
        topk_w = jax.nn.softmax(topk_vals, axis=-1)
        slot_mask = (topk_idx < NUM_LOCAL).astype(topk_w.dtype)
        comb_w = jnp.sum(topk_w * slot_mask, axis=-1).astype(x.dtype)
        shared = _mlp(x, sh_gate, sh_up, sh_down)
        routed = _mlp(x, r_gate, r_up, r_down) * comb_w[:, None]
        return (shared + routed).reshape(Bsz, Seq, H)
    x = x + _L0_attn_ref(_layernorm(x, axis=-1), L0_attn_Wq, L0_attn_Wk, L0_attn_Wv, L0_attn_Wg, L0_attn_Wo, L0_attn_gn_gamma, L0_attn_gn_beta, L0_attn_W1, L0_attn_b1, L0_attn_W2, L0_attn_b2, L0_attn_ln_gamma, L0_attn_ln_beta)
    x = x + _L0_xattn_ref(_layernorm(x, axis=-1), fside_BxS2xS2_0, ctx_1024)
    x = x + _L0_ffn_ref(_layernorm(x, axis=-1), L0_ffn_router_weight, L0_ffn_sh_gate, L0_ffn_sh_up, L0_ffn_sh_down, L0_ffn_r_gate, L0_ffn_r_up, L0_ffn_r_down)
    return x

_drawn_inputs = setup_inputs


def setup_inputs(seed=0):
    import zlib

    import numpy as np

    out = dict(_drawn_inputs(seed))
    spreads = {'L0_attn_gn_gamma': (1.0, 0.2),
     'L0_attn_gn_beta': (0.0, 0.1),
     'L0_attn_b1': (0.0, 0.1),
     'L0_attn_b2': (0.0, 0.1),
     'L0_attn_ln_gamma': (1.0, 0.2),
     'L0_attn_ln_beta': (0.0, 0.1)}
    factors = {'fside_BxS2xS2_0': 3.853,
     'ctx_1024': 3.878,
     'L0_ffn_router_weight': 8.0,
     'L0_ffn_r_gate': 3.918,
     'L0_ffn_r_up': 3.743,
     'L0_ffn_r_down': 3.744}
    for name, (base, spread) in spreads.items():
        noise = np.random.default_rng([zlib.crc32(name.encode()), seed]).standard_normal(out[name].shape)
        drawn = base * np.exp(spread * noise) if base else spread * noise
        out[name] = jnp.asarray(drawn.astype(out[name].dtype))
    for name, factor in factors.items():
        out[name] = (out[name] * factor).astype(out[name].dtype)
    return out
```

```python
import concourse.bass as bass
from concourse import mybir
from contextlib import ExitStack

P = 128
BATCH, SEQ, DIM = 4, 512, 512
LAYERS, HEADS, FF = 2, 8, 2048
HEAD = DIM // HEADS
KT = DIM // P
TT = SEQ // P
CHUNKS = 4
FT = FF // CHUNKS // P
INTER, MOE = 2048, 256
GW = 256
GCH = INTER // GW
QO = 512
QI = QO // 2
EXPERTS = 8
EPS = 1e-5
QEPS = 1e-6
QMAX = 127.0
MAGIC = 1.5 * 2 ** 23
SHARED = INTER // GW
MASK_AT = [0, 512, 896, 1152]
SCOLS = 1280
GROUPS = [(0, 0, 512), (512, 1, 384), (896, 2, 384)]

I_DVE = ["stats", "aggr", "vareps", "xn"]
LN_DVE = ["stats", "aggr", "vareps", "xn", "lo0", "lo1", "lo2", "lo3"]
LN_POOL = ["rstd", "hi0", "hi1", "hi2", "hi3"]
LN_PE = ["t0", "t1", "t2", "t3"]
LN_ACT = ["x0", "x1", "x2", "x3"]
A_PE = ["v", "q", "k", "g", "vt", "s0", "s1", "s2", "s3", "s4", "s5", "y"]
A_ACT = ["v", "q", "k", "g", "s0", "s1", "s2", "s3", "s4", "s5"]
A_DVE = ["q", "k", "v", "s0", "s1", "s2", "s3", "s4", "s5", "y", "ysum", "ymean", "yc", "ysq", "yvar", "yn"]
A_POOL = ["vhi", "vlo", "s0", "s1", "s2", "s3", "s4", "s5", "ysq", "rstd"]
AT_PE = ["t", "o0", "o1", "o2", "o3"]
AT_ACT = ["t", "hi"]
AT_DVE = ["lo", "o0", "o1", "o2", "o3"]
AT_POOL = ["gate"]
F_PE = ["h0", "h1", "h2", "h3"]
F_ACT = ["h0", "h1", "h2", "h3"]
F_DVE = ["lo0", "lo1", "lo2", "lo3"]
F_POOL = ["hi0", "hi1", "hi2", "hi3"]
FT_PE = ["o0", "o1", "o2", "o3"]
FT_DVE = ["o0", "o1", "o2", "o3"]
QK = {1: KT, 2: QI // P}
Q_PE = [n + s for s in "12" for k in [QK[int(s)]] for n in
        [f"x{j}_" for j in range(k)] + [f"w{j}_" for j in range(k)] + ["row_s_", "row_r_"]
        + [f"xq{j}_" for j in range(k)] + ["scale_row_"] + [f"wq{j}_" for j in range(k)]
        + [f"o{t}_" for t in range(TT)]]
Q_ACT = [n + s for s in "12" for k in [QK[int(s)]] for n in
         ["row_s_", "xq_", "xT_", "scale_row_", "wq_", "wT_"] + ["silu_"] * (s == "1")]
Q_DVE = ["x0", "stats", "aggr", "vareps", "xn"] + [n + s for s in "12" for k in [QK[int(s)]] for n in
         [f"x{j}_" for j in range(k)] + [f"w{j}_" for j in range(k)]
         + ["xmax_", "wmax_", "winv_", "ratio_", "s_", "rs_", "diag_", "xs_", "xabs_", "xscale_", "xrecip_", "xmul_", "xq_",
            "wabs_", "wscale_", "wrecip_", "diagw_", "wmul_", "wq_"]
         + [f"o{t}_" for t in range(TT)] + (["a_"] if s == "1" else ["add_"])]
Q_POOL = ["rstd"] + [n + s for s in "12" for n in ["s_", "ws_"]]
G_PE = ["g0", "u0", "g1", "u1"]
G_ACT = ["g0", "g1"]
G_DVE = ["p0", "p1", "lo0", "lo1"]
G_POOL = ["hi0", "hi1"]
GT_PE = ["o0", "o1", "o2", "o3"]
GT_DVE = ["o0", "o1", "o2", "o3"]
R_DVE = ["weights", "logits", "top", "gap", "den", "rden", "w2", "comb"]


def at(item, steps, name):
    return item * len(steps) + (steps.index(name) + 1)


def decoder_kernel(nc, x, wa_attn, wb_attn, wa_ffn, wb_ffn, params, b2, consts, decay,
                   q_w, q_ctx, wa_mlp, wb_mlp, router, out):
    f32, f32r, bf16 = mybir.dt.float32, mybir.dt.float32r, mybir.dt.bfloat16
    ALU = mybir.AluOpType
    ACT = mybir.ActivationFunctionType
    AX = mybir.AxisListType

    with ExitStack() as ctx:
        def sb(name, shape, dt):
            return ctx.enter_context(nc.sbuf_tensor(name, shape, dt))

        def sem(name):
            return ctx.enter_context(nc.semaphore(name))

        X = sb("resid", [P, BATCH * TT, DIM], f32)
        XT = sb("xT", [P, 2, BATCH, KT, SEQ], f32r)
        WA = sb("w_in", [P, 2, 2048], f32r)
        WB = sb("w_out", [P, 2, 2048], f32r)
        rawA = sb("raw_in", [P, 2048], f32)
        rawB = sb("raw_out", [P, 2048], f32)
        OP = sb("operands", [P, 8192], f32r)
        WK = sb("work", [P, 3584], f32)
        xn = sb("x_norm", [P, TT, DIM], f32)
        xtmp = sb("x_affine", [P, 2, SEQ], f32)
        ident = sb("ident", [P, P], f32)
        causal = sb("causal", [P, P], f32)
        prm = sb("params", [P, 56], f32)
        gncol = sb("gn_columns", [P, 2], f32)
        b1col = sb("b1_columns", [P, FT], f32)
        b2row = sb("b2_row", [P, DIM], f32)
        dec = sb("decay", [P, CHUNKS, 2, TT, 2], f32)
        half = sb("minus_half", [P, 8], f32)
        one = sb("one", [P, 1], f32)
        stats = sb("stats", [P, TT, 6], f32)
        mv = sb("mean_var", [P, TT, 2], f32)
        ve = sb("var_eps", [P, TT], f32)
        rstd = sb("rstd", [P, TT], f32)
        ysum = sb("y_sum", [P, 8], f32)
        ymean = sb("y_mean", [P, 8], f32)
        yssq = sb("y_sumsq", [P, 8], f32)
        yvar = sb("y_var", [P, 8], f32)
        yrs = sb("y_rstd", [P, 8], f32)
        bank = [ctx.enter_context(nc.psum_tensor(f"bank{i}", [P, 512], f32)) for i in range(8)]

        ones = sb("ones", [P, P], f32)
        identb = sb("ident_bf16", [P, P], bf16)
        Rraw = sb("router_raw", [P, KT, EXPERTS], f32)
        R = sb("router", [P, 2, KT, EXPERTS], f32r)
        lg = b2row[:, 0:128].rearrange("p (t n) -> p t n", n=EXPERTS)
        top = b2row[:, 128:256].rearrange("p (t n) -> p t n", n=8)
        rt = b2row[:, 256:352].rearrange("p (k t) -> p k t", k=6)
        qs = sb("quant_scales", [P, 12, 4], f32)
        phalf = sb("plus_half", [P, 4], f32)

        xrows = xn
        w_rows = {1: rawA[:, :].rearrange("p (t n) -> p t n", t=4),
                  2: WK[:, 0:1024].rearrange("p (t n) -> p t n", t=4)}
        hrows = rawB[:, :].rearrange("p (t n) -> p t n", t=4)
        xT_q = WK[:, 1024:2048].bitcast(bf16).rearrange("p (k n) -> p k n", k=KT)
        wT_q = WK[:, 2048:3072].bitcast(bf16).rearrange("p (k n) -> p k n", k=KT)
        row = WK[:, 3072:3584]
        diag = xtmp[:, :, :].rearrange("p a (k n) -> p a k n", k=KT)
        qrow = xtmp[:, :, :].rearrange("p a n -> p (a n)").bitcast(bf16).rearrange("p (t n) -> p t n", t=4)
        G = OP[:, 0:4096].rearrange("p (i s f n) -> p i s f n", i=2, s=2, f=2)
        wg = WA[:, :, :].rearrange("p s (r k n) -> p s r k n", r=2, k=KT)
        wd = WB[:, :, 0:1024].rearrange("p s (k n) -> p s k n", k=2)
        qT = OP[:, 0:1024].rearrange("p (s n) -> p s n", s=2)
        kT = OP[:, 1024:2048].rearrange("p (s n) -> p s n", s=2)
        vH = OP[:, 2048:3072].rearrange("p (s t n) -> p s t n", s=2, t=TT)
        S = OP[:, 3072:3072 + 4 * SCOLS].rearrange("p (r s n) -> p r s n", r=2, s=2)
        gated = WB[:, :, 1536:2048]
        wq4 = WA[:, :, :].rearrange("p s (r k n) -> p s r k n", r=4, k=KT)
        H = OP[:, :].rearrange("p (i s f n) -> p i s f n", i=2, s=2, f=FT)
        w1 = WA[:, :, :].rearrange("p s (k n) -> p s k n", k=KT)
        w2 = WB[:, :, :].rearrange("p s (k n) -> p s k n", k=FT)
        vraw = WK[:, 0:512]
        vdec = WK[:, 512:1024]
        sg = WK[:, 1024:2048].rearrange("p (i n) -> p i n", i=2)
        y = WK[:, 2048:2560]
        ysq = WK[:, 2560:3072]
        gt = WK[:, 3072:3584]
        hid = WK[:, 0:2048].rearrange("p (f n) -> p f n", f=FT)
        lng, lnb = prm[:, 0:4], prm[:, 4:8]
        gn = prm[:, 8:24].rearrange("p (a c) -> p a c", a=2)
        b1 = prm[:, 24:56].rearrange("p (c f) -> p c f", f=FT)

        loaded = sem("consts_loaded")
        halves = sem("minus_half_set")
        rawA_in, rawB_in, b2_in = sem("raw_in_loaded"), sem("raw_out_loaded"), sem("b2_loaded")
        x_in = [sem(f"x_loaded{b}") for b in range(BATCH)]
        out_done = sem("out_stored")
        wa_hi, wa_lo = sem("w_in_hi"), sem("w_in_lo")
        wb_hi, wb_lo = sem("w_out_hi"), sem("w_out_lo")
        b2_added = sem("b2_added")
        i_dve, i_pool = sem("first_norm_dve"), sem("first_norm_pool")
        gn_col, b1_col = sem("gn_columns_set"), sem("b1_columns_set")
        ln_dve, ln_pool, ln_pe, ln_act = sem("ln_dve"), sem("ln_pool"), sem("ln_pe"), sem("ln_act")
        a_pe, a_act, a_dve, a_pool = sem("attn_pe"), sem("attn_act"), sem("attn_dve"), sem("attn_pool")
        at_pe, at_act, at_dve, at_pool = (sem("attn_out_pe"), sem("attn_out_act"),
                                          sem("attn_out_dve"), sem("attn_out_pool"))
        f_pe, f_act, f_dve, f_pool = sem("ffn_pe"), sem("ffn_act"), sem("ffn_dve"), sem("ffn_pool")
        ft_pe, ft_dve = sem("ffn_out_pe"), sem("ffn_out_dve")
        q_in, qc_in, x0_in = sem("quant_w_loaded"), sem("quant_ctx_loaded"), sem("x_again_loaded")
        q_pe, q_act, q_dve, q_pool = sem("quant_pe"), sem("quant_act"), sem("quant_dve"), sem("quant_pool")
        g_pe, g_act, g_dve, g_pool = sem("mlp_pe"), sem("mlp_act"), sem("mlp_dve"), sem("mlp_pool")
        gt_pe, gt_dve = sem("mlp_out_pe"), sem("mlp_out_dve")
        r_pe, r_act, r_dve, r_hi = sem("router_pe"), sem("router_act"), sem("router_dve"), sem("router_hi")
        block = ctx.enter_context(nc.Block())

        def f(ap):
            return ap.bitcast(f32)

        def split_product(pe, out_, w, v, start, stop):
            (wh, wl), (vh, vl) = w, v
            pe.matmul(out_, wh, vh, start=start, stop=False)
            pe.matmul(out_, wh, vl, start=False, stop=False)
            return pe.matmul(out_, wl, vh, start=False, stop=stop)

        def hl(ap, *i):
            return ap[(slice(None), 0, *i)], ap[(slice(None), 1, *i)]

        LOADS = 16 * 5
        GITEM = (SHARED + 1) * BATCH
        ADEPTH = LAYERS * 2 * CHUNKS
        LN_LAST = LAYERS * 2 * BATCH
        NITEM = CHUNKS * BATCH

        @block.sync
        def _(sp):
            sp.dma_start(prm[:, :], params).then_inc(loaded, 16)
            sp.dma_start(ident[:, :], consts[:, 0:P]).then_inc(loaded, 16)
            sp.dma_start(causal[:, :], consts[:, P:2 * P]).then_inc(loaded, 16)
            sp.dma_start(dec[:, :, :, :, :].rearrange("p a b c d -> p (a b c d)"), decay).then_inc(loaded, 16)
            sp.dma_start(Rraw[:, :, :].rearrange("p k n -> p (k n)"), router).then_inc(loaded, 16)
            for b in range(BATCH):
                sp.dma_start(X[:, b * TT:(b + 1) * TT, :],
                             x[b * SEQ:(b + 1) * SEQ, :].rearrange("(t p) n -> p t n", p=P)).then_inc(x_in[b], 16)

            def load_w(w_a, cols_a, w_b, cols_b, j, chunk):
                sp.wait_ge(wa_lo, chunk + 1)
                sp.dma_start(rawA[:, 0:cols_a], w_a[bass.ds(j, 1), :, :].rearrange("o p n -> p (o n)")).then_inc(rawA_in, 16)
                sp.wait_ge(wb_lo, chunk + 1)
                sp.dma_start(rawB[:, 0:cols_b], w_b[bass.ds(j, 1), :, :].rearrange("o p n -> p (o n)")).then_inc(rawB_in, 16)

            with sp.Fori(0, LAYERS) as layer:
                sp.wait_ge(b2_added, layer * BATCH + 1)
                sp.dma_start(b2row[:, :], b2[bass.ds(layer, 1), :].rearrange("o n -> (o n)").partition_broadcast(P)).then_inc(b2_in, 16)
                with sp.Fori(0, CHUNKS) as c:
                    load_w(wa_attn, 2048, wb_attn, 512, layer * CHUNKS + c, layer * 2 * CHUNKS + c)
                with sp.Fori(0, CHUNKS) as c:
                    load_w(wa_ffn, 2048, wb_ffn, 2048, layer * CHUNKS + c, layer * 2 * CHUNKS + CHUNKS + c)
            sp.wait_ge(ft_dve, LAYERS * NITEM * len(FT_DVE))
            def load_quant(b):
                sp.dma_start(rawB[:, :].rearrange("p (t n) -> p t n", t=TT),
                             x[bass.ds(b * SEQ, SEQ), :].rearrange("(t p) n -> p t n", p=P)).then_inc(x0_in, 16)
                sp.dma_start(rawA[:, :], q_w[bass.ds(b, 1), :, :].rearrange("o p n -> p (o n)")).then_inc(q_in, 16)
                sp.dma_start(WK[:, 0:1024], q_ctx[bass.ds(b, 1), :, :].rearrange("o p n -> p (o n)")).then_inc(qc_in, 16)

            load_quant(0)
            with sp.Fori(1, BATCH) as b:
                sp.wait_ge(q_dve, b * len(Q_DVE))
                load_quant(b)
            sp.wait_ge(q_dve, BATCH * len(Q_DVE))
            with sp.Fori(0, SHARED + 1) as j:
                load_w(wa_mlp, 2048, wb_mlp, 1024, j, ADEPTH + j)
            for b in range(BATCH):
                sp.wait_ge(gt_dve, at(SHARED * BATCH + b, GT_DVE, "o3"))
                sp.dma_start(out[b * SEQ:(b + 1) * SEQ, :].rearrange("(t p) n -> p t n", p=P),
                             X[:, b * TT:(b + 1) * TT, :]).then_inc(out_done, 16)
            sp.wait_ge(out_done, 16 * BATCH)

        @block.tensor
        def _(pe):
            pe.wait_ge(loaded, LOADS)
            pe.wait_ge(halves, 5)

            def ln_transpose(n, free):
                pe.wait_ge(ln_dve, at(n, LN_DVE, "xn"))
                for k in range(KT):
                    if k < 2:
                        if free:
                            free(k)
                    else:
                        pe.wait_ge(ln_act, at(n, LN_ACT, f"x{k - 2}"))
                    for t in range(TT):
                        mm = pe.transpose(bank[k % 2][:, t * P:(t + 1) * P], xn[:, t, k * P:(k + 1) * P], ident[:, :])
                    mm.then_inc(ln_pe, 1)

            def xt_ready(n):
                pe.wait_ge(ln_dve, at(n, LN_DVE, "lo3"))
                pe.wait_ge(ln_pool, at(n, LN_POOL, "hi3"))
                pe.wait_ge(ln_act, at(n, LN_ACT, "x3"))

            def attn_head(b, i, chunk0, ln0, first):
                for n, role in enumerate(["v", "q", "k", "g"]):
                    if n < 2 and not first:
                        pe.wait_ge(a_act, at(i - 1, A_ACT, ["k", "g"][n]))
                        if n == 0:
                            pe.wait_ge(a_dve, at(i - 1, A_DVE, "k"))
                    if n == 2:
                        pe.wait_ge(a_act, at(i, A_ACT, "v"))
                    if n == 3:
                        pe.wait_ge(a_dve, at(i, A_DVE, "q"))
                    w = ["q", "k", "v", "g"].index(role)
                    for k in range(KT):
                        mm = split_product(pe, bank[n % 2][:, :], hl(wq4, w, k), hl(XT, b, k), k == 0, k == KT - 1)
                    mm.then_inc(a_pe, 1)
                if chunk0 and b + 1 < BATCH:
                    def free(k):
                        if k == 0:
                            pe.wait_ge(a_act, at(i, A_ACT, "k"))
                            pe.wait_ge(a_dve, at(i, A_DVE, "k"))
                        else:
                            pe.wait_ge(a_act, at(i, A_ACT, "g"))
                    ln_transpose(ln0 + b + 1, free)

            def attn_rest(i, first):
                pe.wait_ge(a_act, at(i, A_ACT, "v"))
                if not first:
                    pe.wait_ge(at_act, at(i - 1, AT_ACT, "t"))
                for t in range(TT):
                    mm = pe.transpose(bank[4][:, t * P:(t + 1) * P], vraw[:, t * P:(t + 1) * P], ident[:, :])
                mm.then_inc(a_pe, 1)
                pe.wait_ge(a_act, at(i, A_ACT, "k"))
                pe.wait_ge(a_dve, at(i, A_DVE, "k"))
                for g in range(6):
                    col, m0, n = GROUPS[g // 2]
                    r = g % 2
                    if g >= 2:
                        pe.wait_ge(a_dve, at(i, A_DVE, f"s{g - 2}"))
                    elif not first:
                        pe.wait_ge(a_dve, at(i - 1, A_DVE, f"s{g + 4}"))
                    rows = slice(64 * r, 64 * r + 64)
                    for m in ([0], [1], [2, 3])[g // 2]:
                        w = SEQ - m * P
                        o = bank[2 + r][:, MASK_AT[m] - col:MASK_AT[m] - col + w]
                        mm = split_product(pe, o,
                                           (kT[rows, 0, m * P:(m + 1) * P], kT[rows, 1, m * P:(m + 1) * P]),
                                           (qT[rows, 0, m * P:SEQ], qT[rows, 1, m * P:SEQ]), True, True)
                    mm.then_inc(a_pe, 1)

            def attn_values(i, first):
                pe.wait_ge(a_pool, at(i, A_POOL, "s5"))
                pe.wait_ge(a_act, at(i, A_ACT, "s5"))
                if not first:
                    pe.wait_ge(a_dve, at(i - 1, A_DVE, "y"))
                for r in range(2):
                    for n in range(TT):
                        o = bank[5][:, n * P + HEAD * r:n * P + HEAD * r + HEAD]
                        for m in range(n + 1):
                            c = MASK_AT[m] + (n - m) * P
                            mm = split_product(pe, o, (S[:, r, 0, c:c + P], S[:, r, 1, c:c + P]),
                                               (vH[:, 0, m, HEAD * r:HEAD * r + HEAD],
                                                vH[:, 1, m, HEAD * r:HEAD * r + HEAD]), m == 0, m == n)
                mm.then_inc(a_pe, 1)

            def attn_out_transpose(i):
                pe.wait_ge(a_dve, at(i, A_DVE, "yn"))
                for t in range(TT):
                    mm = pe.transpose(bank[4][:, t * P:(t + 1) * P], y[:, t * P:(t + 1) * P], ident[:, :])
                mm.then_inc(at_pe, 1)

            def attn_out(i, first):
                pe.wait_ge(at_act, at(i, AT_ACT, "hi"))
                pe.wait_ge(at_dve, at(i, AT_DVE, "lo"))
                for t in range(TT):
                    if t >= 2:
                        pe.wait_ge(at_dve, at(i, AT_DVE, f"o{t - 2}"))
                    elif not first:
                        pe.wait_ge(at_dve, at(i - 1, AT_DVE, f"o{t + 2}"))
                    split_product(pe, bank[6 + t % 2][:, :],
                                  (gated[:, 0, t * P:(t + 1) * P], gated[:, 1, t * P:(t + 1) * P]),
                                  (WB[:, 0, 0:DIM], WB[:, 1, 0:DIM]), True, True).then_inc(at_pe, 1)

            def attn_chunk(base, gc, ln0):
                chunk0 = ln0 is not None
                pe.wait_ge(wa_hi, gc + 1)
                pe.wait_ge(wa_lo, gc + 2)
                for b in range(BATCH):
                    i = base + b
                    first = chunk0 and b == 0
                    if chunk0:
                        xt_ready(ln0 + b)
                    attn_head(b, i, chunk0, ln0, first)
                    if not first:
                        attn_out_transpose(i - 1)
                    attn_rest(i, first)
                    if not first:
                        attn_out(i - 1, chunk0 and b == 1)
                    attn_values(i, first)
                    if b == 0:
                        pe.wait_ge(wb_hi, gc + 1)
                        pe.wait_ge(wb_lo, gc + 2)

            def ffn_head(b, i, chunk0, ln0, first):
                for ft in range(FT):
                    if not first:
                        pe.wait_ge(f_act, at(i - 1, F_ACT, f"h{ft}"))
                    for k in range(KT):
                        mm = split_product(pe, bank[ft][:, :], hl(w1, k, slice(ft * P, (ft + 1) * P)), hl(XT, b, k),
                                           k == 0, k == KT - 1)
                    mm.then_inc(f_pe, 1)
                if chunk0 and b + 1 < BATCH:
                    ln_transpose(ln0 + b + 1, lambda k: pe.wait_ge(f_act, at(i, F_ACT, f"h{k}")))

            def ffn_out(b, i, first):
                pe.wait_ge(f_dve, at(i, F_DVE, "lo3"))
                pe.wait_ge(f_pool, at(i, F_POOL, "hi3"))
                for t in range(TT):
                    if t >= 2:
                        pe.wait_ge(ft_dve, at(i, FT_DVE, f"o{t - 2}"))
                    elif not first:
                        pe.wait_ge(ft_dve, at(i - 1, FT_DVE, f"o{t + 2}"))
                    for k in range(FT):
                        mm = split_product(pe, bank[6 + t % 2][:, :], hl(H[:, b % 2], k, slice(t * P, (t + 1) * P)),
                                           hl(w2, k), k == 0, k == FT - 1)
                    mm.then_inc(ft_pe, 1)

            def ffn_chunk(base, gc, ln0):
                chunk0 = ln0 is not None
                pe.wait_ge(wa_hi, gc + 1)
                pe.wait_ge(wa_lo, gc + 2)
                for b in range(BATCH):
                    i = base + b
                    first = chunk0 and b == 0
                    if chunk0:
                        xt_ready(ln0 + b)
                    ffn_head(b, i, chunk0, ln0, first)
                    if not first:
                        ffn_out((b - 1) % BATCH, i - 1, chunk0 and b == 1)
                    if b == 0:
                        pe.wait_ge(wb_hi, gc + 1)
                        pe.wait_ge(wb_lo, gc + 2)

            with pe.Fori(0, LAYERS) as layer:
                base, gc, ln0 = layer * NITEM, layer * 2 * CHUNKS, layer * 2 * BATCH
                ln_transpose(ln0, None)
                attn_chunk(base, gc, ln0)
                with pe.Fori(1, CHUNKS) as c:
                    attn_chunk(base + c * BATCH, gc + c, None)
                attn_out_transpose(base + NITEM - 1)
                attn_out(base + NITEM - 1, False)
                pe.wait_ge(at_dve, at(base + NITEM - 1, AT_DVE, "o3"))
                ln_transpose(ln0 + BATCH, None)
                ffn_chunk(base, gc + CHUNKS, ln0 + BATCH)
                with pe.Fori(1, CHUNKS) as c:
                    ffn_chunk(base + c * BATCH, gc + CHUNKS + c, None)
                ffn_out(BATCH - 1, base + NITEM - 1, False)

            def quant_stage(b, s):
                K = QK[s]
                W = w_rows[s]
                if s == 1:
                    pe.wait_ge(q_dve, at(b, Q_DVE, "xn"))
                else:
                    pe.wait_ge(q_dve, at(b, Q_DVE, "a_1"))
                for k in range(K):
                    if k >= 2:
                        pe.wait_ge(q_dve, at(b, Q_DVE, f"x{k - 2}_{s}"))
                    for t in range(TT):
                        mm = pe.transpose(bank[k % 2][:, t * P:(t + 1) * P], xrows[:, t, k * P:(k + 1) * P], ident[:, :])
                    mm.then_inc(q_pe, 1)
                pe.wait_ge([q_in, qc_in][s - 1], 16 * (b + 1))
                for k in range(K):
                    if k >= 2:
                        pe.wait_ge(q_dve, at(b, Q_DVE, f"w{k - 2}_{s}"))
                    for t in range(TT):
                        mm = pe.transpose(bank[6 + k % 2][:, t * P:(t + 1) * P], W[:, t, k * P:(k + 1) * P], ident[:, :])
                    mm.then_inc(q_pe, 1)
                pe.wait_ge(q_dve, at(b, Q_DVE, f"diag_{s}"))
                for a in range(2):
                    for k in range(K):
                        mm = pe.matmul(bank[2 + a][:, k * P:(k + 1) * P], ones[:, :], diag[:, a, k, :], start=True, stop=True)
                    mm.then_inc(q_pe, 1)
                pe.wait_ge(q_act, at(b, Q_ACT, f"xq_{s}"))
                for k in range(K):
                    for t in range(TT):
                        mm = pe.transpose(bank[k].bitcast(bf16)[:, t * P:(t + 1) * P] if k < 2 else
                                          bank[4 + k % 2].bitcast(bf16)[:, t * P:(t + 1) * P],
                                          qrow[:, t, k * P:(k + 1) * P], identb[:, :])
                    mm.then_inc(q_pe, 1)
                pe.wait_ge(q_dve, at(b, Q_DVE, f"diagw_{s}"))
                for k in range(4):
                    mm = pe.matmul(bank[2][:, k * P:(k + 1) * P], ones[:, :], diag[:, 0, k, :], start=True, stop=True)
                mm.then_inc(q_pe, 1)
                pe.wait_ge(q_act, at(b, Q_ACT, f"wq_{s}"))
                for k in range(K):
                    for t in range(4):
                        mm = pe.transpose([bank[6], bank[7], bank[3], bank[0]][k].bitcast(bf16)[:, t * P:(t + 1) * P],
                                          qrow[:, t, k * P:(k + 1) * P], identb[:, :])
                    mm.then_inc(q_pe, 1)
                pe.wait_ge(q_act, at(b, Q_ACT, f"wT_{s}"))
                for t in range(TT):
                    if t >= 2:
                        pe.wait_ge(q_dve, at(b, Q_DVE, f"o{t - 2}_{s}"))
                    for k in range(K):
                        mm = pe.matmul(bank[4 + t % 2][:, :], xT_q[:, k, t * P:(t + 1) * P], wT_q[:, k, :],
                                       start=k == 0, stop=k == K - 1)
                    mm.then_inc(q_pe, 1)

            with pe.Fori(0, BATCH) as b:
                quant_stage(b, 1)
                quant_stage(b, 2)

            def mlp_head(b, i, chunk0, first):
                for n, (role, ft) in enumerate([(0, 0), (1, 0), (0, 1), (1, 1)]):
                    if not first:
                        sem_, steps, name = (g_act, G_ACT, f"g{ft}") if role == 0 else (g_dve, G_DVE, f"p{ft}")
                        pe.wait_ge(sem_, at(i - 1, steps, name))
                    for k in range(KT):
                        mm = split_product(pe, bank[n][:, :], hl(wg, role, k, slice(ft * P, (ft + 1) * P)), hl(XT, b, k),
                                           k == 0, k == KT - 1)
                    mm.then_inc(g_pe, 1)
                if chunk0 and b + 1 < BATCH:
                    def free(k):
                        if k == 0:
                            pe.wait_ge(g_act, at(i, G_ACT, "g0"))
                        else:
                            pe.wait_ge(g_dve, at(i, G_DVE, "p0"))
                    ln_transpose(LN_LAST + b + 1, free)

            def mlp_out(b, i, first):
                pe.wait_ge(g_dve, at(i, G_DVE, "lo1"))
                for t in range(TT):
                    if t >= 2:
                        pe.wait_ge(gt_dve, at(i, GT_DVE, f"o{t - 2}"))
                    elif not first:
                        pe.wait_ge(gt_dve, at(i - 1, GT_DVE, f"o{t + 2}"))
                    for k in range(2):
                        mm = split_product(pe, bank[6 + t % 2][:, :], hl(G[:, b % 2], k, slice(t * P, (t + 1) * P)),
                                           hl(wd, k), k == 0, k == 1)
                    mm.then_inc(gt_pe, 1)

            def mlp_chunk(base, gc, chunk0):
                pe.wait_ge(wa_hi, gc + 1)
                pe.wait_ge(wa_lo, gc + 2)
                for b in range(BATCH):
                    i = base + b
                    first = chunk0 and b == 0
                    if chunk0:
                        xt_ready(LN_LAST + b)
                    mlp_head(b, i, chunk0, first)
                    if not first:
                        mlp_out((b - 1) % BATCH, i - 1, chunk0 and b == 1)
                    if b == 0:
                        pe.wait_ge(wb_hi, gc + 1)
                        pe.wait_ge(wb_lo, gc + 2)

            pe.wait_ge(q_dve, BATCH * len(Q_DVE))
            ln_transpose(LN_LAST, None)
            mlp_chunk(0, ADEPTH, True)
            with pe.Fori(1, SHARED) as j:
                mlp_chunk(j * BATCH, ADEPTH + j, False)
            pe.wait_ge(r_hi, 1)
            pe.wait_ge(r_dve, 1 + R_DVE.index("weights"))
            for bt in range(BATCH * TT):
                b, t = divmod(bt, TT)
                for k in range(KT):
                    (xh, xl) = hl(XT, b, k, slice(t * P, (t + 1) * P))
                    mm = split_product(pe, bank[4][:, bt * EXPERTS:(bt + 1) * EXPERTS], (xh, xl), hl(R, k), k == 0, k == KT - 1)
            mm.then_inc(r_pe, 1)
            mlp_chunk(SHARED * BATCH, ADEPTH + SHARED, False)
            mlp_out(BATCH - 1, GITEM - 1, False)

        @block.scalar
        def _(act):
            act.wait_ge(loaded, LOADS)

            def split_in(gc, last_use):
                act.wait_ge(rawA_in, 16 * (gc + 1))
                last_use()
                act.activation(WA[:, 0, :], rawA[:, :], ACT.Copy).then_inc(wa_hi, 1)

            def split_out(gc, cols, last_use):
                act.wait_ge(rawB_in, 16 * (gc + 1))
                last_use()
                act.activation(WB[:, 0, 0:cols], rawB[:, 0:cols], ACT.Copy).then_inc(wb_hi, 1)

            def ln_affine(n):
                for k in range(KT):
                    act.wait_ge(ln_pe, at(n, LN_PE, f"t{k}"))
                    if k >= 2:
                        act.wait_ge(ln_dve, at(n, LN_DVE, f"lo{k - 2}"))
                        act.wait_ge(ln_pool, at(n, LN_POOL, f"hi{k - 2}"))
                    act.activation(xtmp[:, k % 2, :], bank[k % 2][:, :], ACT.Identity,
                                   scale=lng[:, k:k + 1], bias=lnb[:, k:k + 1]).then_inc(ln_act, 1)

            def attn_chunk(base, gc, ln0, lc):
                chunk0 = ln0 is not None
                split_in(gc, lambda: None if chunk0 else act.wait_ge(a_pe, at(base - 1, A_PE, "g")))
                for b in range(BATCH):
                    i = base + b
                    first = chunk0 and b == 0
                    act.wait_ge(a_pe, at(i, A_PE, "v"))
                    act.activation(vraw, bank[0][:, :], ACT.Copy).then_inc(a_act, 1)
                    if b == 1:
                        attn_columns(lc)
                    act.wait_ge(a_pe, at(i, A_PE, "q"))
                    act.activation(qT[:, 0, :], bank[1][:, :], ACT.Copy).then_inc(a_act, 1)
                    act.wait_ge(a_pe, at(i, A_PE, "k"))
                    act.activation(kT[:, 0, :], bank[0][:, :], ACT.Copy).then_inc(a_act, 1)
                    act.wait_ge(a_pe, at(i, A_PE, "g"))
                    if not (chunk0 and b < 2):
                        act.wait_ge(at_pool, at(i - 2, AT_POOL, "gate"))
                    act.activation(sg[:, b % 2, :], bank[1][:, :], ACT.Silu).then_inc(a_act, 1)
                    if chunk0 and b + 1 < BATCH:
                        ln_affine(ln0 + b + 1)
                    if not first:
                        attn_tail_t(i - 1, lc - 1 if b == 0 else lc)
                    for g in range(6):
                        col, m0, n = GROUPS[g // 2]
                        act.wait_ge(a_pe, at(i, A_PE, f"s{g}"))
                        act.activation(S[:, g % 2, 0, col:col + n], bank[2 + g % 2][:, 0:n], ACT.Copy).then_inc(a_act, 1)
                        if g == 1 and not first:
                            attn_tail_hi(i - 1)
                    if b == 0:
                        split_out(gc, DIM, lambda: None if chunk0 else act.wait_ge(at_pe, at(i - 1, AT_PE, "o3")))

            def attn_columns(lc):
                act.activation(gncol[:, :], gn[:, :, bass.ds(lc, 1)].rearrange("p a o -> p (a o)"), ACT.Copy).then_inc(gn_col, 1)

            def attn_tail_t(i, lc):
                act.wait_ge(gn_col, lc + 1)
                act.wait_ge(at_pe, at(i, AT_PE, "t"))
                act.activation(gt, bank[4][:, :], ACT.Identity, scale=gncol[:, 0:1],
                               bias=gncol[:, 1:2]).then_inc(at_act, 1)

            def attn_tail_hi(i):
                act.wait_ge(at_pool, at(i, AT_POOL, "gate"))
                act.activation(gated[:, 0, :], gt, ACT.Copy).then_inc(at_act, 1)

            def ffn_chunk(base, gc, ln0, lc):
                chunk0 = ln0 is not None
                def inputs_used():
                    if not chunk0:
                        act.wait_ge(f_pe, at(base - 1, F_PE, "h3"))
                        act.wait_ge(f_act, at(base - 1, F_ACT, "h3"))
                split_in(gc, inputs_used)
                act.activation(b1col[:, :], b1[:, bass.ds(lc, 1), :].rearrange("p o f -> p (o f)"), ACT.Copy).then_inc(b1_col, 1)
                act.wait_ge(b1_col, lc + 1)
                for b in range(BATCH):
                    i = base + b
                    first = chunk0 and b == 0
                    for ft in range(FT):
                        act.wait_ge(f_pe, at(i, F_PE, f"h{ft}"))
                        if not first:
                            act.wait_ge(f_dve, at(i - 1, F_DVE, f"lo{ft}"))
                            act.wait_ge(f_pool, at(i - 1, F_POOL, f"hi{ft}"))
                        act.activation(hid[:, ft, :], bank[ft][:, :], ACT.Gelu_apprx_tanh,
                                       bias=b1col[:, ft:ft + 1]).then_inc(f_act, 1)
                    if chunk0 and b + 1 < BATCH:
                        ln_affine(ln0 + b + 1)
                    if b == 0:
                        split_out(gc, 2048, lambda: None if chunk0 else act.wait_ge(ft_pe, at(i - 1, FT_PE, "o3")))

            with act.Fori(0, LAYERS) as layer:
                base, gc, ln0 = layer * NITEM, layer * 2 * CHUNKS, layer * 2 * BATCH
                ln_affine(ln0)
                attn_chunk(base, gc, ln0, layer * CHUNKS)
                with act.Fori(1, CHUNKS) as c:
                    attn_chunk(base + c * BATCH, gc + c, None, layer * CHUNKS + c)
                attn_tail_t(base + NITEM - 1, layer * CHUNKS + CHUNKS - 1)
                attn_tail_hi(base + NITEM - 1)
                ln_affine(ln0 + BATCH)
                ffn_chunk(base, gc + CHUNKS, ln0 + BATCH, layer * CHUNKS)
                with act.Fori(1, CHUNKS) as c:
                    ffn_chunk(base + c * BATCH, gc + CHUNKS + c, None, layer * CHUNKS + c)

            def quant_stage(b, s):
                K = QK[s]
                D = K * P
                W = w_rows[s]
                act.wait_ge(q_pe, at(b, Q_PE, f"row_s_{s}"))
                act.activation(row[:, 0:D], bank[2][:, 0:D], ACT.Copy).then_inc(q_act, 1)
                act.wait_ge(q_pe, at(b, Q_PE, f"row_r_{s}"))
                act.wait_ge(q_dve, at(b, Q_DVE, f"xq_{s}"))
                act.activation(qrow[:, :, 0:D], xrows[:, :, 0:D], ACT.Copy, bias=-MAGIC).then_inc(q_act, 1)
                for k in range(K):
                    act.wait_ge(q_pe, at(b, Q_PE, f"xq{k}_{s}"))
                    src = (bank[k] if k < 2 else bank[4 + k % 2]).bitcast(bf16)[:, 0:SEQ]
                    ins = act.activation(xT_q[:, k, :], src, ACT.Copy)
                ins.then_inc(q_act, 1)
                act.wait_ge(q_pool, at(b, Q_POOL, f"ws_{s}"))
                act.wait_ge(q_pe, at(b, Q_PE, f"scale_row_{s}"))
                act.activation(row, bank[2][:, :], ACT.Copy).then_inc(q_act, 1)
                act.wait_ge(q_dve, at(b, Q_DVE, f"wq_{s}"))
                act.activation(qrow[:, :, 0:D], W, ACT.Copy, bias=-MAGIC).then_inc(q_act, 1)
                for k in range(K):
                    act.wait_ge(q_pe, at(b, Q_PE, f"wq{k}_{s}"))
                    src = [bank[6], bank[7], bank[3], bank[0]][k].bitcast(bf16)[:, 0:QO]
                    ins = act.activation(wT_q[:, k, :], src, ACT.Copy)
                ins.then_inc(q_act, 1)
                if s == 1:
                    act.wait_ge(q_dve, at(b, Q_DVE, "o3_1"))
                    act.activation(xrows[:, :, 0:QI], hrows[:, :, 0:QI], ACT.Silu).then_inc(q_act, 1)

            with act.Fori(0, BATCH) as b:
                quant_stage(b, 1)
                quant_stage(b, 2)

            def ln_copy(n):
                for k in range(KT):
                    act.wait_ge(ln_pe, at(n, LN_PE, f"t{k}"))
                    if k >= 2:
                        act.wait_ge(ln_dve, at(n, LN_DVE, f"lo{k - 2}"))
                        act.wait_ge(ln_pool, at(n, LN_POOL, f"hi{k - 2}"))
                    act.activation(xtmp[:, k % 2, :], bank[k % 2][:, :], ACT.Copy).then_inc(ln_act, 1)

            def mlp_chunk(base, gc, chunk0):
                split_in(gc, lambda: None if chunk0 else act.wait_ge(g_pe, at(base - 1, G_PE, "u1")))
                for b in range(BATCH):
                    i = base + b
                    for ft in range(2):
                        act.wait_ge(g_pe, at(i, G_PE, f"g{ft}"))
                        if not (chunk0 and b == 0):
                            act.wait_ge(g_dve, at(i - 1, G_DVE, f"lo{ft}"))
                            act.wait_ge(g_pool, at(i - 1, G_POOL, f"hi{ft}"))
                        act.activation(hid[:, ft, :], bank[2 * ft][:, :], ACT.Silu).then_inc(g_act, 1)
                    if chunk0 and b + 1 < BATCH:
                        ln_copy(LN_LAST + b + 1)
                    if b == 0:
                        split_out(gc, 1024, lambda: None if chunk0 else act.wait_ge(gt_pe, at(i - 1, GT_PE, "o3")))

            act.activation(R[:, 0, :, :], Rraw[:, :, :], ACT.Copy).then_inc(r_hi, 1)
            ln_copy(LN_LAST)
            mlp_chunk(0, ADEPTH, True)
            with act.Fori(1, SHARED) as j:
                mlp_chunk(j * BATCH, ADEPTH + j, False)
            act.wait_ge(r_dve, 1 + R_DVE.index("gap"))
            act.activation(rt[:, 1, :], rt[:, 0, :], ACT.Exp).then_inc(r_act, 1)
            mlp_chunk(SHARED * BATCH, ADEPTH + SHARED, False)

        @block.vector
        def _(dve):
            dve.wait_ge(loaded, LOADS)
            dve.memset(half[:, :], -0.5).then_inc(halves, 1)
            dve.memset(phalf[:, :], 0.5).then_inc(halves, 1)
            dve.memset(ones[:, :], 1.0).then_inc(halves, 1)
            dve.tensor_copy(identb[:, :], ident[:, :]).then_inc(halves, 1)
            dve.memset(one[:, :], 1.0).then_inc(halves, 1)
            for n, s in enumerate((wa_lo, wb_lo, b2_added)):
                dve.memset(yvar[:, n:n + 1], 0.0).then_inc(s, 1)

            def split_in(gc):
                dve.wait_ge(wa_hi, gc + 1)
                dve.tensor_tensor(WA[:, 1, :], rawA[:, :], f(WA[:, 0, :]), ALU.subtract).then_inc(wa_lo, 1)

            def split_out(gc, cols):
                dve.wait_ge(wb_hi, gc + 1)
                dve.tensor_tensor(WB[:, 1, 0:cols], rawB[:, 0:cols], f(WB[:, 0, 0:cols]), ALU.subtract).then_inc(wb_lo, 1)

            def ln_stats(n, b):
                for t in range(TT):
                    ins = dve.bn_stats(stats[:, t, :], X[:, b * TT + t, :])
                ins.then_inc(ln_dve, 1)
                dve.wait_ge(ln_dve, at(n, LN_DVE, "stats"))
                dve.memset(ve[:, :], 0.0)
                for t in range(TT):
                    ins = dve.bn_aggr(mv[:, t, :], stats[:, t, :])
                ins.then_inc(ln_dve, 1)
                dve.wait_ge(ln_dve, at(n, LN_DVE, "aggr"))
                dve.tensor_scalar(ve[:, :], mv[:, :, 1], EPS, None, ALU.add).then_inc(ln_dve, 1)
                dve.wait_ge(ln_pool, at(n, LN_POOL, "rstd"))
                for t in range(TT):
                    ins = dve.tensor_scalar(xn[:, t, :], X[:, b * TT + t, :], mv[:, t, 0:1], rstd[:, t:t + 1],
                                            ALU.subtract, ALU.mult)
                ins.then_inc(ln_dve, 1)

            def ln_low(n, b):
                for k in range(KT):
                    dve.wait_ge(ln_pool, at(n, LN_POOL, f"hi{k}"))
                    dve.tensor_tensor(XT[:, 1, b, k, :], xtmp[:, k % 2, :], f(XT[:, 0, b, k, :]), ALU.subtract).then_inc(ln_dve, 1)

            def low(dst, full, hi):
                return dve.tensor_tensor(dst, full, f(hi), ALU.subtract)

            def attn_chunk(base, gc, ln0, c):
                chunk0 = ln0 is not None
                split_in(gc)
                for b in range(BATCH):
                    i = base + b
                    first = chunk0 and b == 0
                    dve.wait_ge(a_act, at(i, A_ACT, "q"))
                    low(qT[:, 1, :], bank[1][:, :], qT[:, 0, :]).then_inc(a_dve, 1)
                    dve.wait_ge(a_act, at(i, A_ACT, "k"))
                    low(kT[:, 1, :], bank[0][:, :], kT[:, 0, :]).then_inc(a_dve, 1)
                    if chunk0 and b + 1 < BATCH:
                        ln_stats(ln0 + b + 1, b + 1)
                        ln_low(ln0 + b + 1, b + 1)
                    dve.wait_ge(a_pe, at(i, A_PE, "vt"))
                    dve.tensor_tensor(vdec.rearrange("p (t r n) -> p t r n", t=TT, r=2),
                                      bank[4][:, :].rearrange("p (t r n) -> p t r n", t=TT, r=2),
                                      dec[:, bass.ds(c, 1), 0, :, :].rearrange("p o t r -> p (o t) r").unsqueeze(3).to_broadcast([P, TT, 2, HEAD]),
                                      ALU.mult).then_inc(a_dve, 1)
                    for g in range(6):
                        col, m0, n = GROUPS[g // 2]
                        dve.wait_ge(a_act, at(i, A_ACT, f"s{g}"))
                        low(S[:, g % 2, 1, col:col + n], bank[2 + g % 2][:, 0:n], S[:, g % 2, 0, col:col + n]).then_inc(a_dve, 1)
                        if g == 1 and not first:
                            attn_tail_lo(i - 1)
                    if not first:
                        attn_tail_out(i - 1, (b - 1) % BATCH)
                    if b == 0:
                        split_out(gc, DIM)
                    attn_norm(i, c)

            def attn_norm(i, c):
                y8 = y.rearrange("p (g n) -> p g n", n=HEAD)
                dve.wait_ge(a_pe, at(i, A_PE, "y"))
                dve.tensor_tensor(y.rearrange("p (t r n) -> p t r n", t=TT, r=2),
                                  bank[5][:, :].rearrange("p (t r n) -> p t r n", t=TT, r=2),
                                  dec[:, bass.ds(c, 1), 1, :, :].rearrange("p o t r -> p (o t) r").unsqueeze(3).to_broadcast([P, TT, 2, HEAD]),
                                  ALU.mult).then_inc(a_dve, 1)
                dve.wait_ge(a_dve, at(i, A_DVE, "y"))
                dve.tensor_reduce(ysum[:, :], y8, AX.X, ALU.add).then_inc(a_dve, 1)
                dve.wait_ge(a_dve, at(i, A_DVE, "ysum"))
                dve.tensor_scalar(ymean[:, :], ysum[:, :], 1.0 / HEAD, None, ALU.mult).then_inc(a_dve, 1)
                dve.wait_ge(a_dve, at(i, A_DVE, "ymean"))
                dve.tensor_tensor(y8, y8, ymean[:, :].unsqueeze(2).to_broadcast([P, 8, HEAD]), ALU.subtract).then_inc(a_dve, 1)
                dve.wait_ge(a_pool, at(i, A_POOL, "ysq"))
                dve.tensor_reduce(yssq[:, :], ysq.rearrange("p (g n) -> p g n", n=HEAD), AX.X, ALU.add).then_inc(a_dve, 1)
                dve.wait_ge(a_dve, at(i, A_DVE, "ysq"))
                dve.tensor_scalar(yvar[:, :], yssq[:, :], 1.0 / HEAD, EPS, ALU.mult, ALU.add).then_inc(a_dve, 1)
                dve.wait_ge(a_pool, at(i, A_POOL, "rstd"))
                dve.tensor_tensor(y8, y8, yrs[:, :].unsqueeze(2).to_broadcast([P, 8, HEAD]), ALU.mult).then_inc(a_dve, 1)

            def attn_tail_lo(i):
                dve.wait_ge(at_act, at(i, AT_ACT, "hi"))
                low(gated[:, 1, :], gt, gated[:, 0, :]).then_inc(at_dve, 1)

            def attn_tail_out(i, b):
                for t in range(TT):
                    dve.wait_ge(at_pe, at(i, AT_PE, f"o{t}"))
                    dve.tensor_tensor(X[:, b * TT + t, :], X[:, b * TT + t, :], bank[6 + t % 2][:, :], ALU.add).then_inc(at_dve, 1)

            def ffn_chunk(base, gc, ln0, layer):
                chunk0 = ln0 is not None
                split_in(gc)
                for b in range(BATCH):
                    i = base + b
                    first = chunk0 and b == 0
                    for ft in range(FT):
                        dve.wait_ge(f_pool, at(i, F_POOL, f"hi{ft}"))
                        low(H[:, b % 2, 1, ft, :], hid[:, ft, :], H[:, b % 2, 0, ft, :]).then_inc(f_dve, 1)
                    if chunk0 and b + 1 < BATCH:
                        ln_stats(ln0 + b + 1, b + 1)
                        add_b2(layer, b + 1, ln0 + b + 1)
                        ln_low(ln0 + b + 1, b + 1)
                    if not first:
                        ffn_tail(i - 1, (b - 1) % BATCH)
                    if b == 0:
                        split_out(gc, 2048)

            def ffn_tail(i, b):
                for t in range(TT):
                    dve.wait_ge(ft_pe, at(i, FT_PE, f"o{t}"))
                    dve.tensor_tensor(X[:, b * TT + t, :], X[:, b * TT + t, :], bank[6 + t % 2][:, :], ALU.add).then_inc(ft_dve, 1)

            def add_b2(layer, b, n):
                dve.wait_ge(b2_in, 16 * (layer + 1))
                dve.wait_ge(ln_dve, at(n, LN_DVE, "xn"))
                dve.tensor_tensor(X[:, b * TT:(b + 1) * TT, :], X[:, b * TT:(b + 1) * TT, :],
                                  b2row[:, :].unsqueeze(1).to_broadcast([P, TT, DIM]), ALU.add).then_inc(b2_added, 1)

            for b in range(BATCH):
                dve.wait_ge(x_in[b], 16)
                for t in range(TT):
                    ins = dve.bn_stats(stats[:, t, :], X[:, b * TT + t, :])
                ins.then_inc(i_dve, 1)
                dve.wait_ge(i_dve, at(b, I_DVE, "stats"))
                for t in range(TT):
                    ins = dve.bn_aggr(mv[:, t, :], stats[:, t, :])
                ins.then_inc(i_dve, 1)
                dve.wait_ge(i_dve, at(b, I_DVE, "aggr"))
                dve.tensor_scalar(ve[:, :], mv[:, :, 1], EPS, None, ALU.add).then_inc(i_dve, 1)
                dve.wait_ge(i_pool, b + 1)
                for t in range(TT):
                    Xt = X[:, b * TT + t, :]
                    ins = dve.tensor_scalar(Xt, Xt, mv[:, t, 0:1], rstd[:, t:t + 1], ALU.subtract, ALU.mult)
                ins.then_inc(i_dve, 1)
            dve.wait_ge(i_dve, BATCH * len(I_DVE))

            with dve.Fori(0, LAYERS) as layer:
                base, gc, ln0 = layer * NITEM, layer * 2 * CHUNKS, layer * 2 * BATCH
                ln_stats(ln0, 0)
                ln_low(ln0, 0)
                attn_chunk(base, gc, ln0, 0)
                with dve.Fori(1, CHUNKS) as c:
                    attn_chunk(base + c * BATCH, gc + c, None, c)
                attn_tail_lo(base + NITEM - 1)
                attn_tail_out(base + NITEM - 1, BATCH - 1)
                dve.wait_ge(at_dve, at(base + NITEM - 1, AT_DVE, "o3"))
                ln_stats(ln0 + BATCH, 0)
                add_b2(layer, 0, ln0 + BATCH)
                ln_low(ln0 + BATCH, 0)
                ffn_chunk(base, gc + CHUNKS, ln0 + BATCH, layer)
                with dve.Fori(1, CHUNKS) as c:
                    ffn_chunk(base + c * BATCH, gc + CHUNKS + c, None, layer)
                ffn_tail(base + NITEM - 1, BATCH - 1)

            AX_, AW, WI, RA, S_, RS, XM, XS, XR, WM, WS, WR = range(12)

            def quant_stage(b, s):
                K = QK[s]
                D = K * P
                W = w_rows[s]

                def done(name):
                    dve.wait_ge(q_dve, at(b, Q_DVE, f"{name}_{s}"))

                for k in range(K):
                    dve.wait_ge(q_pe, at(b, Q_PE, f"x{k}_{s}"))
                    dve.tensor_reduce(qs[:, AX_, k:k + 1], bank[k % 2][:, :], AX.X, ALU.max,
                                      apply_absolute_value=True).then_inc(q_dve, 1)
                for k in range(K):
                    dve.wait_ge(q_pe, at(b, Q_PE, f"w{k}_{s}"))
                    dve.tensor_reduce(qs[:, AW, k:k + 1], bank[6 + k % 2][:, :], AX.X, ALU.max,
                                      apply_absolute_value=True).then_inc(q_dve, 1)
                done(f"w{K - 1}")
                dve.tensor_scalar(qs[:, AX_, 0:K], qs[:, AX_, 0:K], QEPS, None, ALU.max).then_inc(q_dve, 1)
                dve.tensor_scalar(qs[:, AW, 0:K], qs[:, AW, 0:K], QEPS, None, ALU.max).then_inc(q_dve, 1)
                done("wmax")
                dve.reciprocal(qs[:, WI, 0:K], qs[:, AW, 0:K]).then_inc(q_dve, 1)
                done("winv")
                dve.tensor_tensor(qs[:, RA, 0:K], qs[:, AX_, 0:K], qs[:, WI, 0:K], ALU.mult).then_inc(q_dve, 1)
                dve.wait_ge(q_pool, at(b, Q_POOL, f"s_{s}"))
                dve.tensor_scalar(qs[:, S_, 0:K], qs[:, S_, 0:K], QEPS, None, ALU.max).then_inc(q_dve, 1)
                done("s")
                dve.reciprocal(qs[:, RS, 0:K], qs[:, S_, 0:K]).then_inc(q_dve, 1)
                done("rs")
                for a, r in enumerate((S_, RS)):
                    for k in range(K):
                        ins = dve.tensor_scalar(diag[:, a, k, :], ident[:, :], qs[:, r, k:k + 1], None, ALU.mult)
                ins.then_inc(q_dve, 1)

                def rounded(V, recip, mul):
                    for t in range(4):
                        ins = dve.tensor_scalar(V[:, t, 0:D], V[:, t, 0:D], qs[:, recip, t:t + 1], -QMAX, ALU.mult, ALU.max)
                    ins.then_inc(q_dve, 1)
                    done(mul)
                    dve.tensor_scalar(V[:, :, 0:D], V[:, :, 0:D], QMAX, MAGIC, ALU.min, ALU.add).then_inc(q_dve, 1)

                dve.wait_ge(q_pe, at(b, Q_PE, f"row_r_{s}"))
                dve.tensor_tensor(xrows[:, :, 0:D], xrows[:, :, 0:D], bank[3][:, 0:D].unsqueeze(1).to_broadcast([P, TT, D]),
                                  ALU.mult).then_inc(q_dve, 1)
                done("xs")
                dve.tensor_reduce(qs[:, XM, :], xrows[:, :, 0:D], AX.X, ALU.max, apply_absolute_value=True).then_inc(q_dve, 1)
                done("xabs")
                dve.tensor_scalar(qs[:, XS, :], qs[:, XM, :], QEPS, 1.0 / QMAX, ALU.max, ALU.mult).then_inc(q_dve, 1)
                done("xscale")
                dve.reciprocal(qs[:, XR, :], qs[:, XS, :]).then_inc(q_dve, 1)
                done("xrecip")
                rounded(xrows, XR, "xmul")
                dve.wait_ge(q_pool, at(b, Q_POOL, f"ws_{s}"))
                dve.tensor_reduce(qs[:, WM, :], W, AX.X, ALU.max, apply_absolute_value=True).then_inc(q_dve, 1)
                done("wabs")
                dve.tensor_scalar(qs[:, WS, :], qs[:, WM, :], QEPS, 1.0 / QMAX, ALU.max, ALU.mult).then_inc(q_dve, 1)
                done("wscale")
                dve.reciprocal(qs[:, WR, :], qs[:, WS, :]).then_inc(q_dve, 1)
                dve.wait_ge(q_pe, at(b, Q_PE, f"xq{K - 1}_{s}"))
                for k in range(4):
                    ins = dve.tensor_scalar(diag[:, 0, k, :], ident[:, :], qs[:, WS, k:k + 1], None, ALU.mult)
                ins.then_inc(q_dve, 1)
                done("wrecip")
                rounded(W, WR, "wmul")
                dve.wait_ge(q_act, at(b, Q_ACT, f"scale_row_{s}"))
                for t in range(TT):
                    dve.wait_ge(q_pe, at(b, Q_PE, f"o{t}_{s}"))
                    dve.scalar_tensor_tensor(out=hrows[:, t, :], in0=bank[4 + t % 2][:, :], scalar=qs[:, XS, t:t + 1],
                                             in1=row, op0=ALU.mult, op1=ALU.mult).then_inc(q_dve, 1)

            with dve.Fori(0, BATCH) as b:
                Xb = X[:, bass.ds(b * TT, TT), :]
                dve.wait_ge(x0_in, 16 * (b + 1))
                dve.tensor_tensor(Xb, Xb, hrows, ALU.add).then_inc(q_dve, 1)
                dve.wait_ge(q_dve, at(b, Q_DVE, "x0"))
                dve.memset(ve[:, :], 0.0)
                for t in range(TT):
                    ins = dve.bn_stats(stats[:, t, :], X[:, bass.ds(b * TT + t, 1), :].rearrange("p o n -> p (o n)"))
                ins.then_inc(q_dve, 1)
                dve.wait_ge(q_dve, at(b, Q_DVE, "stats"))
                dve.memset(ve[:, :], 0.0)
                for t in range(TT):
                    ins = dve.bn_aggr(mv[:, t, :], stats[:, t, :])
                ins.then_inc(q_dve, 1)
                dve.wait_ge(q_dve, at(b, Q_DVE, "aggr"))
                dve.tensor_scalar(ve[:, :], mv[:, :, 1], EPS, None, ALU.add).then_inc(q_dve, 1)
                dve.wait_ge(q_pool, at(b, Q_POOL, "rstd"))
                for t in range(TT):
                    ins = dve.tensor_scalar(xn[:, t, :], X[:, bass.ds(b * TT + t, 1), :].rearrange("p o n -> p (o n)"),
                                            mv[:, t, 0:1], rstd[:, t:t + 1], ALU.subtract, ALU.mult)
                ins.then_inc(q_dve, 1)
                quant_stage(b, 1)
                dve.wait_ge(q_act, at(b, Q_ACT, "silu_1"))
                dve.tensor_tensor(xrows[:, :, 0:QI], xrows[:, :, 0:QI], hrows[:, :, QI:QO], ALU.mult).then_inc(q_dve, 1)
                quant_stage(b, 2)
                dve.wait_ge(q_dve, at(b, Q_DVE, "o3_2"))
                dve.tensor_tensor(Xb, Xb, hrows, ALU.add).then_inc(q_dve, 1)

            def mlp_chunk(base, gc, chunk0, routed=False):
                split_in(gc)
                for b in range(BATCH):
                    i = base + b
                    for ft in range(2):
                        dve.wait_ge(g_pe, at(i, G_PE, f"u{ft}"))
                        dve.wait_ge(g_act, at(i, G_ACT, f"g{ft}"))
                        dve.tensor_tensor(hid[:, ft, :], hid[:, ft, :], bank[2 * ft + 1][:, :], ALU.mult).then_inc(g_dve, 1)
                    for ft in range(2):
                        dve.wait_ge(g_pool, at(i, G_POOL, f"hi{ft}"))
                        low(G[:, b % 2, 1, ft, :], hid[:, ft, :], G[:, b % 2, 0, ft, :]).then_inc(g_dve, 1)
                    if chunk0 and b + 1 < BATCH:
                        ln_stats(LN_LAST + b + 1, b + 1)
                        ln_low(LN_LAST + b + 1, b + 1)
                    if not (chunk0 and b == 0):
                        mlp_tail(i - 1, (b - 1) % BATCH, routed and b > 0)
                    if b == 0:
                        split_out(gc, 1024)

            def mlp_tail(i, b, routed):
                for t in range(TT):
                    dve.wait_ge(gt_pe, at(i, GT_PE, f"o{t}"))
                    Xt = X[:, b * TT + t, :]
                    if routed:
                        dve.scalar_tensor_tensor(out=Xt, in0=bank[6 + t % 2][:, :], scalar=rt[:, 5, b * TT + t:b * TT + t + 1],
                                                 in1=Xt, op0=ALU.mult, op1=ALU.add).then_inc(gt_dve, 1)
                    else:
                        dve.tensor_tensor(Xt, Xt, bank[6 + t % 2][:, :], ALU.add).then_inc(gt_dve, 1)

            dve.wait_ge(r_hi, 1)
            dve.tensor_tensor(R[:, 1, :, :], Rraw[:, :, :], f(R[:, 0, :, :]), ALU.subtract).then_inc(r_dve, 1)
            dve.wait_ge(q_dve, BATCH * len(Q_DVE))
            ln_stats(LN_LAST, 0)
            ln_low(LN_LAST, 0)
            mlp_chunk(0, ADEPTH, True)
            with dve.Fori(1, SHARED) as j:
                mlp_chunk(j * BATCH, ADEPTH + j, False)
            dve.wait_ge(r_pe, 1)
            dve.tensor_copy(lg[:, :, :].rearrange("p t n -> p (t n)"), bank[4][:, 0:BATCH * TT * EXPERTS]).then_inc(r_dve, 1)
            dve.wait_ge(r_dve, 1 + R_DVE.index("logits"))
            for t in range(BATCH * TT):
                ins = dve.max(top[:, t, :], lg[:, t, :])
            ins.then_inc(r_dve, 1)
            dve.wait_ge(r_dve, 1 + R_DVE.index("top"))
            dve.tensor_tensor(rt[:, 0, :], top[:, :, 1], top[:, :, 0], ALU.subtract).then_inc(r_dve, 1)
            dve.wait_ge(r_act, 1)
            dve.tensor_scalar(rt[:, 2, :], rt[:, 1, :], 1.0, None, ALU.add).then_inc(r_dve, 1)
            dve.wait_ge(r_dve, 1 + R_DVE.index("den"))
            dve.reciprocal(rt[:, 3, :], rt[:, 2, :]).then_inc(r_dve, 1)
            dve.wait_ge(r_dve, 1 + R_DVE.index("rden"))
            dve.tensor_tensor(rt[:, 4, :], rt[:, 1, :], rt[:, 3, :], ALU.mult).then_inc(r_dve, 1)
            dve.wait_ge(r_dve, 1 + R_DVE.index("w2"))
            dve.tensor_tensor(rt[:, 5, :], rt[:, 3, :], rt[:, 4, :], ALU.add).then_inc(r_dve, 1)
            dve.wait_ge(r_dve, 1 + R_DVE.index("comb"))
            mlp_chunk(SHARED * BATCH, ADEPTH + SHARED, False, routed=True)
            mlp_tail(GITEM - 1, BATCH - 1, True)

        @block.gpsimd
        def _(pool):
            pool.wait_ge(loaded, LOADS)
            pool.wait_ge(halves, 5)

            def round_high(hi, full):
                return pool.tensor_tensor(hi, full, one[:, 0:1].to_broadcast([P, SEQ]) if len(full.shape) == 2 else
                                          one[:, 0:1].unsqueeze(2).to_broadcast([P, TT, P]), ALU.mult)

            def ln_high(n, b):
                pool.wait_ge(ln_dve, at(n, LN_DVE, "vareps"))
                pool.tensor_tensor(rstd[:, :], ve[:, :], half[:, 0:TT], ALU.pow).then_inc(ln_pool, 1)
                for k in range(KT):
                    pool.wait_ge(ln_act, at(n, LN_ACT, f"x{k}"))
                    round_high(XT[:, 0, b, k, :], xtmp[:, k % 2, :]).then_inc(ln_pool, 1)

            def gate(i, b):
                pool.wait_ge(at_act, at(i, AT_ACT, "t"))
                pool.tensor_tensor(gt, gt, sg[:, b % 2, :], ALU.mult).then_inc(at_pool, 1)

            def attn_chunk(base, ln0):
                chunk0 = ln0 is not None
                for b in range(BATCH):
                    i = base + b
                    if chunk0 and b + 1 < BATCH:
                        ln_high(ln0 + b + 1, b + 1)
                    if not (chunk0 and b == 0):
                        gate(i - 1, (b - 1) % BATCH)
                    pool.wait_ge(a_dve, at(i, A_DVE, "v"))
                    vd = vdec.rearrange("p (t n) -> p t n", t=TT)
                    round_high(vH[:, 0, :, :], vd).then_inc(a_pool, 1)
                    pool.wait_ge(a_pool, at(i, A_POOL, "vhi"))
                    pool.tensor_tensor(vH[:, 1, :, :], vd, f(vH[:, 0, :, :]), ALU.subtract).then_inc(a_pool, 1)
                    for g in range(6):
                        pool.wait_ge(a_dve, at(i, A_DVE, f"s{g}"))
                        c0 = MASK_AT[g // 2]
                        if g < 4:
                            part = S[:, g % 2, :, c0:c0 + P]
                            m = causal[:, :].unsqueeze(1).to_broadcast([P, 2, P])
                        else:
                            part = S[:, g % 2, :, c0:SCOLS].rearrange("p s (m n) -> p s m n", n=P)[:, :, 0:3:2, :]
                            m = causal[:, :].unsqueeze(1).unsqueeze(1).to_broadcast([P, 2, 2, P])
                        pool.tensor_tensor(part, f(part), m, ALU.mult).then_inc(a_pool, 1)
                    pool.wait_ge(a_dve, at(i, A_DVE, "yc"))
                    pool.tensor_tensor(ysq, y, y, ALU.mult).then_inc(a_pool, 1)
                    pool.wait_ge(a_dve, at(i, A_DVE, "yvar"))
                    pool.tensor_tensor(yrs[:, :], yvar[:, :], half[:, :], ALU.pow).then_inc(a_pool, 1)

            def ffn_chunk(base, ln0):
                chunk0 = ln0 is not None
                for b in range(BATCH):
                    i = base + b
                    for ft in range(FT):
                        pool.wait_ge(f_act, at(i, F_ACT, f"h{ft}"))
                        if ft == 0 and not (chunk0 and b < 2):
                            pool.wait_ge(ft_pe, at(i - 2, FT_PE, "o3"))
                        round_high(H[:, b % 2, 0, ft, :], hid[:, ft, :]).then_inc(f_pool, 1)
                    if chunk0 and b + 1 < BATCH:
                        ln_high(ln0 + b + 1, b + 1)

            for b in range(BATCH):
                pool.wait_ge(i_dve, at(b, I_DVE, "vareps"))
                pool.tensor_tensor(rstd[:, :], ve[:, :], half[:, 0:TT], ALU.pow).then_inc(i_pool, 1)

            with pool.Fori(0, LAYERS) as layer:
                base, ln0 = layer * NITEM, layer * 2 * BATCH
                ln_high(ln0, 0)
                attn_chunk(base, ln0)
                with pool.Fori(1, CHUNKS) as c:
                    attn_chunk(base + c * BATCH, None)
                gate(base + NITEM - 1, BATCH - 1)
                ln_high(ln0 + BATCH, 0)
                ffn_chunk(base, ln0 + BATCH)
                with pool.Fori(1, CHUNKS) as c:
                    ffn_chunk(base + c * BATCH, None)

            def quant_stage(b, s):
                pool.wait_ge(q_dve, at(b, Q_DVE, f"ratio_{s}"))
                K = QK[s]
                pool.tensor_tensor(qs[:, 4, 0:K], qs[:, 3, 0:K], phalf[:, 0:K], ALU.pow).then_inc(q_pool, 1)
                pool.wait_ge(q_act, at(b, Q_ACT, f"row_s_{s}"))
                W = w_rows[s]
                pool.tensor_tensor(W, W, row[:, 0:K * P].unsqueeze(1).to_broadcast([P, 4, K * P]), ALU.mult).then_inc(q_pool, 1)

            with pool.Fori(0, BATCH) as b:
                pool.wait_ge(q_dve, at(b, Q_DVE, "vareps"))
                pool.tensor_tensor(rstd[:, :], ve[:, :], half[:, 0:TT], ALU.pow).then_inc(q_pool, 1)
                quant_stage(b, 1)
                quant_stage(b, 2)

            def mlp_chunk(base, chunk0):
                for b in range(BATCH):
                    i = base + b
                    for ft in range(2):
                        pool.wait_ge(g_dve, at(i, G_DVE, f"p{ft}"))
                        if ft == 0 and not (chunk0 and b < 2):
                            pool.wait_ge(gt_pe, at(i - 2, GT_PE, "o3"))
                        round_high(G[:, b % 2, 0, ft, :], hid[:, ft, :]).then_inc(g_pool, 1)
                    if chunk0 and b + 1 < BATCH:
                        ln_high(LN_LAST + b + 1, b + 1)

            ln_high(LN_LAST, 0)
            mlp_chunk(0, True)
            with pool.Fori(1, SHARED) as j:
                mlp_chunk(j * BATCH, False)
            mlp_chunk(SHARED * BATCH, False)


def kernel(**inputs):
    import numpy as np
    import concourse.bacc as bacc
    from concourse.bass_utils import run_bass_kernel_spmd as run

    I = {k: np.asarray(v) for k, v in inputs.items()}

    def column_blocks(w, n):
        K, N = w.shape
        return w.reshape(K // P, P, N // n, n).transpose(2, 1, 0, 3).reshape(N // n, P, K // P * n)

    def row_blocks(w, k):
        K, N = w.shape
        return w.reshape(K // k, k // P, P, N).transpose(0, 2, 1, 3).reshape(K // k, P, k // P * N)

    def columns(v):
        return v.reshape(-1, P).T

    L = range(LAYERS)
    arrays = {
        "x_rows": I["x"].reshape(BATCH * SEQ, DIM),
        "wa_attn": np.concatenate([np.stack([column_blocks(I["L0_attn_W" + r][l], P) for r in "qkvg"], 2)
                                   .reshape(CHUNKS, P, -1) for l in L]),
        "wb_attn": np.concatenate([row_blocks(I["L0_attn_Wo"][l], P) for l in L]),
        "wa_ffn": np.concatenate([column_blocks(I["L0_attn_W1"][l], FF // CHUNKS) for l in L]),
        "wb_ffn": np.concatenate([row_blocks(I["L0_attn_W2"][l], FF // CHUNKS) for l in L]),
        "param_columns": np.concatenate([columns(I["L0_attn_" + n]) for n in
                                         ("ln_gamma", "ln_beta", "gn_gamma", "gn_beta", "b1")], 1),
        "b2": I["L0_attn_b2"],
    }
    gammas = (1.0 - np.exp(np.linspace(np.log(1.0 / 32), np.log(1.0 / 128), HEADS))).astype(np.float32)
    steps = np.arange(SEQ) - SEQ // 2
    decay = np.stack([gammas.astype(np.float64)[:, None] ** -steps, gammas.astype(np.float64)[:, None] ** steps])
    arrays["consts"] = np.concatenate([np.eye(P), np.triu(np.ones((P, P)))], 1).astype(np.float32)
    arrays["decays"] = (decay.reshape(2, CHUNKS, 2, TT, P).transpose(4, 1, 0, 3, 2)
                        .reshape(P, -1).astype(np.float32))
    arrays["quant_w"] = np.stack([row_blocks(w, QO)[0] for w in I["fside_BxS2xS2_0"]])
    arrays["quant_ctx"] = np.stack([row_blocks(w, DIM)[0] for w in I["ctx_1024"]])
    gate, up = (np.concatenate([column_blocks(I["L0_ffn_" + p + n].T, GW) for p in ("sh_", "r_")]) for n in ("gate", "up"))
    arrays["wa_mlp"] = np.concatenate([gate, up], 2)
    arrays["wb_mlp"] = np.concatenate([row_blocks(I["L0_ffn_" + p + "down"].T, GW) for p in ("sh_", "r_")])
    arrays["router_w"] = column_blocks(I["L0_ffn_router_weight"].T, EXPERTS)[0]

    nc = bacc.Bacc("TRN2", target_bir_lowering=False, num_devices=1)
    arrays = {k + "_dram": np.ascontiguousarray(v) for k, v in arrays.items()}
    args = [nc.dram_tensor(k, v.shape, mybir.dt.from_np(v.dtype), kind="ExternalInput").ap() for k, v in arrays.items()]
    out = nc.dram_tensor("out_dram", (BATCH * SEQ, DIM), mybir.dt.float32, kind="ExternalOutput").ap()
    decoder_kernel(nc, *args, out)
    r = run(nc, [arrays], core_ids=[0])
    return r.results[0]["out_dram"].reshape(BATCH, SEQ, DIM)
```

```python
import concourse.bass as bass
from concourse import mybir
from contextlib import ExitStack

P = 128
BATCH, SEQ, DIM = 4, 512, 512
LAYERS, HEADS, FF = 2, 8, 2048
HEAD = DIM // HEADS
KT = DIM // P
TT = SEQ // P
CHUNKS = 4
FT = FF // CHUNKS // P
INTER, MOE = 2048, 256
GW = 256
GCH = INTER // GW
QO = 512
QI = QO // 2
EXPERTS = 8
EPS = 1e-5
QEPS = 1e-6
QMAX = 127.0
MAGIC = 1.5 * 2 ** 23
SHARED = INTER // GW
MASK_AT = [0, 512, 896, 1152]
SCOLS = 1280
SCORE_TILES = [[0], [1], [2, 3]]
SCORES_AT = [0, 512, 896]
SCORES_N = [512, 384, 384]

I_DVE = ["stats", "aggr", "vareps", "xn"]
LN_DVE = ["stats", "aggr", "vareps", "xn", "lo0", "lo1", "lo2", "lo3"]
LN_POOL = ["rstd"]
LN_PE = ["t0", "t1", "t2", "t3"]
LN_ACT = ["x0", "h0", "x1", "h1", "x2", "h2", "x3", "h3"]
A_PE = ["q", "k", "v", "s0", "s1", "g", "vt", "s2", "s3", "s4", "s5", "y"]
A_ACT = ["q", "k", "v", "s0", "s1", "g", "vhi", "s2", "s3", "s4", "s5"]
A_DVE = ["q", "k", "m0", "m1", "s0", "s1", "v", "m2", "m3", "s2", "s3", "m4", "m5", "s4", "s5"]
A_POOL = ["vlo"]
N_ACT = ["ylow", "ysq"]
N_DVE = ["y", "ysum", "ymean", "yc", "ysq", "yvar", "yn"]
N_POOL = ["rstd"]
AT_PE = ["t", "o0", "o1", "o2", "o3"]
AT_ACT = ["t", "hi"]
AT_DVE = ["gate", "lo", "o0", "o1", "o2", "o3"]
F_PE = ["h0", "h1", "h2", "h3"]
F_ACT = ["h0", "h1", "h2", "h3"]
F_DVE = ["lo0", "lo1", "lo2", "lo3"]
F_POOL = ["hi0", "hi1", "hi2", "hi3"]
FT_PE = ["o0", "o1", "o2", "o3"]
FT_DVE = ["o0", "o1", "o2", "o3"]
QK = {1: KT, 2: QI // P}
Q_PE = [n + s for s in "12" for k in [QK[int(s)]] for n in
        [f"x{j}_" for j in range(k)] + [f"w{j}_" for j in range(k)] + ["row_s_", "row_r_"]
        + [f"xq{j}_" for j in range(k)] + ["scale_row_"] + [f"wq{j}_" for j in range(k)]
        + [f"o{t}_" for t in range(TT)]]
Q_ACT = [n + s for s in "12" for k in [QK[int(s)]] for n in
         ["row_s_", "xq_", "xT_", "scale_row_", "wq_", "wT_"] + ["silu_"] * (s == "1")]
Q_DVE = ["x0", "stats", "aggr", "vareps", "xn"] + [n + s for s in "12" for k in [QK[int(s)]] for n in
         [f"x{j}_" for j in range(k)] + [f"w{j}_" for j in range(k)]
         + ["xmax_", "wmax_", "winv_", "ratio_", "s_", "rs_", "diag_", "xs_", "xabs_", "xscale_", "xrecip_", "xmul_", "xq_",
            "wabs_", "wscale_", "wrecip_", "diagw_", "wmul_", "wq_"]
         + [f"o{t}_" for t in range(TT)] + (["a_"] if s == "1" else ["add_"])]
Q_POOL = ["rstd"] + [n + s for s in "12" for n in ["s_", "ws_"]]
G_PE = ["g0", "u0", "g1", "u1"]
G_ACT = ["g0", "g1"]
G_DVE = ["p0", "lo0", "p1", "lo1"]
G_POOL = ["hi0", "hi1"]
GT_PE = ["o0", "o1", "o2", "o3"]
GT_DVE = ["o0", "o1", "o2", "o3"]
R_PE = ["l0", "l1", "l2", "l3", "t"]
R_ACT = ["l0", "l1", "l2", "l3", "exp"]
R_DVE = ["weights", "logits", "top", "gap", "den", "rden", "w2", "comb"]


def at(item, steps, name):
    return item * len(steps) + (steps.index(name) + 1)


def decoder_kernel(nc, x, wa_attn, wb_attn, wa_ffn, wb_ffn, params, b2, consts, decay,
                   q_w, q_ctx, wa_mlp, wb_mlp, router, out):
    f32, f32r, bf16 = mybir.dt.float32, mybir.dt.float32r, mybir.dt.bfloat16
    ALU = mybir.AluOpType
    ACT = mybir.ActivationFunctionType
    AX = mybir.AxisListType

    with ExitStack() as ctx:
        def sb(name, shape, dt):
            return ctx.enter_context(nc.sbuf_tensor(name, shape, dt))

        def sem(name):
            return ctx.enter_context(nc.semaphore(name))

        X = sb("resid", [P, BATCH * TT, DIM], f32)
        XT = sb("xT", [P, 2, BATCH, KT, SEQ], f32r)
        WA = sb("w_in", [P, 2, 2048], f32r)
        WB = sb("w_out", [P, 2, 2048], f32r)
        rawA = sb("raw_in", [P, 2048], f32)
        rawB = sb("raw_out", [P, 2048], f32)
        OP = sb("operands", [P, 8192], f32r)
        WK = sb("work", [P, 3584], f32)
        xn = sb("x_norm", [P, TT, DIM], f32)
        xtmp = sb("x_affine", [P, 2, SEQ], f32)
        ident = sb("ident", [P, P], f32)
        causal = sb("causal", [P, P], f32)
        prm = sb("params", [P, 56], f32)
        gncol = sb("gn_columns", [P, 2], f32)
        b1col = sb("b1_columns", [P, FT], f32)
        b2row = sb("b2_row", [P, DIM], f32)
        dec = sb("decay", [P, CHUNKS, 2, TT, 2], f32)
        half = sb("minus_half", [P, 8], f32)
        one = sb("one", [P, 1], f32)
        stats = sb("stats", [P, TT, 6], f32)
        mv = sb("mean_var", [P, TT, 2], f32)
        ve = sb("var_eps", [P, TT], f32)
        rstd = sb("rstd", [P, TT], f32)
        ysum = sb("y_sum", [P, 8], f32)
        ymean = sb("y_mean", [P, 8], f32)
        yssq = sb("y_sumsq", [P, 8], f32)
        yvar = sb("y_var", [P, 8], f32)
        yrs = sb("y_rstd", [P, 8], f32)
        bank = [ctx.enter_context(nc.psum_tensor(f"bank{i}", [P, 512], f32)) for i in range(8)]

        ones = sb("ones", [P, P], f32)
        identb = sb("ident_bf16", [P, P], bf16)
        Rraw = sb("router_raw", [P, KT, EXPERTS], f32)
        R = sb("router", [P, 2, KT, EXPERTS], f32r)
        lg = b2row[:, 0:128].rearrange("p (t n) -> p t n", n=EXPERTS)
        lgT = xn[0:EXPERTS, :, :]
        top = b2row[:, 128:256].rearrange("p (t n) -> p t n", n=8)
        rt = b2row[:, 256:352].rearrange("p (k t) -> p k t", k=6)
        qs = sb("quant_scales", [P, 12, 4], f32)
        phalf = sb("plus_half", [P, 4], f32)

        xrows = xn
        w_rows = {1: rawA[:, :].rearrange("p (t n) -> p t n", t=4),
                  2: WK[:, 0:1024].rearrange("p (t n) -> p t n", t=4)}
        hrows = rawB[:, :].rearrange("p (t n) -> p t n", t=4)
        xT_q = WK[:, 1024:2048].bitcast(bf16).rearrange("p (k n) -> p k n", k=KT)
        wT_q = WK[:, 2048:3072].bitcast(bf16).rearrange("p (k n) -> p k n", k=KT)
        row = WK[:, 3072:3584]
        diag = xtmp[:, :, :].rearrange("p a (k n) -> p a k n", k=KT)
        qrow = xtmp[:, :, :].rearrange("p a n -> p (a n)").bitcast(bf16).rearrange("p (t n) -> p t n", t=4)
        G = OP[:, 0:4096].rearrange("p (i s f n) -> p i s f n", i=2, s=2, f=2)
        wg = WA[:, :, :].rearrange("p s (r k n) -> p s r k n", r=2, k=KT)
        wd = WB[:, :, 0:1024].rearrange("p s (k n) -> p s k n", k=2)
        qT = OP[:, 0:1024].rearrange("p (s n) -> p s n", s=2)
        kT = OP[:, 1024:2048].rearrange("p (s n) -> p s n", s=2)
        vH = OP[:, 2048:3072].rearrange("p (t r s n) -> p t r s n", t=TT, r=2, s=2)
        S = OP[:, 3072:3072 + 4 * SCOLS].rearrange("p (r s n) -> p r s n", r=2, s=2)
        gated = WB[:, :, 1536:2048]
        wq4 = WA[:, :, :].rearrange("p s (r k n) -> p s r k n", r=4, k=KT)
        H = OP[:, :].rearrange("p (i s f n) -> p i s f n", i=2, s=2, f=FT)
        w1 = WA[:, :, :].rearrange("p s (k n) -> p s k n", k=KT)
        w2 = WB[:, :, :].rearrange("p s (k n) -> p s k n", k=FT)
        vraw = WK[:, 0:512]
        vdec = WK[:, 512:1024]
        sg = WK[:, 1536:2048]
        y = WK[:, 2048:2560]
        ylow = WK[:, 2560:3072].rearrange("p (t r n) -> p t r n", t=TT, r=2)
        ysq = WK[:, 2560:3072]
        gt = WK[:, 3072:3584]
        hid = WK[:, 0:2048].rearrange("p (f n) -> p f n", f=FT)
        lng, lnb = prm[:, 0:4], prm[:, 4:8]
        gn = prm[:, 8:24].rearrange("p (a c) -> p a c", a=2)
        b1 = prm[:, 24:56].rearrange("p (c f) -> p c f", f=FT)

        loaded = sem("consts_loaded")
        halves = sem("minus_half_set")
        rawA_in, rawB_in, b2_in = sem("raw_in_loaded"), sem("raw_out_loaded"), sem("b2_loaded")
        x_in = [sem(f"x_loaded{b}") for b in range(BATCH)]
        out_done = sem("out_stored")
        wa_hi, wa_lo = sem("w_in_hi"), sem("w_in_lo")
        wb_hi, wb_lo = sem("w_out_hi"), sem("w_out_lo")
        b2_added = sem("b2_added")
        i_dve, i_pool = sem("first_norm_dve"), sem("first_norm_pool")
        gn_col, b1_col = sem("gn_columns_set"), sem("b1_columns_set")
        ln_dve, ln_pool, ln_pe, ln_act = sem("ln_dve"), sem("ln_pool"), sem("ln_pe"), sem("ln_act")
        a_pe, a_act, a_dve, a_pool = sem("attn_pe"), sem("attn_act"), sem("attn_dve"), sem("attn_pool")
        n_act, n_dve, n_pool = sem("head_norm_act"), sem("head_norm_dve"), sem("head_norm_pool")
        at_pe, at_act, at_dve = sem("attn_out_pe"), sem("attn_out_act"), sem("attn_out_dve")
        f_pe, f_act, f_dve, f_pool = sem("ffn_pe"), sem("ffn_act"), sem("ffn_dve"), sem("ffn_pool")
        ft_pe, ft_dve = sem("ffn_out_pe"), sem("ffn_out_dve")
        q_in, qc_in, x0_in = sem("quant_w_loaded"), sem("quant_ctx_loaded"), sem("x_again_loaded")
        q_pe, q_act, q_dve, q_pool = sem("quant_pe"), sem("quant_act"), sem("quant_dve"), sem("quant_pool")
        g_pe, g_act, g_dve, g_pool = sem("mlp_pe"), sem("mlp_act"), sem("mlp_dve"), sem("mlp_pool")
        gt_pe, gt_dve = sem("mlp_out_pe"), sem("mlp_out_dve")
        r_pe, r_act, r_dve, r_hi = sem("router_pe"), sem("router_act"), sem("router_dve"), sem("router_hi")
        block = ctx.enter_context(nc.Block())

        def f(ap):
            return ap.bitcast(f32)

        def split_product(pe, out_, w, v, start, stop):
            (wh, wl), (vh, vl) = w, v
            pe.matmul(out_, wh, vh, start=start, stop=False)
            pe.matmul(out_, wh, vl, start=False, stop=False)
            return pe.matmul(out_, wl, vh, start=False, stop=stop)

        def hl(ap, *i):
            return ap[(slice(None), 0, *i)], ap[(slice(None), 1, *i)]

        LOADS = 16 * 5
        GITEM = (SHARED + 1) * BATCH
        ADEPTH = LAYERS * 2 * CHUNKS
        LN_LAST = LAYERS * 2 * BATCH + 1
        LAST = CHUNKS - 1
        NITEM = CHUNKS * BATCH

        def norm_beside(b, ln0, ln_next):
            if ln0 is not None and b + 1 < BATCH:
                return ln0 + b + 1, b + 1
            if ln_next is not None and b == BATCH - 1:
                return ln_next, 0
            return None

        @block.sync
        def _(sp):
            sp.dma_start(prm[:, :], params).then_inc(loaded, 16)
            sp.dma_start(ident[:, :], consts[:, 0:P]).then_inc(loaded, 16)
            sp.dma_start(causal[:, :], consts[:, P:2 * P]).then_inc(loaded, 16)
            sp.dma_start(dec[:, :, :, :, :].rearrange("p a b c d -> p (a b c d)"), decay).then_inc(loaded, 16)
            sp.dma_start(Rraw[:, :, :].rearrange("p k n -> p (k n)"), router).then_inc(loaded, 16)
            for b in range(BATCH):
                sp.dma_start(X[:, b * TT:(b + 1) * TT, :],
                             x[b * SEQ:(b + 1) * SEQ, :].rearrange("(t p) n -> p t n", p=P)).then_inc(x_in[b], 16)

            def load_w(w_a, cols_a, w_b, cols_b, j, chunk):
                sp.wait_ge(wa_lo, chunk + 1)
                sp.dma_start(rawA[:, 0:cols_a], w_a[bass.ds(j, 1), :, :].rearrange("o p n -> p (o n)")).then_inc(rawA_in, 16)
                sp.wait_ge(wb_lo, chunk + 1)
                sp.dma_start(rawB[:, 0:cols_b], w_b[bass.ds(j, 1), :, :].rearrange("o p n -> p (o n)")).then_inc(rawB_in, 16)

            with sp.Fori(0, LAYERS) as layer:
                sp.wait_ge(b2_added, layer * BATCH + 1)
                sp.dma_start(b2row[:, :], b2[bass.ds(layer, 1), :].rearrange("o n -> (o n)").partition_broadcast(P)).then_inc(b2_in, 16)
                with sp.Fori(0, CHUNKS) as c:
                    load_w(wa_attn, 2048, wb_attn, 512, layer * CHUNKS + c, layer * 2 * CHUNKS + c)
                with sp.Fori(0, CHUNKS) as c:
                    load_w(wa_ffn, 2048, wb_ffn, 2048, layer * CHUNKS + c, layer * 2 * CHUNKS + CHUNKS + c)
            sp.wait_ge(wa_lo, ADEPTH + 1)
            sp.dma_start(rawA[:, :], wa_mlp[0]).then_inc(rawA_in, 16)
            sp.wait_ge(wa_lo, ADEPTH + 2)
            sp.wait_ge(wb_lo, ADEPTH + 1)
            sp.wait_ge(ft_dve, LAYERS * NITEM * len(FT_DVE))
            def load_quant(b):
                sp.dma_start(rawB[:, :].rearrange("p (t n) -> p t n", t=TT),
                             x[bass.ds(b * SEQ, SEQ), :].rearrange("(t p) n -> p t n", p=P)).then_inc(x0_in, 16)
                sp.dma_start(rawA[:, :], q_w[bass.ds(b, 1), :, :].rearrange("o p n -> p (o n)")).then_inc(q_in, 16)
                sp.dma_start(WK[:, 0:1024], q_ctx[bass.ds(b, 1), :, :].rearrange("o p n -> p (o n)")).then_inc(qc_in, 16)

            load_quant(0)
            with sp.Fori(1, BATCH) as b:
                sp.wait_ge(q_dve, b * len(Q_DVE))
                load_quant(b)
            sp.wait_ge(q_dve, BATCH * len(Q_DVE))
            sp.dma_start(rawB[:, 0:1024], wb_mlp[0]).then_inc(rawB_in, 16)
            with sp.Fori(1, SHARED + 1) as j:
                load_w(wa_mlp, 2048, wb_mlp, 1024, j, ADEPTH + j)
            for b in range(BATCH):
                sp.wait_ge(gt_dve, at(SHARED * BATCH + b, GT_DVE, "o3"))
                sp.dma_start(out[b * SEQ:(b + 1) * SEQ, :].rearrange("(t p) n -> p t n", p=P),
                             X[:, b * TT:(b + 1) * TT, :]).then_inc(out_done, 16)
            sp.wait_ge(out_done, 16 * BATCH)

        @block.tensor
        def _(pe):
            pe.wait_ge(loaded, LOADS)
            pe.wait_ge(halves, 5)

            def ln_transpose(n, bank0, free=None):
                pe.wait_ge(ln_dve, at(n, LN_DVE, "xn"))
                for k in range(KT):
                    if k < 2:
                        if free:
                            free(k)
                    else:
                        pe.wait_ge(ln_act, at(n, LN_ACT, f"h{k - 2}"))
                    for t in range(TT):
                        mm = pe.transpose(bank[bank0 + k % 2][:, t * P:(t + 1) * P], xn[:, t, k * P:(k + 1) * P], ident[:, :])
                    mm.then_inc(ln_pe, 1)

            def xt_ready(n):
                pe.wait_ge(ln_act, at(n, LN_ACT, "h3"))
                pe.wait_ge(ln_dve, at(n, LN_DVE, "lo3"))

            def attn_role(b, role, n):
                for k in range(KT):
                    mm = split_product(pe, bank[n][:, :], hl(wq4, "qkvg".index(role), k), hl(XT, b, k), k == 0, k == KT - 1)
                mm.then_inc(a_pe, 1)

            def attn_scores(i, pair):
                for r in range(2):
                    if pair:
                        pe.wait_ge(a_dve, at(i, A_DVE, f"s{2 * pair - 2 + r}"))
                    rows = slice(64 * r, 64 * r + 64)
                    for m in SCORE_TILES[pair]:
                        o = bank[2 + r][:, MASK_AT[m] - SCORES_AT[pair]:MASK_AT[m] - SCORES_AT[pair] + SEQ - m * P]
                        mm = split_product(pe, o,
                                           (kT[rows, 0, m * P:(m + 1) * P], kT[rows, 1, m * P:(m + 1) * P]),
                                           (qT[rows, 0, m * P:SEQ], qT[rows, 1, m * P:SEQ]), True, True)
                    mm.then_inc(a_pe, 1)

            def attn_values(i):
                pe.wait_ge(a_act, at(i, A_ACT, "vhi"))
                pe.wait_ge(a_pool, at(i, A_POOL, "vlo"))
                for n in range(TT):
                    pe.wait_ge(a_dve, at(i, A_DVE, f"s{min(2 * n, 4) + 1}"))
                    for r in range(2):
                        o = bank[5 - r][:, n * P:(n + 1) * P]
                        for m in range(n + 1):
                            c = MASK_AT[m] + (n - m) * P
                            pe.matmul(o, S[:, r, 0, c:c + P], vH[:, m, r, :, :].rearrange("p s n -> p (s n)"),
                                      start=m == 0, stop=False)
                            mm = pe.matmul(o[:, 0:HEAD], S[:, r, 1, c:c + P], vH[:, m, r, 0, :],
                                           start=False, stop=m == n)
                mm.then_inc(a_pe, 1)

            def attn_out_transpose(i):
                pe.wait_ge(n_dve, at(i, N_DVE, "yn"))
                for t in range(TT):
                    mm = pe.transpose(bank[4][:, t * P:(t + 1) * P], y[:, t * P:(t + 1) * P], ident[:, :])
                mm.then_inc(at_pe, 1)

            def attn_out(i, tiles, first):
                pe.wait_ge(at_act, at(i, AT_ACT, "hi"))
                pe.wait_ge(at_dve, at(i, AT_DVE, "lo"))
                for t in tiles:
                    if t >= 2:
                        pe.wait_ge(at_dve, at(i, AT_DVE, f"o{t - 2}"))
                    elif not first:
                        pe.wait_ge(at_dve, at(i - 1, AT_DVE, f"o{t + 2}"))
                    split_product(pe, bank[6 + t % 2][:, :],
                                  (gated[:, 0, t * P:(t + 1) * P], gated[:, 1, t * P:(t + 1) * P]),
                                  (WB[:, 0, 0:DIM], WB[:, 1, 0:DIM]), True, True).then_inc(at_pe, 1)

            def attn_chunk(base, gc, ln0=None, ln_next=None):
                chunk0 = ln0 is not None
                pe.wait_ge(wa_hi, gc + 1)
                pe.wait_ge(wa_lo, gc + 2)
                for b in range(BATCH):
                    i = base + b
                    first = chunk0 and b == 0
                    if chunk0:
                        xt_ready(ln0 + b)
                    if not first:
                        pe.wait_ge(a_act, at(i - 1, A_ACT, "v"))
                    attn_role(b, "q", 0)
                    if not first:
                        pe.wait_ge(a_act, at(i - 1, A_ACT, "g"))
                    attn_role(b, "k", 1)
                    pe.wait_ge(a_dve, at(i, A_DVE, "q"))
                    attn_role(b, "v", 0)
                    pe.wait_ge(a_dve, at(i, A_DVE, "k"))
                    attn_scores(i, 0)
                    if not first:
                        attn_out_transpose(i - 1)
                    attn_role(b, "g", 1)
                    pe.wait_ge(a_act, at(i, A_ACT, "v"))
                    if not first:
                        pe.wait_ge(at_act, at(i - 1, AT_ACT, "t"))
                    for t in range(TT):
                        mm = pe.transpose(bank[4][:, t * P:(t + 1) * P], vraw[:, t * P:(t + 1) * P], ident[:, :])
                    mm.then_inc(a_pe, 1)
                    attn_scores(i, 1)
                    norm = norm_beside(b, ln0, ln_next)
                    if norm:
                        ln_transpose(norm[0], 0, lambda k: pe.wait_ge(a_act, at(i, A_ACT, "vg"[k])))
                    if b == 1:
                        pe.wait_ge(wb_hi, gc + 1)
                        pe.wait_ge(wb_lo, gc + 2)
                    if not first:
                        attn_out(i - 1, (0, 1), chunk0 and b == 1)
                    attn_scores(i, 2)
                    if not first:
                        attn_out(i - 1, (2, 3), False)
                    attn_values(i)

            def ffn_head(b, i, chunk0, attn_last):
                for ft in range(FT):
                    if not (chunk0 and b == 0):
                        pe.wait_ge(f_act, at(i - 1, F_ACT, f"h{ft}"))
                    if attn_last is not None and ft == FT - 1:
                        attn_out_transpose(attn_last)
                    for k in range(KT):
                        mm = split_product(pe, bank[ft][:, :], hl(w1, k, slice(ft * P, (ft + 1) * P)), hl(XT, b, k),
                                           k == 0, k == KT - 1)
                    mm.then_inc(f_pe, 1)

            def ffn_out(b, i, first):
                pe.wait_ge(f_dve, at(i, F_DVE, "lo3"))
                pe.wait_ge(f_pool, at(i, F_POOL, "hi3"))
                for t in range(TT):
                    if t >= 2:
                        pe.wait_ge(ft_dve, at(i, FT_DVE, f"o{t - 2}"))
                    elif not first:
                        pe.wait_ge(ft_dve, at(i - 1, FT_DVE, f"o{t + 2}"))
                    for k in range(FT):
                        mm = split_product(pe, bank[6 + t % 2][:, :], hl(H[:, b % 2], k, slice(t * P, (t + 1) * P)),
                                           hl(w2, k), k == 0, k == FT - 1)
                    mm.then_inc(ft_pe, 1)

            def ffn_chunk(base, gc, ln0=None, ln_next=None, attn_last=None):
                chunk0 = ln0 is not None
                pe.wait_ge(wa_hi, gc + 1)
                pe.wait_ge(wa_lo, gc + 2)
                for b in range(BATCH):
                    i = base + b
                    if chunk0:
                        xt_ready(ln0 + b)
                    ffn_head(b, i, chunk0, attn_last if b == 0 else None)
                    norm = norm_beside(b, ln0, ln_next)
                    if chunk0 and b == 0:
                        attn_out(attn_last, range(TT), False)
                        ln_transpose(norm[0], 4)
                    else:
                        if norm:
                            ln_transpose(norm[0], 4)
                        if b == 1:
                            pe.wait_ge(wb_hi, gc + 1)
                            pe.wait_ge(wb_lo, gc + 2)
                        ffn_out((b - 1) % BATCH, i - 1, chunk0 and b == 1)

            ln_transpose(0, 0)
            with pe.Fori(0, LAYERS) as layer:
                base, gc, ln0 = layer * NITEM, layer * 2 * CHUNKS, layer * 2 * BATCH
                attn_chunk(base, gc, ln0=ln0)
                with pe.Fori(1, LAST) as c:
                    attn_chunk(base + c * BATCH, gc + c)
                attn_chunk(base + LAST * BATCH, gc + LAST, ln_next=ln0 + BATCH)
                ffn_chunk(base, gc + CHUNKS, ln0=ln0 + BATCH, attn_last=base + NITEM - 1)
                with pe.Fori(1, LAST) as c:
                    ffn_chunk(base + c * BATCH, gc + CHUNKS + c)
                ffn_chunk(base + LAST * BATCH, gc + CHUNKS + LAST, ln_next=ln0 + 2 * BATCH)
                ffn_out(BATCH - 1, base + NITEM - 1, False)

            def quant_stage(b, s):
                K = QK[s]
                W = w_rows[s]
                if s == 1:
                    pe.wait_ge(q_dve, at(b, Q_DVE, "xn"))
                else:
                    pe.wait_ge(q_dve, at(b, Q_DVE, "a_1"))
                for k in range(K):
                    if k >= 2:
                        pe.wait_ge(q_dve, at(b, Q_DVE, f"x{k - 2}_{s}"))
                    for t in range(TT):
                        mm = pe.transpose(bank[k % 2][:, t * P:(t + 1) * P], xrows[:, t, k * P:(k + 1) * P], ident[:, :])
                    mm.then_inc(q_pe, 1)
                pe.wait_ge([q_in, qc_in][s - 1], 16 * (b + 1))
                for k in range(K):
                    if k >= 2:
                        pe.wait_ge(q_dve, at(b, Q_DVE, f"w{k - 2}_{s}"))
                    for t in range(TT):
                        mm = pe.transpose(bank[6 + k % 2][:, t * P:(t + 1) * P], W[:, t, k * P:(k + 1) * P], ident[:, :])
                    mm.then_inc(q_pe, 1)
                pe.wait_ge(q_dve, at(b, Q_DVE, f"diag_{s}"))
                for a in range(2):
                    for k in range(K):
                        mm = pe.matmul(bank[2 + a][:, k * P:(k + 1) * P], ones[:, :], diag[:, a, k, :], start=True, stop=True)
                    mm.then_inc(q_pe, 1)
                pe.wait_ge(q_act, at(b, Q_ACT, f"xq_{s}"))
                for k in range(K):
                    for t in range(TT):
                        mm = pe.transpose(bank[k].bitcast(bf16)[:, t * P:(t + 1) * P] if k < 2 else
                                          bank[4 + k % 2].bitcast(bf16)[:, t * P:(t + 1) * P],
                                          qrow[:, t, k * P:(k + 1) * P], identb[:, :])
                    mm.then_inc(q_pe, 1)
                pe.wait_ge(q_dve, at(b, Q_DVE, f"diagw_{s}"))
                for k in range(4):
                    mm = pe.matmul(bank[2][:, k * P:(k + 1) * P], ones[:, :], diag[:, 0, k, :], start=True, stop=True)
                mm.then_inc(q_pe, 1)
                pe.wait_ge(q_act, at(b, Q_ACT, f"wq_{s}"))
                for k in range(K):
                    for t in range(4):
                        mm = pe.transpose([bank[6], bank[7], bank[3], bank[0]][k].bitcast(bf16)[:, t * P:(t + 1) * P],
                                          qrow[:, t, k * P:(k + 1) * P], identb[:, :])
                    mm.then_inc(q_pe, 1)
                pe.wait_ge(q_act, at(b, Q_ACT, f"wT_{s}"))
                for t in range(TT):
                    if t >= 2:
                        pe.wait_ge(q_dve, at(b, Q_DVE, f"o{t - 2}_{s}"))
                    for k in range(K):
                        mm = pe.matmul(bank[4 + t % 2][:, :], xT_q[:, k, t * P:(t + 1) * P], wT_q[:, k, :],
                                       start=k == 0, stop=k == K - 1)
                    mm.then_inc(q_pe, 1)

            with pe.Fori(0, BATCH) as b:
                quant_stage(b, 1)
                quant_stage(b, 2)

            def mlp_head(b, i, chunk0, first):
                for n, (role, ft) in enumerate([(0, 0), (1, 0), (0, 1), (1, 1)]):
                    if not first:
                        sem_, steps, name = (g_act, G_ACT, f"g{ft}") if role == 0 else (g_dve, G_DVE, f"p{ft}")
                        pe.wait_ge(sem_, at(i - 1, steps, name))
                    for k in range(KT):
                        mm = split_product(pe, bank[n][:, :], hl(wg, role, k, slice(ft * P, (ft + 1) * P)), hl(XT, b, k),
                                           k == 0, k == KT - 1)
                    mm.then_inc(g_pe, 1)

            def mlp_out(b, i, first):
                pe.wait_ge(g_dve, at(i, G_DVE, "lo1"))
                for t in range(TT):
                    if t >= 2:
                        pe.wait_ge(gt_dve, at(i, GT_DVE, f"o{t - 2}"))
                    elif not first:
                        pe.wait_ge(gt_dve, at(i - 1, GT_DVE, f"o{t + 2}"))
                    for k in range(2):
                        mm = split_product(pe, bank[6 + t % 2][:, :], hl(G[:, b % 2], k, slice(t * P, (t + 1) * P)),
                                           hl(wd, k), k == 0, k == 1)
                    mm.then_inc(gt_pe, 1)

            def mlp_chunk(base, gc, chunk0):
                pe.wait_ge(wa_hi, gc + 1)
                pe.wait_ge(wa_lo, gc + 2)
                for b in range(BATCH):
                    i = base + b
                    first = chunk0 and b == 0
                    if chunk0:
                        xt_ready(LN_LAST + b)
                    mlp_head(b, i, chunk0, first)
                    if chunk0 and b + 1 < BATCH:
                        ln_transpose(LN_LAST + b + 1, 4)
                    if b == 1:
                        pe.wait_ge(wb_hi, gc + 1)
                        pe.wait_ge(wb_lo, gc + 2)
                    if not first:
                        mlp_out((b - 1) % BATCH, i - 1, chunk0 and b == 1)

            pe.wait_ge(q_dve, BATCH * len(Q_DVE))
            ln_transpose(LN_LAST, 4)
            mlp_chunk(0, ADEPTH, True)
            pe.wait_ge(r_hi, 1)
            pe.wait_ge(r_dve, at(0, R_DVE, "weights"))
            for b in range(BATCH):
                if b >= 2:
                    pe.wait_ge(r_act, at(0, R_ACT, f"l{b - 2}"))
                for k in range(KT):
                    mm = split_product(pe, bank[4 + b % 2][0:EXPERTS, :], hl(R, k), hl(XT, b, k), k == 0, k == KT - 1)
                mm.then_inc(r_pe, 1)
            for b in range(BATCH):
                pe.wait_ge(r_act, at(0, R_ACT, f"l{b}"))
                if b == 0:
                    pe.wait_ge(r_act, at(0, R_ACT, "l2"))
                for t in range(TT):
                    bt = b * TT + t
                    mm = pe.transpose(bank[4][:, bt * EXPERTS:(bt + 1) * EXPERTS], lgT[:, b, t * P:(t + 1) * P],
                                      ident[0:EXPERTS, 0:EXPERTS])
            mm.then_inc(r_pe, 1)
            with pe.Fori(1, SHARED) as j:
                mlp_chunk(j * BATCH, ADEPTH + j, False)
            mlp_chunk(SHARED * BATCH, ADEPTH + SHARED, False)
            mlp_out(BATCH - 1, GITEM - 1, False)

        @block.scalar
        def _(act):
            act.wait_ge(loaded, LOADS)

            def split_in(gc, last_use):
                act.wait_ge(rawA_in, 16 * (gc + 1))
                last_use()
                act.activation(WA[:, 0, :], rawA[:, :], ACT.Copy).then_inc(wa_hi, 1)

            def split_out(gc, cols, last_use):
                act.wait_ge(rawB_in, 16 * (gc + 1))
                last_use()
                act.activation(WB[:, 0, 0:cols], rawB[:, 0:cols], ACT.Copy).then_inc(wb_hi, 1)

            def ln_affine(norm, bank0):
                n, b = norm
                for k in range(KT):
                    act.wait_ge(ln_pe, at(n, LN_PE, f"t{k}"))
                    if k >= 2:
                        act.wait_ge(ln_dve, at(n, LN_DVE, f"lo{k - 2}"))
                    for dst in (xtmp[:, k % 2, :], XT[:, 0, b, k, :]):
                        act.activation(dst, bank[bank0 + k % 2][:, :], ACT.Identity,
                                       scale=lng[:, k:k + 1], bias=lnb[:, k:k + 1]).then_inc(ln_act, 1)

            def attn_chunk(base, gc, lc, ln0=None, ln_next=None):
                chunk0 = ln0 is not None
                for b in range(BATCH):
                    i = base + b
                    first = chunk0 and b == 0
                    if not first:
                        attn_low_sums(i - 1)
                    act.wait_ge(a_pe, at(i, A_PE, "q"))
                    act.activation(qT[:, 0, :], bank[0][:, :], ACT.Copy).then_inc(a_act, 1)
                    if not first:
                        attn_squares(i - 1)
                    if b == 1:
                        attn_columns(lc)
                    act.wait_ge(a_pe, at(i, A_PE, "k"))
                    act.activation(kT[:, 0, :], bank[1][:, :], ACT.Copy).then_inc(a_act, 1)
                    act.wait_ge(a_pe, at(i, A_PE, "v"))
                    act.activation(vraw, bank[0][:, :], ACT.Copy).then_inc(a_act, 1)
                    attn_scores_hi(i, 0, 0)
                    if not first:
                        attn_tail_t(i - 1, lc - 1 if b == 0 else lc)
                    attn_scores_hi(i, 0, 1)
                    if not first:
                        attn_tail_hi(i - 1)
                    act.wait_ge(a_pe, at(i, A_PE, "g"))
                    act.activation(sg, bank[1][:, :], ACT.Silu).then_inc(a_act, 1)
                    act.wait_ge(a_dve, at(i, A_DVE, "v"))
                    act.activation(vH.rearrange("p t r s n -> p (t r) s n")[:, :, 0, :],
                                   vdec.rearrange("p (g n) -> p g n", n=HEAD), ACT.Copy).then_inc(a_act, 1)
                    attn_scores_hi(i, 1, 0)
                    attn_scores_hi(i, 1, 1)
                    norm = norm_beside(b, ln0, ln_next)
                    if norm:
                        ln_affine(norm, 0)
                    attn_scores_hi(i, 2, 0)
                    attn_scores_hi(i, 2, 1)
                    if b == 0:
                        split_out(gc, DIM, lambda: None if chunk0 else act.wait_ge(at_pe, at(i - 1, AT_PE, "o3")))
                    if b == BATCH - 1:
                        split_in(gc + 1, lambda: act.wait_ge(a_pe, at(i, A_PE, "g")))

            def attn_low_sums(i):
                act.wait_ge(a_pe, at(i, A_PE, "y"))
                for r in range(2):
                    ins = act.activation(ylow[:, :, r, :], bank[5 - r][:, :].rearrange("p (t s n) -> p t s n", t=TT, s=2)[:, :, 1, :],
                                         ACT.Copy)
                ins.then_inc(n_act, 1)

            def attn_squares(i):
                act.wait_ge(n_dve, at(i, N_DVE, "yc"))
                act.activation(ysq, y, ACT.Square).then_inc(n_act, 1)

            def attn_scores_hi(i, pair, r):
                act.wait_ge(a_dve, at(i, A_DVE, f"m{2 * pair + r}"))
                col, n = SCORES_AT[pair], SCORES_N[pair]
                act.activation(S[:, r, 0, col:col + n], bank[2 + r][:, 0:n], ACT.Copy).then_inc(a_act, 1)

            def attn_columns(lc):
                act.activation(gncol[:, :], gn[:, :, bass.ds(lc, 1)].rearrange("p a o -> p (a o)"), ACT.Copy).then_inc(gn_col, 1)

            def attn_tail_t(i, lc):
                act.wait_ge(gn_col, lc + 1)
                act.wait_ge(at_pe, at(i, AT_PE, "t"))
                act.activation(gt, bank[4][:, :], ACT.Identity, scale=gncol[:, 0:1],
                               bias=gncol[:, 1:2]).then_inc(at_act, 1)

            def attn_tail_hi(i):
                act.wait_ge(at_dve, at(i, AT_DVE, "gate"))
                act.activation(gated[:, 0, :], gt, ACT.Copy).then_inc(at_act, 1)

            def ffn_chunk(base, gc, lc, ln0=None, ln_next=None, attn_last=None):
                chunk0 = ln0 is not None
                if not chunk0:
                    act.wait_ge(f_act, at(base - 1, F_ACT, "h3"))
                act.activation(b1col[:, :], b1[:, bass.ds(lc, 1), :].rearrange("p o f -> p (o f)"), ACT.Copy).then_inc(b1_col, 1)
                act.wait_ge(b1_col, lc + 1)
                if attn_last is not None:
                    attn_low_sums(attn_last)
                    attn_squares(attn_last)
                for b in range(BATCH):
                    i = base + b
                    first = chunk0 and b == 0
                    for ft in range(FT):
                        if first and ft == FT - 1:
                            attn_tail_t(attn_last, lc + LAST)
                            attn_tail_hi(attn_last)
                        act.wait_ge(f_pe, at(i, F_PE, f"h{ft}"))
                        if not first:
                            act.wait_ge(f_dve, at(i - 1, F_DVE, f"lo{ft}"))
                            act.wait_ge(f_pool, at(i - 1, F_POOL, f"hi{ft}"))
                        act.activation(hid[:, ft, :], bank[ft][:, :], ACT.Gelu_apprx_tanh,
                                       bias=b1col[:, ft:ft + 1]).then_inc(f_act, 1)
                    norm = norm_beside(b, ln0, ln_next)
                    if norm:
                        ln_affine(norm, 4)
                    if b == 0:
                        split_out(gc, 2048, lambda: act.wait_ge(at_pe, at(attn_last, AT_PE, "o3")) if chunk0 else
                                  act.wait_ge(ft_pe, at(i - 1, FT_PE, "o3")))
                    if b == BATCH - 1:
                        split_in(gc + 1, lambda: act.wait_ge(f_pe, at(i, F_PE, "h3")))

            split_in(0, lambda: None)
            ln_affine((0, 0), 0)
            with act.Fori(0, LAYERS) as layer:
                base, gc, ln0 = layer * NITEM, layer * 2 * CHUNKS, layer * 2 * BATCH
                attn_chunk(base, gc, layer * CHUNKS, ln0=ln0)
                with act.Fori(1, LAST) as c:
                    attn_chunk(base + c * BATCH, gc + c, layer * CHUNKS + c)
                attn_chunk(base + LAST * BATCH, gc + LAST, layer * CHUNKS + LAST, ln_next=ln0 + BATCH)
                ffn_chunk(base, gc + CHUNKS, layer * CHUNKS, ln0=ln0 + BATCH, attn_last=base + NITEM - 1)
                with act.Fori(1, LAST) as c:
                    ffn_chunk(base + c * BATCH, gc + CHUNKS + c, layer * CHUNKS + c)
                ffn_chunk(base + LAST * BATCH, gc + CHUNKS + LAST, layer * CHUNKS + LAST, ln_next=ln0 + 2 * BATCH)

            def quant_stage(b, s):
                K = QK[s]
                D = K * P
                W = w_rows[s]
                act.wait_ge(q_pe, at(b, Q_PE, f"row_s_{s}"))
                act.activation(row[:, 0:D], bank[2][:, 0:D], ACT.Copy).then_inc(q_act, 1)
                act.wait_ge(q_pe, at(b, Q_PE, f"row_r_{s}"))
                act.wait_ge(q_dve, at(b, Q_DVE, f"xq_{s}"))
                act.activation(qrow[:, :, 0:D], xrows[:, :, 0:D], ACT.Copy, bias=-MAGIC).then_inc(q_act, 1)
                for k in range(K):
                    act.wait_ge(q_pe, at(b, Q_PE, f"xq{k}_{s}"))
                    src = (bank[k] if k < 2 else bank[4 + k % 2]).bitcast(bf16)[:, 0:SEQ]
                    ins = act.activation(xT_q[:, k, :], src, ACT.Copy)
                ins.then_inc(q_act, 1)
                act.wait_ge(q_pool, at(b, Q_POOL, f"ws_{s}"))
                act.wait_ge(q_pe, at(b, Q_PE, f"scale_row_{s}"))
                act.activation(row, bank[2][:, :], ACT.Copy).then_inc(q_act, 1)
                act.wait_ge(q_dve, at(b, Q_DVE, f"wq_{s}"))
                act.activation(qrow[:, :, 0:D], W, ACT.Copy, bias=-MAGIC).then_inc(q_act, 1)
                for k in range(K):
                    act.wait_ge(q_pe, at(b, Q_PE, f"wq{k}_{s}"))
                    src = [bank[6], bank[7], bank[3], bank[0]][k].bitcast(bf16)[:, 0:QO]
                    ins = act.activation(wT_q[:, k, :], src, ACT.Copy)
                ins.then_inc(q_act, 1)
                if s == 1:
                    act.wait_ge(q_dve, at(b, Q_DVE, "o3_1"))
                    act.activation(xrows[:, :, 0:QI], hrows[:, :, 0:QI], ACT.Silu).then_inc(q_act, 1)

            with act.Fori(0, BATCH) as b:
                quant_stage(b, 1)
                quant_stage(b, 2)

            def ln_copy(b):
                n = LN_LAST + b
                for k in range(KT):
                    act.wait_ge(ln_pe, at(n, LN_PE, f"t{k}"))
                    if k >= 2:
                        act.wait_ge(ln_dve, at(n, LN_DVE, f"lo{k - 2}"))
                    for dst in (xtmp[:, k % 2, :], XT[:, 0, b, k, :]):
                        act.activation(dst, bank[4 + k % 2][:, :], ACT.Copy).then_inc(ln_act, 1)

            def mlp_chunk(base, gc, chunk0, last=False):
                for b in range(BATCH):
                    i = base + b
                    for ft in range(2):
                        act.wait_ge(g_pe, at(i, G_PE, f"g{ft}"))
                        if not (chunk0 and b == 0):
                            act.wait_ge(g_dve, at(i - 1, G_DVE, f"lo{ft}"))
                            act.wait_ge(g_pool, at(i - 1, G_POOL, f"hi{ft}"))
                        act.activation(hid[:, ft, :], bank[2 * ft][:, :], ACT.Silu).then_inc(g_act, 1)
                    if chunk0 and b + 1 < BATCH:
                        ln_copy(b + 1)
                    if b == 0:
                        split_out(gc, 1024, lambda: None if chunk0 else act.wait_ge(gt_pe, at(i - 1, GT_PE, "o3")))
                    if b == BATCH - 1 and not last:
                        split_in(gc + 1, lambda: act.wait_ge(g_pe, at(i, G_PE, "u1")))

            act.activation(R[:, 0, :, :], Rraw[:, :, :], ACT.Copy).then_inc(r_hi, 1)
            ln_copy(0)
            mlp_chunk(0, ADEPTH, True)
            for b in range(BATCH):
                act.wait_ge(r_pe, at(0, R_PE, f"l{b}"))
                act.activation(lgT[:, b, :], bank[4 + b % 2][0:EXPERTS, :], ACT.Copy).then_inc(r_act, 1)
            act.wait_ge(r_dve, at(0, R_DVE, "gap"))
            act.activation(rt[:, 1, :], rt[:, 0, :], ACT.Exp).then_inc(r_act, 1)
            with act.Fori(1, SHARED) as j:
                mlp_chunk(j * BATCH, ADEPTH + j, False)
            mlp_chunk(SHARED * BATCH, ADEPTH + SHARED, False, last=True)

        @block.vector
        def _(dve):
            dve.wait_ge(loaded, LOADS)
            dve.memset(half[:, :], -0.5).then_inc(halves, 1)
            dve.memset(phalf[:, :], 0.5).then_inc(halves, 1)
            dve.memset(ones[:, :], 1.0).then_inc(halves, 1)
            dve.tensor_copy(identb[:, :], ident[:, :]).then_inc(halves, 1)
            dve.memset(one[:, :], 1.0).then_inc(halves, 1)
            for n, s in enumerate((wa_lo, wb_lo, b2_added)):
                dve.memset(yvar[:, n:n + 1], 0.0).then_inc(s, 1)

            def split_in(gc):
                dve.wait_ge(wa_hi, gc + 1)
                dve.tensor_tensor(WA[:, 1, :], rawA[:, :], f(WA[:, 0, :]), ALU.subtract).then_inc(wa_lo, 1)

            def split_out(gc, cols):
                dve.wait_ge(wb_hi, gc + 1)
                dve.tensor_tensor(WB[:, 1, 0:cols], rawB[:, 0:cols], f(WB[:, 0, 0:cols]), ALU.subtract).then_inc(wb_lo, 1)

            def ln_stats(norm):
                n, b = norm
                for t in range(TT):
                    ins = dve.bn_stats(stats[:, t, :], X[:, b * TT + t, :])
                ins.then_inc(ln_dve, 1)

            def ln_var(norm):
                n, b = norm
                dve.wait_ge(ln_dve, at(n, LN_DVE, "stats"))
                dve.memset(ve[:, :], 0.0)
                for t in range(TT):
                    ins = dve.bn_aggr(mv[:, t, :], stats[:, t, :])
                ins.then_inc(ln_dve, 1)
                dve.wait_ge(ln_dve, at(n, LN_DVE, "aggr"))
                dve.tensor_scalar(ve[:, :], mv[:, :, 1], EPS, None, ALU.add).then_inc(ln_dve, 1)

            def ln_rows(norm):
                n, b = norm
                dve.wait_ge(ln_pool, at(n, LN_POOL, "rstd"))
                for t in range(TT):
                    ins = dve.tensor_scalar(xn[:, t, :], X[:, b * TT + t, :], mv[:, t, 0:1], rstd[:, t:t + 1],
                                            ALU.subtract, ALU.mult)
                ins.then_inc(ln_dve, 1)

            def ln_low(norm, tiles=range(KT)):
                n, b = norm
                for k in tiles:
                    dve.wait_ge(ln_act, at(n, LN_ACT, f"h{k}"))
                    dve.tensor_tensor(XT[:, 1, b, k, :], xtmp[:, k % 2, :], f(XT[:, 0, b, k, :]), ALU.subtract).then_inc(ln_dve, 1)

            def low(dst, full, hi):
                return dve.tensor_tensor(dst, full, f(hi), ALU.subtract)

            def attn_chunk(base, gc, c, ln0=None, ln_next=None, layer=None):
                chunk0 = ln0 is not None
                for b in range(BATCH):
                    i = base + b
                    first = chunk0 and b == 0
                    norm = norm_beside(b, ln0, ln_next)
                    if not first:
                        attn_norm_mean(i - 1)
                    dve.wait_ge(a_act, at(i, A_ACT, "q"))
                    low(qT[:, 1, :], bank[0][:, :], qT[:, 0, :]).then_inc(a_dve, 1)
                    if not first:
                        attn_norm_var(i - 1, c - 1 if b == 0 else c)
                    dve.wait_ge(a_act, at(i, A_ACT, "k"))
                    low(kT[:, 1, :], bank[1][:, :], kT[:, 0, :]).then_inc(a_dve, 1)
                    if not first:
                        attn_norm_scale(i - 1)
                    if norm:
                        ln_stats(norm)
                        ln_var(norm)
                    attn_mask(i, 0)
                    attn_scores_low(i, 0, 0)
                    if not first:
                        attn_gate(i - 1)
                    attn_scores_low(i, 0, 1)
                    if not first:
                        attn_tail_lo(i - 1)
                    if norm:
                        ln_rows(norm)
                        if ln_next is not None:
                            add_b2(layer, 0, ln_next)
                    dve.wait_ge(a_pe, at(i, A_PE, "vt"))
                    dve.tensor_tensor(vdec.rearrange("p (t r n) -> p t r n", t=TT, r=2),
                                      bank[4][:, :].rearrange("p (t r n) -> p t r n", t=TT, r=2),
                                      dec[:, bass.ds(c, 1), 0, :, :].rearrange("p o t r -> p (o t) r").unsqueeze(3).to_broadcast([P, TT, 2, HEAD]),
                                      ALU.mult).then_inc(a_dve, 1)
                    attn_mask(i, 1)
                    attn_scores_low(i, 1, 0)
                    attn_scores_low(i, 1, 1)
                    if norm:
                        ln_low(norm, range(0, 2))
                    if not first:
                        attn_tail_out(i - 1, (b - 1) % BATCH, (0, 1))
                    attn_mask(i, 2)
                    attn_scores_low(i, 2, 0)
                    attn_scores_low(i, 2, 1)
                    if norm:
                        ln_low(norm, range(2, KT))
                    if not first:
                        attn_tail_out(i - 1, (b - 1) % BATCH, (2, 3))
                    if b == 0:
                        split_out(gc, DIM)
                    if b == BATCH - 1:
                        split_in(gc + 1)

            def attn_mask(i, pair):
                for r in range(2):
                    dve.wait_ge(a_pe, at(i, A_PE, f"s{2 * pair + r}"))
                    for m in SCORE_TILES[pair]:
                        tile = bank[2 + r][:, MASK_AT[m] - SCORES_AT[pair]:MASK_AT[m] - SCORES_AT[pair] + P]
                        ins = dve.tensor_tensor(tile, tile, causal[:, :], ALU.mult)
                    ins.then_inc(a_dve, 1)

            def attn_scores_low(i, pair, r):
                dve.wait_ge(a_act, at(i, A_ACT, f"s{2 * pair + r}"))
                col, n = SCORES_AT[pair], SCORES_N[pair]
                low(S[:, r, 1, col:col + n], bank[2 + r][:, 0:n], S[:, r, 0, col:col + n]).then_inc(a_dve, 1)

            y8 = y.rearrange("p (g n) -> p g n", n=HEAD)

            def attn_norm_mean(i):
                dve.wait_ge(n_act, at(i, N_ACT, "ylow"))
                for r in range(2):
                    ins = dve.tensor_tensor(y.rearrange("p (t r n) -> p t r n", t=TT, r=2)[:, :, r, :],
                                            bank[5 - r][:, :].rearrange("p (t s n) -> p t s n", t=TT, s=2)[:, :, 0, :],
                                            ylow[:, :, r, :], ALU.add)
                ins.then_inc(n_dve, 1)
                dve.wait_ge(n_dve, at(i, N_DVE, "y"))
                dve.tensor_reduce(ysum[:, :], y8, AX.X, ALU.add).then_inc(n_dve, 1)
                dve.wait_ge(n_dve, at(i, N_DVE, "ysum"))
                dve.tensor_scalar(ymean[:, :], ysum[:, :], 1.0 / HEAD, None, ALU.mult).then_inc(n_dve, 1)
                dve.wait_ge(n_dve, at(i, N_DVE, "ymean"))
                dve.tensor_tensor(y8, y8, ymean[:, :].unsqueeze(2).to_broadcast([P, 8, HEAD]), ALU.subtract).then_inc(n_dve, 1)

            def attn_norm_var(i, c):
                dve.wait_ge(n_act, at(i, N_ACT, "ysq"))
                dve.tensor_reduce(yssq[:, :], ysq.rearrange("p (g n) -> p g n", n=HEAD), AX.X, ALU.add).then_inc(n_dve, 1)
                dve.wait_ge(n_dve, at(i, N_DVE, "ysq"))
                dve.scalar_tensor_tensor(out=yvar[:, :], in0=yssq[:, :], scalar=1.0 / HEAD,
                                         in1=dec[:, bass.ds(c, 1), 1, :, :].rearrange("p o t r -> p (o t r)"),
                                         op0=ALU.mult, op1=ALU.add).then_inc(n_dve, 1)

            def attn_norm_scale(i):
                dve.wait_ge(n_pool, at(i, N_POOL, "rstd"))
                dve.tensor_tensor(y8, y8, yrs[:, :].unsqueeze(2).to_broadcast([P, 8, HEAD]), ALU.mult).then_inc(n_dve, 1)

            def attn_gate(i):
                dve.wait_ge(at_act, at(i, AT_ACT, "t"))
                dve.tensor_tensor(gt, gt, sg, ALU.mult).then_inc(at_dve, 1)

            def attn_tail_lo(i):
                dve.wait_ge(at_act, at(i, AT_ACT, "hi"))
                low(gated[:, 1, :], gt, gated[:, 0, :]).then_inc(at_dve, 1)

            def attn_tail_out(i, b, tiles):
                for t in tiles:
                    dve.wait_ge(at_pe, at(i, AT_PE, f"o{t}"))
                    dve.tensor_tensor(X[:, b * TT + t, :], X[:, b * TT + t, :], bank[6 + t % 2][:, :], ALU.add).then_inc(at_dve, 1)

            def ffn_chunk(base, gc, layer, ln0=None, ln_next=None, attn_last=None):
                chunk0 = ln0 is not None
                for b in range(BATCH):
                    i = base + b
                    first = chunk0 and b == 0
                    norm = norm_beside(b, ln0, ln_next)
                    def rows():
                        ln_stats(norm)
                        ln_var(norm)
                        ln_rows(norm)
                        if chunk0:
                            add_b2(layer, b + 1, ln0 + b + 1)
                    if first:
                        attn_norm_mean(attn_last)
                        attn_norm_var(attn_last, LAST)
                        attn_norm_scale(attn_last)
                    elif norm:
                        rows()
                    for ft in range(FT):
                        dve.wait_ge(f_pool, at(i, F_POOL, f"hi{ft}"))
                        low(H[:, b % 2, 1, ft, :], hid[:, ft, :], H[:, b % 2, 0, ft, :]).then_inc(f_dve, 1)
                        if first and ft == FT - 2:
                            attn_gate(attn_last)
                            attn_tail_lo(attn_last)
                    if first:
                        attn_tail_out(attn_last, BATCH - 1, (0, 1))
                        rows()
                        attn_tail_out(attn_last, BATCH - 1, (2, 3))
                        ln_low(norm)
                    else:
                        if norm:
                            ln_low(norm, range(0, 2))
                        ffn_tail(i - 1, (b - 1) % BATCH, (0,))
                        if b == BATCH - 1:
                            split_in(gc + 1)
                        if norm:
                            ln_low(norm, range(2, KT))
                        ffn_tail(i - 1, (b - 1) % BATCH, (1, 2, 3))
                    if b == 0:
                        split_out(gc, 2048)

            def ffn_tail(i, b, tiles=range(TT)):
                for t in tiles:
                    dve.wait_ge(ft_pe, at(i, FT_PE, f"o{t}"))
                    dve.tensor_tensor(X[:, b * TT + t, :], X[:, b * TT + t, :], bank[6 + t % 2][:, :], ALU.add).then_inc(ft_dve, 1)

            def add_b2(layer, b, n):
                dve.wait_ge(b2_in, 16 * (layer + 1))
                dve.wait_ge(ln_dve, at(n, LN_DVE, "xn"))
                dve.tensor_tensor(X[:, b * TT:(b + 1) * TT, :], X[:, b * TT:(b + 1) * TT, :],
                                  b2row[:, :].unsqueeze(1).to_broadcast([P, TT, DIM]), ALU.add).then_inc(b2_added, 1)

            split_in(0)
            for b in range(BATCH):
                dve.wait_ge(x_in[b], 16)
                for t in range(TT):
                    ins = dve.bn_stats(stats[:, t, :], X[:, b * TT + t, :])
                ins.then_inc(i_dve, 1)
                dve.wait_ge(i_dve, at(b, I_DVE, "stats"))
                for t in range(TT):
                    ins = dve.bn_aggr(mv[:, t, :], stats[:, t, :])
                ins.then_inc(i_dve, 1)
                dve.wait_ge(i_dve, at(b, I_DVE, "aggr"))
                dve.tensor_scalar(ve[:, :], mv[:, :, 1], EPS, None, ALU.add).then_inc(i_dve, 1)
                dve.wait_ge(i_pool, b + 1)
                for t in range(TT):
                    Xt = X[:, b * TT + t, :]
                    ins = dve.tensor_scalar(Xt, Xt, mv[:, t, 0:1], rstd[:, t:t + 1], ALU.subtract, ALU.mult)
                ins.then_inc(i_dve, 1)
                if b == 0:
                    dve.wait_ge(i_dve, at(0, I_DVE, "xn"))
                    ln_stats((0, 0))
                    ln_var((0, 0))
                    ln_rows((0, 0))
                if b == 1:
                    ln_low((0, 0))
            dve.wait_ge(i_dve, BATCH * len(I_DVE))

            with dve.Fori(0, LAYERS) as layer:
                base, gc, ln0 = layer * NITEM, layer * 2 * CHUNKS, layer * 2 * BATCH
                attn_chunk(base, gc, 0, ln0=ln0)
                with dve.Fori(1, LAST) as c:
                    attn_chunk(base + c * BATCH, gc + c, c)
                attn_chunk(base + LAST * BATCH, gc + LAST, LAST, ln_next=ln0 + BATCH, layer=layer)
                ffn_chunk(base, gc + CHUNKS, layer, ln0=ln0 + BATCH, attn_last=base + NITEM - 1)
                with dve.Fori(1, LAST) as c:
                    ffn_chunk(base + c * BATCH, gc + CHUNKS + c, layer)
                ffn_chunk(base + LAST * BATCH, gc + CHUNKS + LAST, layer, ln_next=ln0 + 2 * BATCH)
                ffn_tail(base + NITEM - 1, BATCH - 1)

            AX_, AW, WI, RA, S_, RS, XM, XS, XR, WM, WS, WR = range(12)

            def quant_stage(b, s):
                K = QK[s]
                D = K * P
                W = w_rows[s]

                def done(name):
                    dve.wait_ge(q_dve, at(b, Q_DVE, f"{name}_{s}"))

                for k in range(K):
                    dve.wait_ge(q_pe, at(b, Q_PE, f"x{k}_{s}"))
                    dve.tensor_reduce(qs[:, AX_, k:k + 1], bank[k % 2][:, :], AX.X, ALU.max,
                                      apply_absolute_value=True).then_inc(q_dve, 1)
                for k in range(K):
                    dve.wait_ge(q_pe, at(b, Q_PE, f"w{k}_{s}"))
                    dve.tensor_reduce(qs[:, AW, k:k + 1], bank[6 + k % 2][:, :], AX.X, ALU.max,
                                      apply_absolute_value=True).then_inc(q_dve, 1)
                done(f"w{K - 1}")
                dve.tensor_scalar(qs[:, AX_, 0:K], qs[:, AX_, 0:K], QEPS, None, ALU.max).then_inc(q_dve, 1)
                dve.tensor_scalar(qs[:, AW, 0:K], qs[:, AW, 0:K], QEPS, None, ALU.max).then_inc(q_dve, 1)
                done("wmax")
                dve.reciprocal(qs[:, WI, 0:K], qs[:, AW, 0:K]).then_inc(q_dve, 1)
                done("winv")
                dve.tensor_tensor(qs[:, RA, 0:K], qs[:, AX_, 0:K], qs[:, WI, 0:K], ALU.mult).then_inc(q_dve, 1)
                dve.wait_ge(q_pool, at(b, Q_POOL, f"s_{s}"))
                dve.tensor_scalar(qs[:, S_, 0:K], qs[:, S_, 0:K], QEPS, None, ALU.max).then_inc(q_dve, 1)
                done("s")
                dve.reciprocal(qs[:, RS, 0:K], qs[:, S_, 0:K]).then_inc(q_dve, 1)
                done("rs")
                for a, r in enumerate((S_, RS)):
                    for k in range(K):
                        ins = dve.tensor_scalar(diag[:, a, k, :], ident[:, :], qs[:, r, k:k + 1], None, ALU.mult)
                ins.then_inc(q_dve, 1)

                def rounded(V, recip, mul):
                    for t in range(4):
                        ins = dve.tensor_scalar(V[:, t, 0:D], V[:, t, 0:D], qs[:, recip, t:t + 1], -QMAX, ALU.mult, ALU.max)
                    ins.then_inc(q_dve, 1)
                    done(mul)
                    dve.tensor_scalar(V[:, :, 0:D], V[:, :, 0:D], QMAX, MAGIC, ALU.min, ALU.add).then_inc(q_dve, 1)

                dve.wait_ge(q_pe, at(b, Q_PE, f"row_r_{s}"))
                dve.tensor_tensor(xrows[:, :, 0:D], xrows[:, :, 0:D], bank[3][:, 0:D].unsqueeze(1).to_broadcast([P, TT, D]),
                                  ALU.mult).then_inc(q_dve, 1)
                done("xs")
                dve.tensor_reduce(qs[:, XM, :], xrows[:, :, 0:D], AX.X, ALU.max, apply_absolute_value=True).then_inc(q_dve, 1)
                done("xabs")
                dve.tensor_scalar(qs[:, XS, :], qs[:, XM, :], QEPS, 1.0 / QMAX, ALU.max, ALU.mult).then_inc(q_dve, 1)
                done("xscale")
                dve.reciprocal(qs[:, XR, :], qs[:, XS, :]).then_inc(q_dve, 1)
                done("xrecip")
                rounded(xrows, XR, "xmul")
                dve.wait_ge(q_pool, at(b, Q_POOL, f"ws_{s}"))
                dve.tensor_reduce(qs[:, WM, :], W, AX.X, ALU.max, apply_absolute_value=True).then_inc(q_dve, 1)
                done("wabs")
                dve.tensor_scalar(qs[:, WS, :], qs[:, WM, :], QEPS, 1.0 / QMAX, ALU.max, ALU.mult).then_inc(q_dve, 1)
                done("wscale")
                dve.reciprocal(qs[:, WR, :], qs[:, WS, :]).then_inc(q_dve, 1)
                dve.wait_ge(q_pe, at(b, Q_PE, f"xq{K - 1}_{s}"))
                for k in range(4):
                    ins = dve.tensor_scalar(diag[:, 0, k, :], ident[:, :], qs[:, WS, k:k + 1], None, ALU.mult)
                ins.then_inc(q_dve, 1)
                done("wrecip")
                rounded(W, WR, "wmul")
                dve.wait_ge(q_act, at(b, Q_ACT, f"scale_row_{s}"))
                for t in range(TT):
                    dve.wait_ge(q_pe, at(b, Q_PE, f"o{t}_{s}"))
                    dve.scalar_tensor_tensor(out=hrows[:, t, :], in0=bank[4 + t % 2][:, :], scalar=qs[:, XS, t:t + 1],
                                             in1=row, op0=ALU.mult, op1=ALU.mult).then_inc(q_dve, 1)

            with dve.Fori(0, BATCH) as b:
                Xb = X[:, bass.ds(b * TT, TT), :]
                dve.wait_ge(x0_in, 16 * (b + 1))
                dve.tensor_tensor(Xb, Xb, hrows, ALU.add).then_inc(q_dve, 1)
                dve.wait_ge(q_dve, at(b, Q_DVE, "x0"))
                dve.memset(ve[:, :], 0.0)
                for t in range(TT):
                    ins = dve.bn_stats(stats[:, t, :], X[:, bass.ds(b * TT + t, 1), :].rearrange("p o n -> p (o n)"))
                ins.then_inc(q_dve, 1)
                dve.wait_ge(q_dve, at(b, Q_DVE, "stats"))
                dve.memset(ve[:, :], 0.0)
                for t in range(TT):
                    ins = dve.bn_aggr(mv[:, t, :], stats[:, t, :])
                ins.then_inc(q_dve, 1)
                dve.wait_ge(q_dve, at(b, Q_DVE, "aggr"))
                dve.tensor_scalar(ve[:, :], mv[:, :, 1], EPS, None, ALU.add).then_inc(q_dve, 1)
                dve.wait_ge(q_pool, at(b, Q_POOL, "rstd"))
                for t in range(TT):
                    ins = dve.tensor_scalar(xn[:, t, :], X[:, bass.ds(b * TT + t, 1), :].rearrange("p o n -> p (o n)"),
                                            mv[:, t, 0:1], rstd[:, t:t + 1], ALU.subtract, ALU.mult)
                ins.then_inc(q_dve, 1)
                quant_stage(b, 1)
                dve.wait_ge(q_act, at(b, Q_ACT, "silu_1"))
                dve.tensor_tensor(xrows[:, :, 0:QI], xrows[:, :, 0:QI], hrows[:, :, QI:QO], ALU.mult).then_inc(q_dve, 1)
                quant_stage(b, 2)
                dve.wait_ge(q_dve, at(b, Q_DVE, "o3_2"))
                dve.tensor_tensor(Xb, Xb, hrows, ALU.add).then_inc(q_dve, 1)

            def mlp_chunk(base, gc, chunk0, routed=False):
                for b in range(BATCH):
                    i = base + b
                    norm = (LN_LAST + b + 1, b + 1) if chunk0 and b + 1 < BATCH else None
                    tail = not (chunk0 and b == 0)

                    def product(ft):
                        dve.wait_ge(g_pe, at(i, G_PE, f"u{ft}"))
                        dve.wait_ge(g_act, at(i, G_ACT, f"g{ft}"))
                        dve.tensor_tensor(hid[:, ft, :], hid[:, ft, :], bank[2 * ft + 1][:, :], ALU.mult).then_inc(g_dve, 1)

                    def product_low(ft):
                        dve.wait_ge(g_pool, at(i, G_POOL, f"hi{ft}"))
                        low(G[:, b % 2, 1, ft, :], hid[:, ft, :], G[:, b % 2, 0, ft, :]).then_inc(g_dve, 1)

                    if norm:
                        ln_stats(norm)
                        ln_var(norm)
                        ln_rows(norm)
                    product(0)
                    product_low(0)
                    product(1)
                    if norm:
                        ln_low(norm, range(0, 2))
                    if tail:
                        mlp_tail(i - 1, (b - 1) % BATCH, routed and b > 0, (0, 1))
                    product_low(1)
                    if b == BATCH - 1 and not routed:
                        split_in(gc + 1)
                    if norm:
                        ln_low(norm, range(2, KT))
                    if tail:
                        mlp_tail(i - 1, (b - 1) % BATCH, routed and b > 0, (2, 3))
                    if b == 0:
                        split_out(gc, 1024)

            def mlp_tail(i, b, routed, tiles=range(TT)):
                for t in tiles:
                    dve.wait_ge(gt_pe, at(i, GT_PE, f"o{t}"))
                    Xt = X[:, b * TT + t, :]
                    if routed:
                        dve.scalar_tensor_tensor(out=Xt, in0=bank[6 + t % 2][:, :], scalar=rt[:, 5, b * TT + t:b * TT + t + 1],
                                                 in1=Xt, op0=ALU.mult, op1=ALU.add).then_inc(gt_dve, 1)
                    else:
                        dve.tensor_tensor(Xt, Xt, bank[6 + t % 2][:, :], ALU.add).then_inc(gt_dve, 1)

            dve.wait_ge(r_hi, 1)
            dve.tensor_tensor(R[:, 1, :, :], Rraw[:, :, :], f(R[:, 0, :, :]), ALU.subtract).then_inc(r_dve, 1)
            dve.wait_ge(q_dve, BATCH * len(Q_DVE))
            ln_stats((LN_LAST, 0))
            ln_var((LN_LAST, 0))
            ln_rows((LN_LAST, 0))
            ln_low((LN_LAST, 0))
            mlp_chunk(0, ADEPTH, True)
            dve.wait_ge(r_pe, at(0, R_PE, "t"))
            dve.tensor_copy(lg[:, :, :].rearrange("p t n -> p (t n)"), bank[4][:, 0:BATCH * TT * EXPERTS]).then_inc(r_dve, 1)
            dve.wait_ge(r_dve, at(0, R_DVE, "logits"))
            for t in range(BATCH * TT):
                ins = dve.max(top[:, t, :], lg[:, t, :])
            ins.then_inc(r_dve, 1)
            dve.wait_ge(r_dve, at(0, R_DVE, "top"))
            dve.tensor_tensor(rt[:, 0, :], top[:, :, 1], top[:, :, 0], ALU.subtract).then_inc(r_dve, 1)
            dve.wait_ge(r_act, at(0, R_ACT, "exp"))
            dve.tensor_scalar(rt[:, 2, :], rt[:, 1, :], 1.0, None, ALU.add).then_inc(r_dve, 1)
            dve.wait_ge(r_dve, at(0, R_DVE, "den"))
            dve.reciprocal(rt[:, 3, :], rt[:, 2, :]).then_inc(r_dve, 1)
            dve.wait_ge(r_dve, at(0, R_DVE, "rden"))
            dve.tensor_tensor(rt[:, 4, :], rt[:, 1, :], rt[:, 3, :], ALU.mult).then_inc(r_dve, 1)
            dve.wait_ge(r_dve, at(0, R_DVE, "w2"))
            dve.tensor_tensor(rt[:, 5, :], rt[:, 3, :], rt[:, 4, :], ALU.add).then_inc(r_dve, 1)
            dve.wait_ge(r_dve, at(0, R_DVE, "comb"))
            with dve.Fori(1, SHARED) as j:
                mlp_chunk(j * BATCH, ADEPTH + j, False)
            mlp_chunk(SHARED * BATCH, ADEPTH + SHARED, False, routed=True)
            mlp_tail(GITEM - 1, BATCH - 1, True)

        @block.gpsimd
        def _(pool):
            pool.wait_ge(loaded, LOADS)
            pool.wait_ge(halves, 5)

            def round_high(hi, full):
                return pool.tensor_tensor(hi, full, one[:, 0:1].to_broadcast([P, SEQ]), ALU.mult)

            def ln_rstd(n):
                pool.wait_ge(ln_dve, at(n, LN_DVE, "vareps"))
                pool.tensor_tensor(rstd[:, :], ve[:, :], half[:, 0:TT], ALU.pow).then_inc(ln_pool, 1)

            def attn_norm_rstd(i):
                pool.wait_ge(n_dve, at(i, N_DVE, "yvar"))
                pool.tensor_tensor(yrs[:, :], yvar[:, :], half[:, :], ALU.pow).then_inc(n_pool, 1)

            def attn_chunk(base, ln0=None, ln_next=None):
                for b in range(BATCH):
                    i = base + b
                    if not (ln0 is not None and b == 0):
                        attn_norm_rstd(i - 1)
                    norm = norm_beside(b, ln0, ln_next)
                    if norm:
                        ln_rstd(norm[0])
                    pool.wait_ge(a_act, at(i, A_ACT, "vhi"))
                    v8 = vH.rearrange("p t r s n -> p (t r) s n")
                    pool.tensor_tensor(v8[:, :, 1, :], vdec.rearrange("p (g n) -> p g n", n=HEAD), f(v8[:, :, 0, :]),
                                       ALU.subtract).then_inc(a_pool, 1)

            def ffn_chunk(base, ln0=None, ln_next=None, attn_last=None):
                for b in range(BATCH):
                    i = base + b
                    first = ln0 is not None and b == 0
                    norm = norm_beside(b, ln0, ln_next)
                    if first:
                        attn_norm_rstd(attn_last)
                    elif norm:
                        ln_rstd(norm[0])
                    for ft in range(FT):
                        pool.wait_ge(f_act, at(i, F_ACT, f"h{ft}"))
                        if ft == 0 and not (ln0 is not None and b < 2):
                            pool.wait_ge(ft_pe, at(i - 2, FT_PE, "o3"))
                        round_high(H[:, b % 2, 0, ft, :], hid[:, ft, :]).then_inc(f_pool, 1)
                    if first:
                        ln_rstd(norm[0])

            for b in range(BATCH):
                pool.wait_ge(i_dve, at(b, I_DVE, "vareps"))
                pool.tensor_tensor(rstd[:, :], ve[:, :], half[:, 0:TT], ALU.pow).then_inc(i_pool, 1)
                if b == 0:
                    ln_rstd(0)

            with pool.Fori(0, LAYERS) as layer:
                base, ln0 = layer * NITEM, layer * 2 * BATCH
                attn_chunk(base, ln0=ln0)
                with pool.Fori(1, LAST) as c:
                    attn_chunk(base + c * BATCH)
                attn_chunk(base + LAST * BATCH, ln_next=ln0 + BATCH)
                ffn_chunk(base, ln0=ln0 + BATCH, attn_last=base + NITEM - 1)
                with pool.Fori(1, LAST) as c:
                    ffn_chunk(base + c * BATCH)
                ffn_chunk(base + LAST * BATCH, ln_next=ln0 + 2 * BATCH)

            def quant_stage(b, s):
                pool.wait_ge(q_dve, at(b, Q_DVE, f"ratio_{s}"))
                K = QK[s]
                pool.tensor_tensor(qs[:, 4, 0:K], qs[:, 3, 0:K], phalf[:, 0:K], ALU.pow).then_inc(q_pool, 1)
                pool.wait_ge(q_act, at(b, Q_ACT, f"row_s_{s}"))
                W = w_rows[s]
                pool.tensor_tensor(W, W, row[:, 0:K * P].unsqueeze(1).to_broadcast([P, 4, K * P]), ALU.mult).then_inc(q_pool, 1)

            with pool.Fori(0, BATCH) as b:
                pool.wait_ge(q_dve, at(b, Q_DVE, "vareps"))
                pool.tensor_tensor(rstd[:, :], ve[:, :], half[:, 0:TT], ALU.pow).then_inc(q_pool, 1)
                quant_stage(b, 1)
                quant_stage(b, 2)

            def mlp_chunk(base, chunk0):
                for b in range(BATCH):
                    i = base + b
                    if chunk0 and b + 1 < BATCH:
                        ln_rstd(LN_LAST + b + 1)
                    for ft in range(2):
                        pool.wait_ge(g_dve, at(i, G_DVE, f"p{ft}"))
                        if ft == 0 and not (chunk0 and b < 2):
                            pool.wait_ge(gt_pe, at(i - 2, GT_PE, "o3"))
                        round_high(G[:, b % 2, 0, ft, :], hid[:, ft, :]).then_inc(g_pool, 1)

            ln_rstd(LN_LAST)
            mlp_chunk(0, True)
            with pool.Fori(1, SHARED) as j:
                mlp_chunk(j * BATCH, False)
            mlp_chunk(SHARED * BATCH, False)


def kernel(**inputs):
    import numpy as np
    import concourse.bacc as bacc
    from concourse.bass_utils import run_bass_kernel_spmd as run

    I = {k: np.asarray(v) for k, v in inputs.items()}

    def column_blocks(w, n):
        K, N = w.shape
        return w.reshape(K // P, P, N // n, n).transpose(2, 1, 0, 3).reshape(N // n, P, K // P * n)

    def row_blocks(w, k):
        K, N = w.shape
        return w.reshape(K // k, k // P, P, N).transpose(0, 2, 1, 3).reshape(K // k, P, k // P * N)

    def columns(v):
        return v.reshape(-1, P).T

    L = range(LAYERS)
    arrays = {
        "x_rows": I["x"].reshape(BATCH * SEQ, DIM),
        "wa_attn": np.concatenate([np.stack([column_blocks(I["L0_attn_W" + r][l], P) for r in "qkvg"], 2)
                                   .reshape(CHUNKS, P, -1) for l in L]),
        "wb_attn": np.concatenate([row_blocks(I["L0_attn_Wo"][l], P) for l in L]),
        "wa_ffn": np.concatenate([column_blocks(I["L0_attn_W1"][l], FF // CHUNKS) for l in L]),
        "wb_ffn": np.concatenate([row_blocks(I["L0_attn_W2"][l], FF // CHUNKS) for l in L]),
        "param_columns": np.concatenate([columns(I["L0_attn_" + n]) for n in
                                         ("ln_gamma", "ln_beta", "gn_gamma", "gn_beta", "b1")], 1),
        "b2": I["L0_attn_b2"],
    }
    gammas = (1.0 - np.exp(np.linspace(np.log(1.0 / 32), np.log(1.0 / 128), HEADS))).astype(np.float32)
    steps = np.arange(SEQ) - SEQ // 2
    decay = np.stack([gammas.astype(np.float64)[:, None] ** -steps, EPS * gammas.astype(np.float64)[:, None] ** (-2 * steps)])
    arrays["consts"] = np.concatenate([np.eye(P), np.triu(np.ones((P, P)))], 1).astype(np.float32)
    arrays["decays"] = (decay.reshape(2, CHUNKS, 2, TT, P).transpose(4, 1, 0, 3, 2)
                        .reshape(P, -1).astype(np.float32))
    arrays["quant_w"] = np.stack([row_blocks(w, QO)[0] for w in I["fside_BxS2xS2_0"]])
    arrays["quant_ctx"] = np.stack([row_blocks(w, DIM)[0] for w in I["ctx_1024"]])
    gate, up = (np.concatenate([column_blocks(I["L0_ffn_" + p + n].T, GW) for p in ("sh_", "r_")]) for n in ("gate", "up"))
    arrays["wa_mlp"] = np.concatenate([gate, up], 2)
    arrays["wb_mlp"] = np.concatenate([row_blocks(I["L0_ffn_" + p + "down"].T, GW) for p in ("sh_", "r_")])
    arrays["router_w"] = column_blocks(I["L0_ffn_router_weight"].T, EXPERTS)[0]

    nc = bacc.Bacc("TRN2", target_bir_lowering=False, num_devices=1)
    arrays = {k + "_dram": np.ascontiguousarray(v) for k, v in arrays.items()}
    args = [nc.dram_tensor(k, v.shape, mybir.dt.from_np(v.dtype), kind="ExternalInput").ap() for k, v in arrays.items()]
    out = nc.dram_tensor("out_dram", (BATCH * SEQ, DIM), mybir.dt.float32, kind="ExternalOutput").ap()
    decoder_kernel(nc, *args, out)
    r = run(nc, [arrays], core_ids=[0])
    return r.results[0]["out_dram"].reshape(BATCH, SEQ, DIM)
```

```python
import concourse.bass as bass
from concourse import mybir
from contextlib import ExitStack

P = 128
BATCH, SEQ, DIM = 4, 512, 512
LAYERS, HEADS, FF = 2, 8, 2048
HEAD = DIM // HEADS
KT = DIM // P
TT = SEQ // P
CHUNKS = 4
FT = FF // CHUNKS // P
INTER = 2048
GW = 256
SHARED = INTER // GW
QO = 512
QI = QO // 2
EXPERTS = 8
EPS = 1e-5
QEPS = 1e-6
QMAX = 127.0
MAGIC = 1.5 * 2 ** 23
MASK_AT = [0, 512, 896, 1152]
SCOLS = 1280
SCORE_TILES = [[0], [2, 3], [1]]
SCORES_AT = [0, 896, 512]
SCORES_N = [512, 384, 384]
SCORES_BANK = [2, 2, 0]

I_DVE = ["stats", "aggr", "vareps", "xn"]
LN_DVE = ["stats", "aggr", "vareps", "xn", "lo0", "lo1", "lo2", "lo3"]
LN_POOL = ["rstd"]
LN_PE = ["t0", "t1", "t2", "t3"]
LN_ACT = ["x0", "h0", "x1", "h1", "x2", "h2", "x3", "h3"]
A_PE = ["q", "k", "v", "s0", "s1", "g", "vt", "s2", "s3", "s4", "s5", "y"]
A_ACT = ["q", "k", "v", "s0", "s1", "g", "vhi", "s2", "s3", "s4", "s5"]
A_DVE = ["q", "k", "m0", "m1", "s0", "s1", "v", "m2", "m3", "s2", "s3", "m4", "m5", "s4", "s5"]
A_POOL = ["vlo"]
N_PE = ["yt"]
N_ACT = ["yT", "ylow", "ysq"]
N_DVE = ["y", "ysum", "ymean", "yc", "ysq", "yvar", "yn"]
N_POOL = ["rstd"]
AT_PE = ["t", "o0", "o1", "o2", "o3"]
AT_ACT = ["t", "hi"]
AT_DVE = ["gate", "lo", "o0", "o1", "o2", "o3"]
F_PE = ["h0", "h1", "h2", "h3"]
F_ACT = ["h0", "h1", "h2", "h3"]
F_DVE = ["lo0", "lo1", "lo2", "lo3"]
F_POOL = ["hi0", "hi1", "hi2", "hi3"]
FT_PE = ["o0", "o1", "o2", "o3"]
FT_DVE = ["o0", "o1", "o2", "o3"]
QK = {1: KT, 2: QI // P}


def quant_steps(*groups):
    steps = []
    for stage, k_tiles in QK.items():
        for g in groups:
            name, kind = g[:-2], g[-2:]
            if kind == "!1":
                steps += [f"{name}_1"] if stage == 1 else []
            elif kind in ("*k", "*t"):
                steps += [f"{name}{j}_{stage}" for j in range(k_tiles if kind == "*k" else TT)]
            else:
                steps += [f"{g}_{stage}"]
    return steps


Q_PE = quant_steps("w*k", "x*k", "xt*t", "xq*k", "ws*k", "wt*t", "row", "wq*k", "o*t")
Q_ACT = quant_steps("xs*k", "xr*t", "ws*k", "wr*t", "row", "silu!1")
Q_DVE = quant_steps("start!1", "x0!1", "stats!1", "aggr!1", "vareps!1", "w*k", "xn!1", "x*k", "max", "winv", "ratio", "s", "rs",
                    "xt*t", "xscale", "xrecip", "xc", "xq*k", "wt*t", "wscale", "wrecip", "wc", "wq*k", "o*t") + ["add_2"]
Q_POOL = ["x0", "rstd", "s_1", "diag_1", "a_1", "s_2", "diag_2", "add_2"]
G_PE = ["g0", "u0", "g1", "u1"]
G_ACT = ["g0", "g1"]
G_DVE = ["p0", "lo0", "p1", "lo1"]
G_POOL = ["hi0", "hi1"]
GT_PE = ["o0", "o1", "o2", "o3"]
GT_DVE = ["o0", "o1", "o2", "o3"]
R_PE = ["l0", "l1", "l2", "l3", "t"]
R_ACT = ["l0", "l1", "l2", "l3", "exp"]
R_DVE = ["weights", "logits", "top", "gap", "den", "rden", "w2", "comb"]


def at(item, steps, name):
    return item * len(steps) + (steps.index(name) + 1)


def decoder_kernel(nc, x, wa_attn, wb_attn, wa_ffn, wb_ffn, params, b2, consts, decay,
                   q_w, q_ctx, wa_mlp, wb_mlp, router, out):
    f32, f32r, bf16 = mybir.dt.float32, mybir.dt.float32r, mybir.dt.bfloat16
    ALU = mybir.AluOpType
    ACT = mybir.ActivationFunctionType
    AX = mybir.AxisListType

    with ExitStack() as ctx:
        def sb(name, shape, dt):
            return ctx.enter_context(nc.sbuf_tensor(name, shape, dt))

        def sem(name):
            return ctx.enter_context(nc.semaphore(name))

        X = sb("resid", [P, BATCH * TT, DIM], f32)
        xT_at = nc.sbuf_base
        XT = sb("xT", [P, 2, BATCH, KT, SEQ], f32r)
        WA = sb("w_in", [P, 2, 2048], f32r)
        WB = sb("w_out", [P, 2, 2048], f32r)
        rawA = sb("raw_in", [P, 2048], f32)
        rawB = sb("raw_out", [P, 2048], f32)
        op_at = nc.sbuf_base
        OP = sb("operands", [P, 8192], f32r)
        WK = sb("work", [P, 3584], f32)
        xn = sb("x_norm", [P, TT, DIM], f32)
        xtmp = sb("x_affine", [P, 2, SEQ], f32)
        ident = sb("ident", [P, P], f32)
        causal = sb("causal", [P, P], f32)
        prm = sb("params", [P, 56], f32)
        gncol = sb("gn_columns", [P, 2], f32)
        b1col = sb("b1_columns", [P, FT], f32)
        b2row = sb("b2_row", [P, DIM], f32)
        dec = sb("decay", [P, CHUNKS, 2, TT, 2], f32)
        half = sb("minus_half", [P, 8], f32)
        one = sb("one", [P, 1], f32)
        stats = sb("stats", [P, TT, 6], f32)
        mv = sb("mean_var", [P, TT, 2], f32)
        ve = sb("var_eps", [P, TT], f32)
        rstd = sb("rstd", [P, TT], f32)
        ysum = sb("y_sum", [P, 8], f32)
        ymean = sb("y_mean", [P, 8], f32)
        yssq = sb("y_sumsq", [P, 8], f32)
        yvar = sb("y_var", [P, 8], f32)
        yrs = sb("y_rstd", [P, 8], f32)
        bank = [ctx.enter_context(nc.psum_tensor(f"bank{i}", [P, 512], f32)) for i in range(8)]

        ones = sb("ones", [P, P], f32)
        identb = sb("ident_bf16", [P, P], bf16)
        Rraw = sb("router_raw", [P, KT, EXPERTS], f32)
        R = sb("router", [P, 2, KT, EXPERTS], f32r)
        lg = b2row[:, 0:128].rearrange("p (t n) -> p t n", n=EXPERTS)
        lgT = xn[0:EXPERTS, :, :]
        top = b2row[:, 128:256].rearrange("p (t n) -> p t n", n=8)
        rt = b2row[:, 256:352].rearrange("p (k t) -> p k t", k=6)
        qs = sb("quant_scales", [P, 2, 12, 4], f32)
        magic = sb("magic", [P, 1], f32)
        scratch = sb("scratch", [P, 10], f32)
        phalf = sb("plus_half", [P, 4], f32)

        areaX = nc.alloc_sbuf_tensor_at("quant_area_x", [P, 16384], f32, offset=xT_at)
        areaO = nc.alloc_sbuf_tensor_at("quant_area_o", [P, 8192], f32, offset=op_at)


        def tiles(ap):
            return ap.rearrange("p (t n) -> p t n", t=TT)

        q_w1 = [tiles(rawA[:, :]), tiles(areaX[:, 2048:4096])]
        q_w2 = [tiles(WK[:, 0:1024]), tiles(areaX[:, 6144:7168])]
        q_rows = [{1: q_w1[u], 2: q_w2[u]} for u in range(2)]
        q_h = [tiles(rawB[:, :]), tiles(areaX[:, 4096:6144])]
        q_x0 = [tiles(areaX[:, 13312:15360]), tiles(areaX[:, 0:2048])]
        q_x = [xn[:, :, :], tiles(areaO[:, 2048:4096])]
        q_sT = [tiles(areaO[:, 0:2048]), tiles(areaX[:, 10240:12288])]
        q_norm = [(stats[:, :, :], mv[:, :, :], ve[:, :], rstd[:, :]),
                  (areaX[:, 15360:15384].rearrange("p (t n) -> p t n", n=6),
                   areaX[:, 15384:15392].rearrange("p (t n) -> p t n", n=2),
                   areaX[:, 15392:15396], areaX[:, 15396:15400])]
        q_row = [WK[:, 1024:1536], areaX[:, 7168:7680]]
        q_diag = [tiles(areaX[:, 12288:12800]), tiles(areaX[:, 12800:13312])]
        q_int = [tiles(xtmp[:, :, :].rearrange("p a n -> p (a n)").bitcast(bf16)),
                 tiles(areaO[:, 6144:7168].bitcast(bf16))]
        q_xT = [tiles(WK[:, 1536:2560].bitcast(bf16)), tiles(areaO[:, 4096:5120].bitcast(bf16))]
        q_wT = [tiles(WK[:, 2560:3584].bitcast(bf16)), tiles(areaO[:, 5120:6144].bitcast(bf16))]
        G = OP[:, 0:4096].rearrange("p (i s f n) -> p i s f n", i=2, s=2, f=2)
        wg = WA[:, :, :].rearrange("p s (r k n) -> p s r k n", r=2, k=KT)
        wd = WB[:, :, 0:1024].rearrange("p s (k n) -> p s k n", k=2)
        qT = OP[:, 0:1024].rearrange("p (s n) -> p s n", s=2)
        kT = OP[:, 1024:2048].rearrange("p (s n) -> p s n", s=2)
        vH = OP[:, 2048:3072].rearrange("p (t r s n) -> p t r s n", t=TT, r=2, s=2)
        S = OP[:, 3072:3072 + 4 * SCOLS].rearrange("p (r s n) -> p r s n", r=2, s=2)
        gated = WB[:, :, 1536:2048]
        wq4 = WA[:, :, :].rearrange("p s (r k n) -> p s r k n", r=4, k=KT)
        H = OP[:, :].rearrange("p (i s f n) -> p i s f n", i=2, s=2, f=FT)
        w1 = WA[:, :, :].rearrange("p s (k n) -> p s k n", k=KT)
        w2 = WB[:, :, :].rearrange("p s (k n) -> p s k n", k=FT)
        vraw = WK[:, 0:512]
        vdec = WK[:, 512:1024]
        yT = WK[:, 512:1536].rearrange("p (r n) -> p r n", r=2)
        sg = WK[:, 1536:2048]
        y = WK[:, 2048:2560]
        ylow = WK[:, 2560:3072].rearrange("p (t r n) -> p t r n", t=TT, r=2)
        ysq = WK[:, 2560:3072]
        gt = WK[:, 3072:3584]
        hid = WK[:, 0:2048].rearrange("p (f n) -> p f n", f=FT)
        lng, lnb = prm[:, 0:4], prm[:, 4:8]
        gn = prm[:, 8:24].rearrange("p (a c) -> p a c", a=2)
        b1 = prm[:, 24:56].rearrange("p (c f) -> p c f", f=FT)

        loaded = sem("consts_loaded")
        halves = sem("minus_half_set")
        rawA_in, rawB_in, b2_in = sem("raw_in_loaded"), sem("raw_out_loaded"), sem("b2_loaded")
        x_in = [sem(f"x_loaded{b}") for b in range(BATCH)]
        out_done = sem("out_stored")
        wa_hi_pool, wa_lo_pool = sem("w_in_hi_pool"), sem("w_in_lo_pool")
        wg_hi, wg_lo = sem("w_gate_up_hi_half"), sem("w_gate_up_lo_half")
        wa_hi, wa_lo = sem("w_in_hi"), sem("w_in_lo")
        wb_hi, wb_lo = sem("w_out_hi"), sem("w_out_lo")
        b2_added = sem("b2_added")
        i_dve, i_pool = sem("first_norm_dve"), sem("first_norm_pool")
        gn_col, b1_col = sem("gn_columns_set"), sem("b1_columns_set")
        ln_dve, ln_pool, ln_pe, ln_act = sem("ln_dve"), sem("ln_pool"), sem("ln_pe"), sem("ln_act")
        a_pe, a_act, a_dve, a_pool = sem("attn_pe"), sem("attn_act"), sem("attn_dve"), sem("attn_pool")
        n_pe, n_act, n_dve, n_pool = (sem("head_norm_pe"), sem("head_norm_act"), sem("head_norm_dve"),
                                      sem("head_norm_pool"))
        at_pe, at_act, at_dve = sem("attn_out_pe"), sem("attn_out_act"), sem("attn_out_dve")
        f_pe, f_act, f_dve, f_pool = sem("ffn_pe"), sem("ffn_act"), sem("ffn_dve"), sem("ffn_pool")
        ft_pe, ft_dve = sem("ffn_out_pe"), sem("ffn_out_dve")
        q1_in, q2_in, x0_in, q_pe, q_act, q_dve, q_pool = (
            [sem(f"quant{u}_{n}") for u in range(2)] for n in
            ("w1_loaded", "w2_loaded", "x_loaded", "pe", "act", "dve", "pool"))
        g_pe, g_act, g_dve, g_pool = sem("mlp_pe"), sem("mlp_act"), sem("mlp_dve"), sem("mlp_pool")
        gt_pe, gt_dve = sem("mlp_out_pe"), sem("mlp_out_dve")
        r_pe, r_act, r_dve, r_hi = sem("router_pe"), sem("router_act"), sem("router_dve"), sem("router_hi")
        block = ctx.enter_context(nc.Block())

        def f(ap):
            return ap.bitcast(f32)

        def split_product(pe, out_, w, v, start, stop):
            (wh, wl), (vh, vl) = w, v
            pe.matmul(out_, wh, vh, start=start, stop=False)
            pe.matmul(out_, wh, vl, start=False, stop=False)
            return pe.matmul(out_, wl, vh, start=False, stop=stop)

        AX_, AW, WI, RA, S_, RS, XM, XS, XR, WM, WS, WR = range(12)

        def w_cols(ap, ft):
            return ap.rearrange("p (k n) -> p k n", n=GW)[:, :, ft * P:(ft + 1) * P]

        def hl(ap, *i):
            return ap[(slice(None), 0, *i)], ap[(slice(None), 1, *i)]

        LOADS = 16 * 5
        GITEM = (SHARED + 1) * BATCH
        ADEPTH = LAYERS * 2 * CHUNKS
        LN_LAST = LAYERS * 2 * BATCH + 1
        LAST = CHUNKS - 1
        NITEM = CHUNKS * BATCH

        def first_norm(batches):
            n, at_ = len(batches) * TT, 2560 + batches[0] * 64
            return (WK[:, at_:at_ + 6 * n].rearrange("p (t n) -> p t n", n=6),
                    WK[:, at_ + 6 * n:at_ + 8 * n].rearrange("p (t n) -> p t n", n=2),
                    WK[:, at_ + 8 * n:at_ + 9 * n], WK[:, at_ + 9 * n:at_ + 10 * n])

        LN_BANKS, LN_BANKS_ATTN, LN_BANKS_FIRST = (4, 5, 4, 5), (6, 7, 6, 7), (6, 7, 4, 5)
        LN_BANKS_FFN = (4, 5, 0, 1)
        OUT_BANKS, OUT_BANKS_ATTN, OUT_BANKS_FFN = (6, 7, 4, 5), (4, 5, 4, 5), (6, 7, 6, 7)

        def norm_beside(b, ln0, ln_next):
            if ln0 is not None and b + 1 < BATCH:
                return ln0 + b + 1, b + 1
            if ln_next is not None and b == BATCH - 1:
                return ln_next, 0
            return None

        @block.sync
        def _(sp):
            sp.dma_start(prm[:, :], params).then_inc(loaded, 16)
            sp.dma_start(ident[:, :], consts[:, 0:P]).then_inc(loaded, 16)
            sp.dma_start(causal[:, :], consts[:, P:2 * P]).then_inc(loaded, 16)
            sp.dma_start(dec[:, :, :, :, :].rearrange("p a b c d -> p (a b c d)"), decay).then_inc(loaded, 16)
            sp.dma_start(Rraw[:, :, :].rearrange("p k n -> p (k n)"), router).then_inc(loaded, 16)
            sp.dma_start(X[:, 0:TT, :], x[0:SEQ, :].rearrange("(t p) n -> p t n", p=P)).then_inc(x_in[0], 16)

            def load_w(w_a, cols_a, w_b, cols_b, j, chunk):
                sp.wait_ge(wa_lo, chunk + 1)
                sp.dma_start(rawA[:, 0:cols_a], w_a[bass.ds(j, 1), :, :].rearrange("o p n -> p (o n)")).then_inc(rawA_in, 16)
                sp.wait_ge(wb_lo, chunk + 1)
                sp.dma_start(rawB[:, 0:cols_b], w_b[bass.ds(j, 1), :, :].rearrange("o p n -> p (o n)")).then_inc(rawB_in, 16)

            with sp.Fori(0, LAYERS) as layer:
                sp.wait_ge(b2_added, layer * BATCH + 1)
                sp.dma_start(b2row[:, :], b2[bass.ds(layer, 1), :].rearrange("o n -> (o n)").partition_broadcast(P)).then_inc(b2_in, 16)
                with sp.Fori(0, CHUNKS) as c:
                    load_w(wa_attn, 2048, wb_attn, 512, layer * CHUNKS + c, layer * 2 * CHUNKS + c)
                with sp.Fori(0, CHUNKS) as c:
                    load_w(wa_ffn, 2048, wb_ffn, 2048, layer * CHUNKS + c, layer * 2 * CHUNKS + CHUNKS + c)
            sp.wait_ge(wa_lo, ADEPTH + 1)
            sp.dma_start(rawA[:, :], wa_mlp[0]).then_inc(rawA_in, 16)
            def load_x0(b, u):
                sp.dma_start(q_x0[u], x[b * SEQ:(b + 1) * SEQ, :].rearrange("(t p) n -> p t n", p=P)).then_inc(x0_in[u], 16)

            def load_quant(b, u):
                sp.dma_start(q_w1[u], q_w[b].rearrange("p (t n) -> p t n", t=TT)).then_inc(q1_in[u], 16)
                sp.dma_start(q_w2[u], q_ctx[b].rearrange("p (t n) -> p t n", t=TT)).then_inc(q2_in[u], 16)

            sp.wait_ge(wa_lo, ADEPTH + 2)
            sp.wait_ge(wb_lo, ADEPTH + 1)
            sp.wait_ge(f_pe, at(LAYERS * NITEM - 1, F_PE, "h3"))
            sp.wait_ge(f_dve, at(LAYERS * NITEM - 1, F_DVE, "lo3"))
            sp.wait_ge(ln_dve, at(LN_LAST - 1, LN_DVE, "lo3"))
            for u in range(2):
                load_x0(u, u)
                load_quant(u, u)
            for u in range(2):
                sp.wait_ge(q_dve[u], at(0, Q_DVE, "x0_1"))
                sp.wait_ge(q_pool[u], at(0, Q_POOL, "x0"))
                load_x0(2 + u, u)
            for u in range(2):
                sp.wait_ge(q_dve[u], at(0, Q_DVE, "o3_2"))
                load_quant(2 + u, u)
            for u in range(2):
                sp.wait_ge(q_pool[u], 2 * len(Q_POOL))
                sp.wait_ge(q_dve[u], 2 * len(Q_DVE))
            sp.dma_start(rawB[:, 0:1024], wb_mlp[0]).then_inc(rawB_in, 16)
            with sp.Fori(1, SHARED + 1) as j:
                load_w(wa_mlp, 2048, wb_mlp, 1024, j, ADEPTH + j)
            for b in range(BATCH):
                sp.wait_ge(gt_dve, at(SHARED * BATCH + b, GT_DVE, "o3"))
                sp.dma_start(out[b * SEQ:(b + 1) * SEQ, :].rearrange("(t p) n -> p t n", p=P),
                             X[:, b * TT:(b + 1) * TT, :]).then_inc(out_done, 16)
            sp.wait_ge(out_done, 16 * BATCH)

        @block.tensor
        def _(pe):
            pe.wait_ge(loaded, LOADS)
            pe.wait_ge(halves, 6)

            def ln_transpose(n, banks, tiles=range(KT)):
                pe.wait_ge(ln_dve, at(n, LN_DVE, "xn"))
                for k in tiles:
                    if k >= 2 and banks[k] == banks[k - 2]:
                        pe.wait_ge(ln_act, at(n, LN_ACT, f"h{k - 2}"))
                    for t in range(TT):
                        mm = pe.transpose(bank[banks[k]][:, t * P:(t + 1) * P], xn[:, t, k * P:(k + 1) * P], ident[:, :])
                    mm.then_inc(ln_pe, 1)

            def xt_ready(n):
                pe.wait_ge(ln_act, at(n, LN_ACT, "h3"))
                pe.wait_ge(ln_dve, at(n, LN_DVE, "lo3"))

            def attn_role(b, role, n, between=None):
                for k in range(KT):
                    if between and k == KT // 2:
                        between()
                    mm = split_product(pe, bank[n][:, :], hl(wq4, "qkvg".index(role), k), hl(XT, b, k), k == 0, k == KT - 1)
                mm.then_inc(a_pe, 1)

            def attn_scores(i, pair):
                for r in range(2):
                    if pair == 1:
                        pe.wait_ge(a_dve, at(i, A_DVE, f"s{r}"))
                    rows = slice(64 * r, 64 * r + 64)
                    for m in SCORE_TILES[pair]:
                        o = bank[SCORES_BANK[pair] + r][:, MASK_AT[m] - SCORES_AT[pair]:MASK_AT[m] - SCORES_AT[pair] + SEQ - m * P]
                        mm = split_product(pe, o,
                                           (kT[rows, 0, m * P:(m + 1) * P], kT[rows, 1, m * P:(m + 1) * P]),
                                           (qT[rows, 0, m * P:SEQ], qT[rows, 1, m * P:SEQ]), True, True)
                    mm.then_inc(a_pe, 1)

            def attn_values(i):
                pe.wait_ge(a_act, at(i, A_ACT, "vhi"))
                pe.wait_ge(a_pool, at(i, A_POOL, "vlo"))
                pe.wait_ge(a_dve, at(i, A_DVE, "s3"))
                for m in (0, 2, 3, 1):
                    if m == 1:
                        pe.wait_ge(a_dve, at(i, A_DVE, "s5"))
                    for r in range(2):
                        o = bank[2 + r][:, m * P:SEQ]
                        queries = slice(MASK_AT[m], MASK_AT[m] + SEQ - m * P)
                        if m:
                            pe.matmul(o[0:HEAD, :], vH[:, m, r, 0, :], S[:, r, 1, queries], start=False, stop=False)
                        mm = pe.matmul(o, vH[:, m, r, :, :].rearrange("p s n -> p (s n)"), S[:, r, 0, queries],
                                       start=m == 0, stop=m == 1)
                        if not m:
                            pe.matmul(o[0:HEAD, :], vH[:, m, r, 0, :], S[:, r, 1, queries], start=False, stop=False)
                mm.then_inc(a_pe, 1)

            def attn_turn(i):
                pe.wait_ge(n_act, at(i, N_ACT, "yT"))
                for r in range(2):
                    for t in range(TT):
                        mm = pe.transpose(bank[2 + r][:, t * P:(t + 1) * P], yT[:, r, t * P:(t + 1) * P], ident[:, :])
                mm.then_inc(n_pe, 1)

            def attn_out_transpose(i, first=False):
                if not first:
                    pe.wait_ge(at_dve, at(i - 1, AT_DVE, "o3"))
                pe.wait_ge(n_dve, at(i, N_DVE, "yn"))
                for t in range(TT):
                    mm = pe.transpose(bank[4][:, t * P:(t + 1) * P], y[:, t * P:(t + 1) * P], ident[:, :])
                mm.then_inc(at_pe, 1)

            def attn_out(i, tiles, banks):
                pe.wait_ge(at_act, at(i, AT_ACT, "hi"))
                pe.wait_ge(at_dve, at(i, AT_DVE, "lo"))
                for t in tiles:
                    if t >= 2 and banks[t] == banks[t - 2]:
                        pe.wait_ge(at_dve, at(i, AT_DVE, f"o{t - 2}"))
                    split_product(pe, bank[banks[t]][:, :],
                                  (gated[:, 0, t * P:(t + 1) * P], gated[:, 1, t * P:(t + 1) * P]),
                                  (WB[:, 0, 0:DIM], WB[:, 1, 0:DIM]), True, True).then_inc(at_pe, 1)

            def attn_chunk(base, gc, ln0=None, ln_next=None):
                chunk0 = ln0 is not None
                pe.wait_ge(wa_hi, gc + 1)
                pe.wait_ge(wa_lo, gc + 2)
                for b in range(BATCH):
                    i = base + b
                    first = chunk0 and b == 0
                    norm = norm_beside(b, ln0, ln_next)
                    out_banks = OUT_BANKS_ATTN if norm else OUT_BANKS
                    if chunk0:
                        xt_ready(ln0 + b)
                    attn_role(b, "q", 0, None if first else lambda: attn_turn(i - 1))
                    attn_role(b, "k", 1)
                    pe.wait_ge(a_dve, at(i, A_DVE, "q"))
                    attn_role(b, "v", 0)
                    pe.wait_ge(a_dve, at(i, A_DVE, "k"))
                    if not first:
                        pe.wait_ge(n_dve, at(i - 1, N_DVE, "y"))
                    attn_scores(i, 0)
                    if not first:
                        attn_out_transpose(i - 1, chunk0 and b == 1)
                    attn_role(b, "g", 1)
                    pe.wait_ge(a_act, at(i, A_ACT, "v"))
                    for t in range(TT):
                        mm = pe.transpose(bank[5][:, t * P:(t + 1) * P], vraw[:, t * P:(t + 1) * P], ident[:, :])
                    mm.then_inc(a_pe, 1)
                    if norm:
                        ln_transpose(norm[0], LN_BANKS_ATTN, range(0, 2))
                    attn_scores(i, 1)
                    pe.wait_ge(a_act, at(i, A_ACT, "g"))
                    attn_scores(i, 2)
                    if b == 1:
                        pe.wait_ge(wb_hi, gc + 1)
                        pe.wait_ge(wb_lo, gc + 2)
                    pe.wait_ge(a_dve, at(i, A_DVE, "v"))
                    if not first:
                        pe.wait_ge(at_act, at(i - 1, AT_ACT, "t"))
                        attn_out(i - 1, range(TT), out_banks)
                    if norm:
                        ln_transpose(norm[0], LN_BANKS_ATTN, range(2, KT))
                    attn_values(i)

            def ffn_head(b, i, chunk0, attn_last):
                for ft in range(FT):
                    if not (chunk0 and b == 0):
                        pe.wait_ge(f_act, at(i - 1, F_ACT, f"h{ft}"))
                    if attn_last is not None and ft == 2:
                        pe.wait_ge(n_dve, at(attn_last, N_DVE, "y"))
                    if attn_last is not None and ft == FT - 1:
                        attn_out_transpose(attn_last)
                    for k in range(KT):
                        if attn_last is not None and ft == 0 and k == KT // 2:
                            attn_turn(attn_last)
                        mm = split_product(pe, bank[ft][:, :], hl(w1, k, slice(ft * P, (ft + 1) * P)), hl(XT, b, k),
                                           k == 0, k == KT - 1)
                    mm.then_inc(f_pe, 1)

            def ffn_out(b, i, first, tiles=range(TT)):
                pe.wait_ge(f_dve, at(i, F_DVE, "lo3"))
                pe.wait_ge(f_pool, at(i, F_POOL, "hi3"))
                for t in tiles:
                    if t >= 2:
                        pe.wait_ge(ft_dve, at(i, FT_DVE, f"o{t - 2}"))
                    elif not first:
                        pe.wait_ge(ft_dve, at(i - 1, FT_DVE, f"o{t + 2}"))
                    for k in range(FT):
                        mm = split_product(pe, bank[6 + t % 2][:, :], hl(H[:, b % 2], k, slice(t * P, (t + 1) * P)),
                                           hl(w2, k), k == 0, k == FT - 1)
                    mm.then_inc(ft_pe, 1)

            def ffn_chunk(base, gc, ln0=None, ln_next=None, attn_last=None):
                chunk0 = ln0 is not None
                pe.wait_ge(wa_hi, gc + 1)
                pe.wait_ge(wa_lo, gc + 2)
                for b in range(BATCH):
                    i = base + b
                    if chunk0:
                        xt_ready(ln0 + b)
                    ffn_head(b, i, chunk0, attn_last if b == 0 else None)
                    norm = norm_beside(b, ln0, ln_next)
                    if chunk0 and b == 0:
                        pe.wait_ge(at_act, at(attn_last, AT_ACT, "t"))
                        pe.wait_ge(f_act, at(i, F_ACT, "h1"))
                        ln_transpose(norm[0], LN_BANKS_FFN)
                        attn_out(attn_last, range(TT), OUT_BANKS_FFN)
                    else:
                        if b == 1:
                            pe.wait_ge(wb_hi, gc + 1)
                            pe.wait_ge(wb_lo, gc + 2)
                        if norm:
                            ln_transpose(norm[0], LN_BANKS, range(0, 2))
                        ffn_out((b - 1) % BATCH, i - 1, chunk0 and b == 1, (0, 1))
                        if norm:
                            ln_transpose(norm[0], LN_BANKS, range(2, KT))
                        ffn_out((b - 1) % BATCH, i - 1, False, (2, 3))

            ln_transpose(0, LN_BANKS_FIRST)
            with pe.Fori(0, LAYERS) as layer:
                base, gc, ln0 = layer * NITEM, layer * 2 * CHUNKS, layer * 2 * BATCH
                attn_chunk(base, gc, ln0=ln0)
                with pe.Fori(1, LAST) as c:
                    attn_chunk(base + c * BATCH, gc + c)
                attn_chunk(base + LAST * BATCH, gc + LAST, ln_next=ln0 + BATCH)
                ffn_chunk(base, gc + CHUNKS, ln0=ln0 + BATCH, attn_last=base + NITEM - 1)
                with pe.Fori(1, LAST) as c:
                    ffn_chunk(base + c * BATCH, gc + CHUNKS + c)
                ffn_chunk(base + LAST * BATCH, gc + CHUNKS + LAST, ln_next=ln0 + 2 * BATCH)
                ffn_out(BATCH - 1, base + NITEM - 1, False)

            def quant_transpose(u, s, src, free):
                for k in range(QK[s]):
                    free(k)
                    for t in range(TT):
                        mm = pe.transpose(bank[4 * u + k][:, t * P:(t + 1) * P], src[:, t, k * P:(k + 1) * P], ident[:, :])
                    mm.then_inc(q_pe[u], 1)

            def quant_back(u, s):
                for t in range(TT):
                    for k in range(QK[s]):
                        mm = pe.transpose(bank[4 * u + t][:, k * P:(k + 1) * P], q_sT[u][:, k, t * P:(t + 1) * P], ident[:, :])
                    mm.then_inc(q_pe[u], 1)

            def quant_integers(u, s, k):
                for t in range(TT):
                    mm = pe.transpose(bank[4 * u + k].bitcast(bf16)[:, t * P:(t + 1) * P],
                                      q_int[u][:, t, k * P:(k + 1) * P], identb[:, :])
                mm.then_inc(q_pe[u], 1)

            def quant_pair(p, s):
                K = QK[s]

                def dve_done(u, name):
                    pe.wait_ge(q_dve[u], at(p, Q_DVE, name))

                for u in range(2):
                    pe.wait_ge([q1_in, q2_in][s - 1][u], 16 * (p + 1))
                    quant_transpose(u, s, q_rows[u][s],
                                    lambda k: dve_done(u, "start_1") if s == 1 else dve_done(u, f"o{k}_1"))
                for u in range(2):
                    if s == 1:
                        dve_done(u, "xn_1")
                    else:
                        pe.wait_ge(q_pool[u], at(p, Q_POOL, "a_1"))
                    quant_transpose(u, s, q_x[u], lambda k: dve_done(u, f"w{k}_{s}"))
                for u in range(2):
                    pe.wait_ge(q_act[u], at(p, Q_ACT, f"xs{K - 1}_{s}"))
                    quant_back(u, s)
                for u in range(2):
                    dve_done(u, f"xc_{s}")
                    for k in range(K):
                        quant_integers(u, s, k)
                for u in range(2):
                    quant_transpose(u, s, q_rows[u][s], lambda k: dve_done(u, f"xq{k}_{s}"))
                for u in range(2):
                    pe.wait_ge(q_act[u], at(p, Q_ACT, f"ws{K - 1}_{s}"))
                    quant_back(u, s)
                for u in range(2):
                    pe.wait_ge(q_pool[u], at(p, Q_POOL, f"diag_{s}"))
                    pe.wait_ge(q_act[u], at(p, Q_ACT, f"wr3_{s}"))
                    for t in range(TT):
                        mm = pe.matmul(bank[4 * u + 3][:, t * P:(t + 1) * P], ones[:, :], q_diag[u][:, t, :], start=True, stop=True)
                    mm.then_inc(q_pe[u], 1)
                    dve_done(u, f"wc_{s}")
                    for k in range(K):
                        if k == 3:
                            pe.wait_ge(q_act[u], at(p, Q_ACT, f"row_{s}"))
                        quant_integers(u, s, k)
                for u in range(2):
                    dve_done(u, f"wq{K - 1}_{s}")
                    pe.wait_ge(q_act[u], at(p, Q_ACT, f"row_{s}"))
                    for t in range(TT):
                        for k in range(K):
                            mm = pe.matmul(bank[4 * u + t][:, :], q_xT[u][:, k, t * P:(t + 1) * P], q_wT[u][:, k, :],
                                           start=k == 0, stop=k == K - 1)
                        mm.then_inc(q_pe[u], 1)

            with pe.Fori(0, BATCH // 2) as p:
                quant_pair(p, 1)
                quant_pair(p, 2)

            def mlp_head(b, i, chunk0, first):
                for n, (role, ft) in enumerate([(0, 0), (1, 0), (0, 1), (1, 1)]):
                    if not first:
                        sem_, steps, name = (g_act, G_ACT, f"g{ft}") if role == 0 else (g_dve, G_DVE, f"p{ft}")
                        pe.wait_ge(sem_, at(i - 1, steps, name))
                    for k in range(KT):
                        mm = split_product(pe, bank[n][:, :], hl(wg, role, k, slice(ft * P, (ft + 1) * P)), hl(XT, b, k),
                                           k == 0, k == KT - 1)
                    mm.then_inc(g_pe, 1)

            def mlp_out(b, i, first, tiles=range(TT)):
                pe.wait_ge(g_dve, at(i, G_DVE, "lo1"))
                for t in tiles:
                    if t >= 2:
                        pe.wait_ge(gt_dve, at(i, GT_DVE, f"o{t - 2}"))
                    elif not first:
                        pe.wait_ge(gt_dve, at(i - 1, GT_DVE, f"o{t + 2}"))
                    for k in range(2):
                        mm = split_product(pe, bank[6 + t % 2][:, :], hl(G[:, b % 2], k, slice(t * P, (t + 1) * P)),
                                           hl(wd, k), k == 0, k == 1)
                    mm.then_inc(gt_pe, 1)

            def mlp_chunk(base, gc, chunk0):
                pe.wait_ge(wa_hi, gc + 1)
                pe.wait_ge(wa_lo, gc + 2)
                for b in range(BATCH):
                    i = base + b
                    first = chunk0 and b == 0
                    if chunk0:
                        xt_ready(LN_LAST + b)
                    mlp_head(b, i, chunk0, first)
                    norm = chunk0 and b + 1 < BATCH
                    if norm:
                        ln_transpose(LN_LAST + b + 1, LN_BANKS, range(0, 2))
                    if b == 1:
                        pe.wait_ge(wb_hi, gc + 1)
                        pe.wait_ge(wb_lo, gc + 2)
                    if not first:
                        mlp_out((b - 1) % BATCH, i - 1, chunk0 and b == 1, (0, 1))
                    if norm:
                        ln_transpose(LN_LAST + b + 1, LN_BANKS, range(2, KT))
                    if not first:
                        mlp_out((b - 1) % BATCH, i - 1, False, (2, 3))

            pe.wait_ge(q_dve[1], BATCH // 2 * len(Q_DVE))
            ln_transpose(LN_LAST, LN_BANKS_FIRST)
            mlp_chunk(0, ADEPTH, True)
            pe.wait_ge(r_hi, 1)
            pe.wait_ge(r_dve, at(0, R_DVE, "weights"))
            for b in range(BATCH):
                if b >= 2:
                    pe.wait_ge(r_act, at(0, R_ACT, f"l{b - 2}"))
                for k in range(KT):
                    mm = split_product(pe, bank[4 + b % 2][0:EXPERTS, :], hl(R, k), hl(XT, b, k), k == 0, k == KT - 1)
                mm.then_inc(r_pe, 1)
            for b in range(BATCH):
                pe.wait_ge(r_act, at(0, R_ACT, f"l{b}"))
                if b == 0:
                    pe.wait_ge(r_act, at(0, R_ACT, "l2"))
                for t in range(TT):
                    bt = b * TT + t
                    mm = pe.transpose(bank[4][:, bt * EXPERTS:(bt + 1) * EXPERTS], lgT[:, b, t * P:(t + 1) * P],
                                      ident[0:EXPERTS, 0:EXPERTS])
            mm.then_inc(r_pe, 1)
            with pe.Fori(1, SHARED) as j:
                mlp_chunk(j * BATCH, ADEPTH + j, False)
            mlp_chunk(SHARED * BATCH, ADEPTH + SHARED, False)
            mlp_out(BATCH - 1, GITEM - 1, False)

        @block.scalar
        def _(act):
            act.wait_ge(loaded, LOADS)
            act.wait_ge(halves, 6)

            def split_in(gc, last_use, part=slice(0, 2048)):
                act.wait_ge(rawA_in, 16 * (gc + 1))
                last_use()
                act.activation(WA[:, 0, part], rawA[:, part], ACT.Copy).then_inc(wa_hi, 1)

            def split_out(gc, cols, last_use):
                act.wait_ge(rawB_in, 16 * (gc + 1))
                last_use()
                act.activation(WB[:, 0, 0:cols], rawB[:, 0:cols], ACT.Copy).then_inc(wb_hi, 1)

            def ln_affine(norm, banks, tiles=range(KT)):
                n, b = norm
                for k in tiles:
                    act.wait_ge(ln_pe, at(n, LN_PE, f"t{k}"))
                    if k >= 2:
                        act.wait_ge(ln_dve, at(n, LN_DVE, f"lo{k - 2}"))
                    for dst in (xtmp[:, k % 2, :], XT[:, 0, b, k, :]):
                        act.activation(dst, bank[banks[k]][:, :], ACT.Identity,
                                       scale=lng[:, k:k + 1], bias=lnb[:, k:k + 1]).then_inc(ln_act, 1)

            def attn_chunk(base, gc, lc, ln0=None, ln_next=None):
                chunk0 = ln0 is not None
                for b in range(BATCH):
                    i = base + b
                    first = chunk0 and b == 0
                    if not first:
                        attn_whole(i - 1)
                        attn_low_sums(i - 1)
                    act.wait_ge(a_pe, at(i, A_PE, "q"))
                    act.activation(qT[:, 0, :], bank[0][:, :], ACT.Copy).then_inc(a_act, 1)
                    if not first:
                        attn_squares(i - 1)
                    if b == 1:
                        attn_columns(lc)
                    act.wait_ge(a_pe, at(i, A_PE, "k"))
                    act.activation(kT[:, 0, :], bank[1][:, :], ACT.Copy).then_inc(a_act, 1)
                    act.wait_ge(a_pe, at(i, A_PE, "v"))
                    act.activation(vraw, bank[0][:, :], ACT.Copy).then_inc(a_act, 1)
                    attn_scores_hi(i, 0, 0)
                    if not first:
                        attn_tail_t(i - 1, lc - 1 if b == 0 else lc)
                    attn_scores_hi(i, 0, 1)
                    if not first:
                        attn_tail_hi(i - 1)
                    act.wait_ge(a_pe, at(i, A_PE, "g"))
                    act.activation(sg, bank[1][:, :], ACT.Silu).then_inc(a_act, 1)
                    act.wait_ge(a_dve, at(i, A_DVE, "v"))
                    act.activation(vH.rearrange("p t r s n -> p (t r) s n")[:, :, 0, :],
                                   vdec.rearrange("p (g n) -> p g n", n=HEAD), ACT.Copy).then_inc(a_act, 1)
                    for pair in (1, 2):
                        attn_scores_hi(i, pair, 0)
                        attn_scores_hi(i, pair, 1)
                    norm = norm_beside(b, ln0, ln_next)
                    if norm:
                        ln_affine(norm, LN_BANKS_ATTN)
                    if b == 0:
                        split_out(gc, DIM, lambda: None if chunk0 else act.wait_ge(at_pe, at(i - 1, AT_PE, "o3")))
                    if b == BATCH - 1:
                        split_in(gc + 1, lambda: act.wait_ge(a_pe, at(i, A_PE, "g")), slice(1024, 2048))

            def attn_whole(i):
                act.wait_ge(a_pe, at(i, A_PE, "y"))
                for r in range(2):
                    ins = act.activation(yT[:, r, :], bank[2 + r][:, :], ACT.Copy)
                ins.then_inc(n_act, 1)

            def attn_low_sums(i):
                act.wait_ge(n_pe, at(i, N_PE, "yt"))
                for r in range(2):
                    ins = act.activation(ylow[:, :, r, :], bank[2 + r][:, :].rearrange("p (t s n) -> p t s n", t=TT, s=2)[:, :, 1, :],
                                         ACT.Copy)
                ins.then_inc(n_act, 1)

            def attn_squares(i):
                act.wait_ge(n_dve, at(i, N_DVE, "yc"))
                act.activation(ysq, y, ACT.Square).then_inc(n_act, 1)

            def attn_scores_hi(i, pair, r):
                act.wait_ge(a_dve, at(i, A_DVE, f"m{2 * pair + r}"))
                col, n = SCORES_AT[pair], SCORES_N[pair]
                act.activation(S[:, r, 0, col:col + n], bank[SCORES_BANK[pair] + r][:, 0:n], ACT.Copy).then_inc(a_act, 1)

            def attn_columns(lc):
                act.activation(gncol[:, :], gn[:, :, bass.ds(lc, 1)].rearrange("p a o -> p (a o)"), ACT.Copy).then_inc(gn_col, 1)

            def attn_tail_t(i, lc):
                act.wait_ge(gn_col, lc + 1)
                act.wait_ge(at_pe, at(i, AT_PE, "t"))
                act.activation(gt, bank[4][:, :], ACT.Identity, scale=gncol[:, 0:1],
                               bias=gncol[:, 1:2]).then_inc(at_act, 1)

            def attn_tail_hi(i):
                act.wait_ge(at_dve, at(i, AT_DVE, "gate"))
                act.activation(gated[:, 0, :], gt, ACT.Copy).then_inc(at_act, 1)

            def ffn_chunk(base, gc, lc, ln0=None, ln_next=None, attn_last=None):
                chunk0 = ln0 is not None
                if not chunk0:
                    act.wait_ge(f_act, at(base - 1, F_ACT, "h3"))
                act.activation(b1col[:, :], b1[:, bass.ds(lc, 1), :].rearrange("p o f -> p (o f)"), ACT.Copy).then_inc(b1_col, 1)
                act.wait_ge(b1_col, lc + 1)
                if attn_last is not None:
                    attn_whole(attn_last)
                    attn_low_sums(attn_last)
                for b in range(BATCH):
                    i = base + b
                    first = chunk0 and b == 0
                    for ft in range(FT):
                        if first and ft == 1:
                            attn_squares(attn_last)
                        if first and ft == FT - 1:
                            attn_tail_t(attn_last, lc + LAST)
                            attn_tail_hi(attn_last)
                        act.wait_ge(f_pe, at(i, F_PE, f"h{ft}"))
                        if not first:
                            act.wait_ge(f_dve, at(i - 1, F_DVE, f"lo{ft}"))
                            act.wait_ge(f_pool, at(i - 1, F_POOL, f"hi{ft}"))
                        act.activation(hid[:, ft, :], bank[ft][:, :], ACT.Gelu_apprx_tanh,
                                       bias=b1col[:, ft:ft + 1]).then_inc(f_act, 1)
                    norm = norm_beside(b, ln0, ln_next)
                    ln_banks = LN_BANKS_FFN if first else LN_BANKS
                    if norm:
                        ln_affine(norm, ln_banks, range(0, 2))
                    if b == BATCH - 1:
                        split_in(gc + 1, lambda: act.wait_ge(f_pe, at(i, F_PE, "h3")))
                    if norm:
                        ln_affine(norm, ln_banks, range(2, KT))
                    if b == 0:
                        split_out(gc, 2048, lambda: act.wait_ge(at_pe, at(attn_last, AT_PE, "o3")) if chunk0 else
                                  act.wait_ge(ft_pe, at(i - 1, FT_PE, "o3")))

            split_in(0, lambda: None)
            for b in range(1, BATCH):
                act.dma_start(X[:, b * TT:(b + 1) * TT, :],
                              x[b * SEQ:(b + 1) * SEQ, :].rearrange("(t p) n -> p t n", p=P)).then_inc(x_in[b], 16)
            ln_affine((0, 0), LN_BANKS_FIRST)
            with act.Fori(0, LAYERS) as layer:
                base, gc, ln0 = layer * NITEM, layer * 2 * CHUNKS, layer * 2 * BATCH
                attn_chunk(base, gc, layer * CHUNKS, ln0=ln0)
                with act.Fori(1, LAST) as c:
                    attn_chunk(base + c * BATCH, gc + c, layer * CHUNKS + c)
                attn_chunk(base + LAST * BATCH, gc + LAST, layer * CHUNKS + LAST, ln_next=ln0 + BATCH)
                ffn_chunk(base, gc + CHUNKS, layer * CHUNKS, ln0=ln0 + BATCH, attn_last=base + NITEM - 1)
                with act.Fori(1, LAST) as c:
                    ffn_chunk(base + c * BATCH, gc + CHUNKS + c, layer * CHUNKS + c)
                ffn_chunk(base + LAST * BATCH, gc + CHUNKS + LAST, layer * CHUNKS + LAST, ln_next=ln0 + 2 * BATCH)

            def quant_round(p, u, s, side, scale, rows):
                D = QK[s] * P
                act.wait_ge(q_dve[u], at(p, Q_DVE, f"{side}recip_{s}"))
                for t in range(TT):
                    act.activation(rows[:, t, 0:D], bank[4 * u + t][:, 0:D], ACT.Identity,
                                   scale=qs[:, u, scale, t:t + 1], bias=magic[:, 0:1]).then_inc(q_act[u], 1)

            def quant_pair(p, s):
                K = QK[s]
                for u in range(2):
                    act.wait_ge(q_dve[u], at(p, Q_DVE, f"rs_{s}"))
                    for k in range(K):
                        act.activation(q_sT[u][:, k, :], bank[4 * u + k][:, :], ACT.Copy,
                                       scale=qs[:, u, RS, k:k + 1]).then_inc(q_act[u], 1)
                for u in range(2):
                    quant_round(p, u, s, "x", XR, q_x[u])
                for u in range(2):
                    for k in range(K):
                        act.wait_ge(q_pe[u], at(p, Q_PE, f"ws{k}_{s}"))
                        act.activation(q_sT[u][:, k, :], bank[4 * u + k][:, :], ACT.Copy,
                                       scale=qs[:, u, S_, k:k + 1]).then_inc(q_act[u], 1)
                for u in range(2):
                    quant_round(p, u, s, "w", WR, q_rows[u][s])
                for u in range(2):
                    act.wait_ge(q_pe[u], at(p, Q_PE, f"row_{s}"))
                    act.activation(q_row[u], bank[4 * u + 3][:, :], ACT.Copy).then_inc(q_act[u], 1)
                if s == 1:
                    for u in range(2):
                        act.wait_ge(q_dve[u], at(p, Q_DVE, "o3_1"))
                        act.activation(q_x[u][:, :, 0:QI], q_h[u][:, :, 0:QI], ACT.Silu).then_inc(q_act[u], 1)

            with act.Fori(0, BATCH // 2) as p:
                quant_pair(p, 1)
                quant_pair(p, 2)

            def ln_copy(b, banks=LN_BANKS):
                n = LN_LAST + b
                for k in range(KT):
                    act.wait_ge(ln_pe, at(n, LN_PE, f"t{k}"))
                    if k >= 2:
                        act.wait_ge(ln_dve, at(n, LN_DVE, f"lo{k - 2}"))
                    for dst in (xtmp[:, k % 2, :], XT[:, 0, b, k, :]):
                        act.activation(dst, bank[banks[k]][:, :], ACT.Copy).then_inc(ln_act, 1)

            def mlp_chunk(base, gc, chunk0, last=False):
                for b in range(BATCH):
                    i = base + b
                    for ft in range(2):
                        act.wait_ge(g_pe, at(i, G_PE, f"g{ft}"))
                        if not (chunk0 and b == 0):
                            act.wait_ge(g_dve, at(i - 1, G_DVE, f"lo{ft}"))
                            act.wait_ge(g_pool, at(i - 1, G_POOL, f"hi{ft}"))
                        act.activation(hid[:, ft, :], bank[2 * ft][:, :], ACT.Silu).then_inc(g_act, 1)
                        if b == BATCH - 1 and not last:
                            act.wait_ge(rawA_in, 16 * (gc + 2))
                            act.wait_ge(g_pe, at(i, G_PE, f"u{ft}"))
                            act.activation(w_cols(WA[:, 0, :], ft), w_cols(rawA[:, :], ft), ACT.Copy).then_inc((wg_hi, wa_hi)[ft], 1)
                    if chunk0 and b + 1 < BATCH:
                        ln_copy(b + 1)
                    if b == 0:
                        split_out(gc, 1024, lambda: None if chunk0 else act.wait_ge(gt_pe, at(i - 1, GT_PE, "o3")))

            act.activation(R[:, 0, :, :], Rraw[:, :, :], ACT.Copy).then_inc(r_hi, 1)
            for u in range(2):
                act.wait_ge(q_pool[u], BATCH // 2 * len(Q_POOL))
                act.wait_ge(q_dve[u], BATCH // 2 * len(Q_DVE))
            ln_copy(0, LN_BANKS_FIRST)
            mlp_chunk(0, ADEPTH, True)
            for b in range(BATCH):
                act.wait_ge(r_pe, at(0, R_PE, f"l{b}"))
                act.activation(lgT[:, b, :], bank[4 + b % 2][0:EXPERTS, :], ACT.Copy).then_inc(r_act, 1)
            act.wait_ge(r_dve, at(0, R_DVE, "gap"))
            act.activation(rt[:, 1, :], rt[:, 0, :], ACT.Exp).then_inc(r_act, 1)
            with act.Fori(1, SHARED) as j:
                mlp_chunk(j * BATCH, ADEPTH + j, False)
            mlp_chunk(SHARED * BATCH, ADEPTH + SHARED, False, last=True)

        @block.vector
        def _(dve):
            dve.wait_ge(loaded, LOADS)
            dve.memset(half[:, :], -0.5).then_inc(halves, 1)
            dve.memset(phalf[:, :], 0.5).then_inc(halves, 1)
            dve.memset(ones[:, :], 1.0).then_inc(halves, 1)
            dve.tensor_copy(identb[:, :], ident[:, :]).then_inc(halves, 1)
            dve.memset(one[:, :], 1.0).then_inc(halves, 1)
            dve.memset(magic[:, :], MAGIC).then_inc(halves, 1)
            for n, s in enumerate((wa_lo, wb_lo, b2_added)):
                dve.memset(yvar[:, n:n + 1], 0.0).then_inc(s, 1)

            def split_in(gc, part=slice(0, 2048)):
                dve.wait_ge(wa_hi, gc + 1)
                dve.tensor_tensor(WA[:, 1, part], rawA[:, part], f(WA[:, 0, part]), ALU.subtract).then_inc(wa_lo, 1)

            def split_in_half(gc, n):
                dve.wait_ge(wa_lo_pool, n + 1)
                split_in(gc, slice(1024, 2048))

            def split_out(gc, cols):
                dve.wait_ge(wb_hi, gc + 1)
                dve.tensor_tensor(WB[:, 1, 0:cols], rawB[:, 0:cols], f(WB[:, 0, 0:cols]), ALU.subtract).then_inc(wb_lo, 1)

            def ln_stats(norm):
                b = norm[1]
                for t in range(TT):
                    ins = dve.bn_stats(stats[:, t, :], X[:, b * TT + t, :])
                ins.then_inc(ln_dve, 1)

            def ln_var(norm):
                n = norm[0]
                dve.wait_ge(ln_dve, at(n, LN_DVE, "stats"))
                dve.memset(ve[:, :], 0.0)
                for t in range(TT):
                    ins = dve.bn_aggr(mv[:, t, :], stats[:, t, :])
                ins.then_inc(ln_dve, 1)
                dve.wait_ge(ln_dve, at(n, LN_DVE, "aggr"))
                dve.tensor_scalar(ve[:, :], mv[:, :, 1], EPS, None, ALU.add).then_inc(ln_dve, 1)

            def ln_rows(norm):
                n, b = norm
                dve.wait_ge(ln_pool, at(n, LN_POOL, "rstd"))
                for t in range(TT):
                    ins = dve.tensor_scalar(xn[:, t, :], X[:, b * TT + t, :], mv[:, t, 0:1], rstd[:, t:t + 1],
                                            ALU.subtract, ALU.mult)
                ins.then_inc(ln_dve, 1)

            def ln_low(norm, tiles=range(KT)):
                n, b = norm
                for k in tiles:
                    dve.wait_ge(ln_act, at(n, LN_ACT, f"h{k}"))
                    dve.tensor_tensor(XT[:, 1, b, k, :], xtmp[:, k % 2, :], f(XT[:, 0, b, k, :]), ALU.subtract).then_inc(ln_dve, 1)

            def low(dst, full, hi):
                return dve.tensor_tensor(dst, full, f(hi), ALU.subtract)

            def attn_chunk(base, gc, c, lc, ln0=None, ln_next=None, layer=None):
                chunk0 = ln0 is not None
                for b in range(BATCH):
                    i = base + b
                    first = chunk0 and b == 0
                    norm = norm_beside(b, ln0, ln_next)
                    out_banks = OUT_BANKS_ATTN if norm else OUT_BANKS
                    if norm:
                        ln_stats(norm)
                        ln_var(norm)
                    if not first:
                        attn_norm_mean(i - 1)
                    dve.wait_ge(a_act, at(i, A_ACT, "q"))
                    low(qT[:, 1, :], bank[0][:, :], qT[:, 0, :]).then_inc(a_dve, 1)
                    if not first:
                        attn_norm_var(i - 1, c - 1 if b == 0 else c)
                    dve.wait_ge(a_act, at(i, A_ACT, "k"))
                    low(kT[:, 1, :], bank[1][:, :], kT[:, 0, :]).then_inc(a_dve, 1)
                    if norm:
                        ln_rows(norm)
                    if not first:
                        attn_norm_scale(i - 1)
                    attn_mask(i, 0)
                    attn_scores_low(i, 0, 0)
                    if not first:
                        attn_gate(i - 1)
                    attn_scores_low(i, 0, 1)
                    if not first:
                        attn_tail_lo(i - 1)
                    dve.wait_ge(a_pe, at(i, A_PE, "vt"))
                    dve.tensor_tensor(vdec.rearrange("p (t r n) -> p t r n", t=TT, r=2),
                                      bank[5][:, :].rearrange("p (t r n) -> p t r n", t=TT, r=2),
                                      dec[:, bass.ds(c, 1), 0, :, :].rearrange("p o t r -> p (o t) r").unsqueeze(3).to_broadcast([P, TT, 2, HEAD]),
                                      ALU.mult).then_inc(a_dve, 1)
                    for pair in (1, 2):
                        attn_mask(i, pair)
                        attn_scores_low(i, pair, 0)
                        attn_scores_low(i, pair, 1)
                    if b == BATCH - 1 and not norm:
                        split_in_half(gc + 1, lc)
                    if not first:
                        attn_tail_out(i - 1, (b - 1) % BATCH, (0, 1), out_banks)
                    if norm:
                        ln_low(norm, range(0, 2))
                    if not first:
                        attn_tail_out(i - 1, (b - 1) % BATCH, (2, 3), out_banks)
                    if norm:
                        ln_low(norm, range(2, KT))
                    if b == BATCH - 1 and norm:
                        split_in_half(gc + 1, lc)
                    if b == 0:
                        split_out(gc, DIM)

            def attn_mask(i, pair):
                for r in range(2):
                    dve.wait_ge(a_pe, at(i, A_PE, f"s{2 * pair + r}"))
                    for m in SCORE_TILES[pair]:
                        tile = bank[SCORES_BANK[pair] + r][:, MASK_AT[m] - SCORES_AT[pair]:MASK_AT[m] - SCORES_AT[pair] + P]
                        ins = dve.tensor_tensor(tile, tile, causal[:, :], ALU.mult)
                    ins.then_inc(a_dve, 1)

            def attn_scores_low(i, pair, r):
                dve.wait_ge(a_act, at(i, A_ACT, f"s{2 * pair + r}"))
                col, n = SCORES_AT[pair], SCORES_N[pair]
                low(S[:, r, 1, col:col + n], bank[SCORES_BANK[pair] + r][:, 0:n], S[:, r, 0, col:col + n]).then_inc(a_dve, 1)

            y8 = y.rearrange("p (g n) -> p g n", n=HEAD)

            def attn_norm_mean(i):
                dve.wait_ge(n_act, at(i, N_ACT, "ylow"))
                for r in range(2):
                    ins = dve.tensor_tensor(y.rearrange("p (t r n) -> p t r n", t=TT, r=2)[:, :, r, :],
                                            bank[2 + r][:, :].rearrange("p (t s n) -> p t s n", t=TT, s=2)[:, :, 0, :],
                                            ylow[:, :, r, :], ALU.add)
                ins.then_inc(n_dve, 1)
                dve.wait_ge(n_dve, at(i, N_DVE, "y"))
                dve.tensor_reduce(ysum[:, :], y8, AX.X, ALU.add).then_inc(n_dve, 1)
                dve.wait_ge(n_dve, at(i, N_DVE, "ysum"))
                dve.tensor_scalar(ymean[:, :], ysum[:, :], 1.0 / HEAD, None, ALU.mult).then_inc(n_dve, 1)
                dve.wait_ge(n_dve, at(i, N_DVE, "ymean"))
                dve.tensor_tensor(y8, y8, ymean[:, :].unsqueeze(2).to_broadcast([P, 8, HEAD]), ALU.subtract).then_inc(n_dve, 1)

            def attn_norm_var(i, c):
                dve.wait_ge(n_act, at(i, N_ACT, "ysq"))
                dve.tensor_reduce(yssq[:, :], ysq.rearrange("p (g n) -> p g n", n=HEAD), AX.X, ALU.add).then_inc(n_dve, 1)
                dve.wait_ge(n_dve, at(i, N_DVE, "ysq"))
                dve.scalar_tensor_tensor(out=yvar[:, :], in0=yssq[:, :], scalar=1.0 / HEAD,
                                         in1=dec[:, bass.ds(c, 1), 1, :, :].rearrange("p o t r -> p (o t r)"),
                                         op0=ALU.mult, op1=ALU.add).then_inc(n_dve, 1)

            def attn_norm_scale(i):
                dve.wait_ge(n_pool, at(i, N_POOL, "rstd"))
                dve.tensor_tensor(y8, y8, yrs[:, :].unsqueeze(2).to_broadcast([P, 8, HEAD]), ALU.mult).then_inc(n_dve, 1)

            def attn_gate(i):
                dve.wait_ge(at_act, at(i, AT_ACT, "t"))
                dve.tensor_tensor(gt, gt, sg, ALU.mult).then_inc(at_dve, 1)

            def attn_tail_lo(i):
                dve.wait_ge(at_act, at(i, AT_ACT, "hi"))
                low(gated[:, 1, :], gt, gated[:, 0, :]).then_inc(at_dve, 1)

            def attn_tail_out(i, b, tiles, banks):
                for t in tiles:
                    dve.wait_ge(at_pe, at(i, AT_PE, f"o{t}"))
                    dve.tensor_tensor(X[:, b * TT + t, :], X[:, b * TT + t, :], bank[banks[t]][:, :], ALU.add).then_inc(at_dve, 1)

            def ffn_chunk(base, gc, layer, ln0=None, ln_next=None, attn_last=None):
                chunk0 = ln0 is not None
                for b in range(BATCH):
                    i = base + b
                    first = chunk0 and b == 0
                    norm = norm_beside(b, ln0, ln_next)
                    if first:
                        attn_norm_mean(attn_last)
                        attn_norm_var(attn_last, LAST)
                        ln_stats(norm)
                        attn_norm_scale(attn_last)
                        ln_var(norm)
                        attn_gate(attn_last)
                        ln_rows(norm)
                        attn_tail_lo(attn_last)
                    elif norm:
                        ln_stats(norm)
                        ln_var(norm)
                        ln_rows(norm)
                        if chunk0:
                            add_b2(layer, b + 1, ln0 + b + 1)
                    for ft in range(FT):
                        dve.wait_ge(f_pool, at(i, F_POOL, f"hi{ft}"))
                        low(H[:, b % 2, 1, ft, :], hid[:, ft, :], H[:, b % 2, 0, ft, :]).then_inc(f_dve, 1)
                    if first:
                        attn_tail_out(attn_last, BATCH - 1, (0, 1), OUT_BANKS_FFN)
                        ln_low(norm, range(0, 2))
                        attn_tail_out(attn_last, BATCH - 1, (2, 3), OUT_BANKS_FFN)
                        ln_low(norm, range(2, KT))
                        add_b2(layer, 0, norm[0] - 1)
                        add_b2(layer, 1, norm[0])
                    else:
                        if norm:
                            ln_low(norm, range(0, 2))
                        ffn_tail(i - 1, (b - 1) % BATCH, (0,))
                        if b == BATCH - 1:
                            split_in(gc + 1)
                        ffn_tail(i - 1, (b - 1) % BATCH, (1,))
                        if norm:
                            ln_low(norm, range(2, KT))
                        ffn_tail(i - 1, (b - 1) % BATCH, (2, 3))
                    if b == 0:
                        split_out(gc, 2048)

            def ffn_tail(i, b, tiles=range(TT)):
                for t in tiles:
                    dve.wait_ge(ft_pe, at(i, FT_PE, f"o{t}"))
                    dve.tensor_tensor(X[:, b * TT + t, :], X[:, b * TT + t, :], bank[6 + t % 2][:, :], ALU.add).then_inc(ft_dve, 1)

            def add_b2(layer, b, n):
                dve.wait_ge(b2_in, 16 * (layer + 1))
                dve.wait_ge(ln_dve, at(n, LN_DVE, "xn"))
                dve.tensor_tensor(X[:, b * TT:(b + 1) * TT, :], X[:, b * TT:(b + 1) * TT, :],
                                  b2row[:, :].unsqueeze(1).to_broadcast([P, TT, DIM]), ALU.add).then_inc(b2_added, 1)

            def input_norm(group, batches):
                stats_, mv_, ve_, rstd_ = first_norm(batches)
                for b in batches:
                    dve.wait_ge(x_in[b], 16)
                    for t in range(TT):
                        ins = dve.bn_stats(stats_[:, (b - batches[0]) * TT + t, :], X[:, b * TT + t, :])
                ins.then_inc(i_dve, 1)
                dve.wait_ge(i_dve, at(group, I_DVE, "stats"))
                for t in range(len(batches) * TT):
                    ins = dve.bn_aggr(mv_[:, t, :], stats_[:, t, :])
                ins.then_inc(i_dve, 1)
                dve.wait_ge(i_dve, at(group, I_DVE, "aggr"))
                dve.tensor_scalar(ve_, mv_[:, :, 1], EPS, None, ALU.add).then_inc(i_dve, 1)
                dve.wait_ge(i_pool, group + 1)
                for t in range(len(batches) * TT):
                    Xt = X[:, batches[0] * TT + t, :]
                    ins = dve.tensor_scalar(Xt, Xt, mv_[:, t, 0:1], rstd_[:, t:t + 1], ALU.subtract, ALU.mult)
                ins.then_inc(i_dve, 1)

            input_norm(0, [0])
            dve.wait_ge(i_dve, at(0, I_DVE, "xn"))
            ln_stats((0, 0))
            ln_var((0, 0))
            split_in(0)
            ln_rows((0, 0))
            ln_low((0, 0))
            input_norm(1, [1, 2, 3])
            dve.wait_ge(i_dve, at(1, I_DVE, "xn"))

            with dve.Fori(0, LAYERS) as layer:
                base, gc, ln0 = layer * NITEM, layer * 2 * CHUNKS, layer * 2 * BATCH
                attn_chunk(base, gc, 0, layer * CHUNKS, ln0=ln0)
                with dve.Fori(1, LAST) as c:
                    attn_chunk(base + c * BATCH, gc + c, c, layer * CHUNKS + c)
                attn_chunk(base + LAST * BATCH, gc + LAST, LAST, layer * CHUNKS + LAST, ln_next=ln0 + BATCH, layer=layer)
                ffn_chunk(base, gc + CHUNKS, layer, ln0=ln0 + BATCH, attn_last=base + NITEM - 1)
                with dve.Fori(1, LAST) as c:
                    ffn_chunk(base + c * BATCH, gc + CHUNKS + c, layer)
                ffn_chunk(base + LAST * BATCH, gc + CHUNKS + LAST, layer, ln_next=ln0 + 2 * BATCH)
                ffn_tail(base + NITEM - 1, BATCH - 1)

            def quant_pair(p, s):
                K = QK[s]
                D = K * P

                def done(u, name):
                    dve.wait_ge(q_dve[u], at(p, Q_DVE, f"{name}_{s}"))

                def pe_done(u, name):
                    dve.wait_ge(q_pe[u], at(p, Q_PE, f"{name}_{s}"))

                def largest(u, row, steps, n, width):
                    for j in range(n):
                        pe_done(u, f"{steps}{j}")
                        dve.tensor_reduce(qs[:, u, row, j:j + 1], bank[4 * u + j][:, 0:width], AX.X, ALU.max,
                                          apply_absolute_value=True).then_inc(q_dve[u], 1)

                def row_scales(u, side, most, scale, recip):
                    done(u, f"{side}t3")
                    dve.tensor_scalar(qs[:, u, scale, :], qs[:, u, most, :], QEPS, 1.0 / QMAX, ALU.max, ALU.mult).then_inc(q_dve[u], 1)
                    done(u, f"{side}scale")
                    dve.reciprocal(qs[:, u, recip, :], qs[:, u, scale, :]).then_inc(q_dve[u], 1)

                def integers(u, side, rows):
                    dve.wait_ge(q_act[u], at(p, Q_ACT, f"{side}r3_{s}"))
                    dve.tensor_scalar(q_int[u][:, :, 0:D], rows[:, :, 0:D], MAGIC, None, ALU.subtract).then_inc(q_dve[u], 1)

                def clip(u, dst, steps):
                    for k in range(K):
                        pe_done(u, f"{steps}{k}")
                        dve.tensor_scalar(dst[:, k, :], bank[4 * u + k].bitcast(bf16)[:, 0:SEQ], QMAX, -QMAX,
                                          ALU.min, ALU.max).then_inc(q_dve[u], 1)

                if s == 1:
                    for u in range(2):
                        dve.memset(scratch[:, u:u + 1], 0.0).then_inc(q_dve[u], 1)
                def ratio(u):
                    largest(u, AX_, "x", K, SEQ)
                    done(u, f"x{K - 1}")
                    dve.tensor_scalar(qs[:, u, AX_:AW + 1, 0:K], qs[:, u, AX_:AW + 1, 0:K], QEPS, None, ALU.max).then_inc(q_dve[u], 1)
                    done(u, "max")
                    dve.reciprocal(qs[:, u, WI, 0:K], qs[:, u, AW, 0:K]).then_inc(q_dve[u], 1)
                    done(u, "winv")
                    dve.tensor_tensor(qs[:, u, RA, 0:K], qs[:, u, AX_, 0:K], qs[:, u, WI, 0:K], ALU.mult).then_inc(q_dve[u], 1)

                def smoothing(u):
                    dve.wait_ge(q_pool[u], at(p, Q_POOL, f"s_{s}"))
                    dve.tensor_scalar(qs[:, u, S_, 0:K], qs[:, u, S_, 0:K], QEPS, None, ALU.max).then_inc(q_dve[u], 1)
                    done(u, "s")
                    dve.reciprocal(qs[:, u, RS, 0:K], qs[:, u, S_, 0:K]).then_inc(q_dve[u], 1)

                if s == 1:
                    quant_add(p, 0)
                    quant_var(p, 0)
                    largest(0, AW, "w", K, SEQ)
                    quant_scale(p, 0)
                    quant_add(p, 1)
                    quant_var(p, 1)
                    ratio(0)
                    largest(1, AW, "w", K, SEQ)
                    smoothing(0)
                    quant_scale(p, 1)
                    ratio(1)
                    smoothing(1)
                else:
                    largest(0, AW, "w", K, SEQ)
                    largest(1, AW, "w", K, SEQ)
                    ratio(0)
                    ratio(1)
                    smoothing(0)
                    smoothing(1)
                for u in range(2):
                    largest(u, XM, "xt", TT, D)
                    row_scales(u, "x", XM, XS, XR)
                for u in range(2):
                    integers(u, "x", q_x[u])
                for u in range(2):
                    clip(u, q_xT[u], "xq")
                for u in range(2):
                    largest(u, WM, "wt", TT, D)
                    row_scales(u, "w", WM, WS, WR)
                for u in range(2):
                    integers(u, "w", q_rows[u][s])
                for u in range(2):
                    clip(u, q_wT[u], "wq")
                for u in range(2):
                    dve.wait_ge(q_act[u], at(p, Q_ACT, f"row_{s}"))
                    for t in range(TT):
                        pe_done(u, f"o{t}")
                        dve.scalar_tensor_tensor(out=q_h[u][:, t, :], in0=bank[4 * u + t][:, :], scalar=qs[:, u, XS, t:t + 1],
                                                 in1=q_row[u], op0=ALU.mult, op1=ALU.mult).then_inc(q_dve[u], 1)
                if s == 2:
                    for u in range(2):
                        Xb = X[:, bass.ds((p * 2 + u) * TT + 2, 2), :]
                        done(u, "o3")
                        dve.tensor_tensor(Xb, Xb, q_h[u][:, 2:4, :], ALU.add).then_inc(q_dve[u], 1)

            def quant_add(p, u):
                Xb = X[:, bass.ds((p * 2 + u) * TT + 2, 2), :]
                dve.wait_ge(x0_in[u], 16 * (p + 1))
                dve.tensor_tensor(Xb, Xb, q_x0[u][:, 2:4, :], ALU.add).then_inc(q_dve[u], 1)

            def quant_var(p, u):
                stats_, mv_, ve_, rstd_ = q_norm[u]
                dve.wait_ge(q_dve[u], at(p, Q_DVE, "x0_1"))
                dve.memset(scratch[:, 4 + u:5 + u], 0.0)
                dve.wait_ge(q_pool[u], at(p, Q_POOL, "x0"))
                dve.memset(scratch[:, 6 + u:7 + u], 0.0)
                for t in range(TT):
                    ins = dve.bn_stats(stats_[:, t, :], X[:, bass.ds((p * 2 + u) * TT + t, 1), :].rearrange("p o n -> p (o n)"))
                ins.then_inc(q_dve[u], 1)
                dve.wait_ge(q_dve[u], at(p, Q_DVE, "stats_1"))
                dve.memset(ve_, 0.0)
                for t in range(TT):
                    ins = dve.bn_aggr(mv_[:, t, :], stats_[:, t, :])
                ins.then_inc(q_dve[u], 1)
                dve.wait_ge(q_dve[u], at(p, Q_DVE, "aggr_1"))
                dve.tensor_scalar(ve_, mv_[:, :, 1], EPS, None, ALU.add).then_inc(q_dve[u], 1)

            def quant_scale(p, u):
                _, mv_, _, rstd_ = q_norm[u]
                dve.wait_ge(q_pool[u], at(p, Q_POOL, "rstd"))
                for t in range(TT):
                    ins = dve.tensor_scalar(q_x[u][:, t, :], X[:, bass.ds((p * 2 + u) * TT + t, 1), :].rearrange("p o n -> p (o n)"),
                                            mv_[:, t, 0:1], rstd_[:, t:t + 1], ALU.subtract, ALU.mult)
                ins.then_inc(q_dve[u], 1)

            with dve.Fori(0, BATCH // 2) as p:
                quant_pair(p, 1)
                quant_pair(p, 2)

            def mlp_chunk(base, gc, chunk0, routed=False):
                for b in range(BATCH):
                    i = base + b
                    norm = (LN_LAST + b + 1, b + 1) if chunk0 and b + 1 < BATCH else None
                    tail = not (chunk0 and b == 0)

                    def product(ft):
                        dve.wait_ge(g_pe, at(i, G_PE, f"u{ft}"))
                        dve.wait_ge(g_act, at(i, G_ACT, f"g{ft}"))
                        dve.tensor_tensor(hid[:, ft, :], hid[:, ft, :], bank[2 * ft + 1][:, :], ALU.mult).then_inc(g_dve, 1)

                    def product_low(ft):
                        dve.wait_ge(g_pool, at(i, G_POOL, f"hi{ft}"))
                        low(G[:, b % 2, 1, ft, :], hid[:, ft, :], G[:, b % 2, 0, ft, :]).then_inc(g_dve, 1)

                    if norm:
                        ln_stats(norm)
                        ln_var(norm)
                        ln_rows(norm)
                    def next_low(ft):
                        if b == BATCH - 1 and not routed:
                            dve.wait_ge(*((wg_hi, gc - ADEPTH + 1), (wa_hi, gc + 2))[ft])
                            dve.tensor_tensor(w_cols(WA[:, 1, :], ft), w_cols(rawA[:, :], ft), f(w_cols(WA[:, 0, :], ft)),
                                              ALU.subtract).then_inc((wg_lo, wa_lo)[ft], 1)

                    product(0)
                    product_low(0)
                    next_low(0)
                    product(1)
                    if norm:
                        ln_low(norm, range(0, 2))
                    if tail:
                        mlp_tail(i - 1, (b - 1) % BATCH, routed and b > 0, (0, 1))
                    product_low(1)
                    next_low(1)
                    if norm:
                        ln_low(norm, range(2, KT))
                    if tail:
                        mlp_tail(i - 1, (b - 1) % BATCH, routed and b > 0, (2, 3))
                    if b == 0:
                        split_out(gc, 1024)

            def mlp_tail(i, b, routed, tiles=range(TT)):
                for t in tiles:
                    dve.wait_ge(gt_pe, at(i, GT_PE, f"o{t}"))
                    Xt = X[:, b * TT + t, :]
                    if routed:
                        dve.scalar_tensor_tensor(out=Xt, in0=bank[6 + t % 2][:, :], scalar=rt[:, 5, b * TT + t:b * TT + t + 1],
                                                 in1=Xt, op0=ALU.mult, op1=ALU.add).then_inc(gt_dve, 1)
                    else:
                        dve.tensor_tensor(Xt, Xt, bank[6 + t % 2][:, :], ALU.add).then_inc(gt_dve, 1)

            dve.wait_ge(r_hi, 1)
            dve.tensor_tensor(R[:, 1, :, :], Rraw[:, :, :], f(R[:, 0, :, :]), ALU.subtract).then_inc(r_dve, 1)
            dve.wait_ge(q_pool[0], len(Q_POOL))
            ln_stats((LN_LAST, 0))
            ln_var((LN_LAST, 0))
            ln_rows((LN_LAST, 0))
            for u in range(2):
                dve.wait_ge(q_pool[u], BATCH // 2 * len(Q_POOL))
            ln_low((LN_LAST, 0))
            mlp_chunk(0, ADEPTH, True)
            dve.wait_ge(r_pe, at(0, R_PE, "t"))
            dve.tensor_copy(lg[:, :, :].rearrange("p t n -> p (t n)"), bank[4][:, 0:BATCH * TT * EXPERTS]).then_inc(r_dve, 1)
            dve.wait_ge(r_dve, at(0, R_DVE, "logits"))
            for t in range(BATCH * TT):
                ins = dve.max(top[:, t, :], lg[:, t, :])
            ins.then_inc(r_dve, 1)
            dve.wait_ge(r_dve, at(0, R_DVE, "top"))
            dve.tensor_tensor(rt[:, 0, :], top[:, :, 1], top[:, :, 0], ALU.subtract).then_inc(r_dve, 1)
            dve.wait_ge(r_act, at(0, R_ACT, "exp"))
            dve.tensor_scalar(rt[:, 2, :], rt[:, 1, :], 1.0, None, ALU.add).then_inc(r_dve, 1)
            dve.wait_ge(r_dve, at(0, R_DVE, "den"))
            dve.reciprocal(rt[:, 3, :], rt[:, 2, :]).then_inc(r_dve, 1)
            dve.wait_ge(r_dve, at(0, R_DVE, "rden"))
            dve.tensor_tensor(rt[:, 4, :], rt[:, 1, :], rt[:, 3, :], ALU.mult).then_inc(r_dve, 1)
            dve.wait_ge(r_dve, at(0, R_DVE, "w2"))
            dve.tensor_tensor(rt[:, 5, :], rt[:, 3, :], rt[:, 4, :], ALU.add).then_inc(r_dve, 1)
            dve.wait_ge(r_dve, at(0, R_DVE, "comb"))
            with dve.Fori(1, SHARED) as j:
                mlp_chunk(j * BATCH, ADEPTH + j, False)
            mlp_chunk(SHARED * BATCH, ADEPTH + SHARED, False, routed=True)
            mlp_tail(GITEM - 1, BATCH - 1, True)

        @block.gpsimd
        def _(pool):
            pool.wait_ge(loaded, LOADS)
            pool.wait_ge(halves, 6)

            def round_high(hi, full):
                return pool.tensor_tensor(hi, full, one[:, 0:1].to_broadcast([P, SEQ]), ALU.mult)

            def ln_rstd(n):
                pool.wait_ge(ln_dve, at(n, LN_DVE, "vareps"))
                pool.tensor_tensor(rstd[:, :], ve[:, :], half[:, 0:TT], ALU.pow).then_inc(ln_pool, 1)

            def attn_norm_rstd(i):
                pool.wait_ge(n_dve, at(i, N_DVE, "yvar"))
                pool.tensor_tensor(yrs[:, :], yvar[:, :], half[:, :], ALU.pow).then_inc(n_pool, 1)

            def attn_chunk(base, gc, lc, ln0=None, ln_next=None):
                for b in range(BATCH):
                    i = base + b
                    norm = norm_beside(b, ln0, ln_next)
                    if norm:
                        ln_rstd(norm[0])
                    if not (ln0 is not None and b == 0):
                        attn_norm_rstd(i - 1)
                    if b == BATCH - 1:
                        pool.wait_ge(rawA_in, 16 * (gc + 2))
                        pool.wait_ge(a_pe, at(i, A_PE, "g"))
                        pool.tensor_tensor(WA[:, 0, 0:1024], rawA[:, 0:1024], one[:, 0:1].to_broadcast([P, 1024]),
                                           ALU.mult).then_inc(wa_hi_pool, 1)
                    pool.wait_ge(a_act, at(i, A_ACT, "vhi"))
                    v8 = vH.rearrange("p t r s n -> p (t r) s n")
                    pool.tensor_tensor(v8[:, :, 1, :], vdec.rearrange("p (g n) -> p g n", n=HEAD), f(v8[:, :, 0, :]),
                                       ALU.subtract).then_inc(a_pool, 1)
                    if b == BATCH - 1:
                        pool.wait_ge(wa_hi_pool, lc + 1)
                        pool.tensor_tensor(WA[:, 1, 0:1024], rawA[:, 0:1024], f(WA[:, 0, 0:1024]),
                                           ALU.subtract).then_inc(wa_lo_pool, 1)

            def ffn_chunk(base, ln0=None, ln_next=None, attn_last=None):
                for b in range(BATCH):
                    i = base + b
                    first = ln0 is not None and b == 0
                    norm = norm_beside(b, ln0, ln_next)
                    if first:
                        attn_norm_rstd(attn_last)
                    if norm:
                        ln_rstd(norm[0])
                    for ft in range(FT):
                        pool.wait_ge(f_act, at(i, F_ACT, f"h{ft}"))
                        if ft == 0 and not (ln0 is not None and b < 2):
                            pool.wait_ge(ft_pe, at(i - 2, FT_PE, "o3"))
                        round_high(H[:, b % 2, 0, ft, :], hid[:, ft, :]).then_inc(f_pool, 1)

            def input_rstd(group, batches):
                _, _, ve_, rstd_ = first_norm(batches)
                pool.wait_ge(i_dve, at(group, I_DVE, "vareps"))
                pool.tensor_tensor(rstd_, ve_, half[:, 0:1].to_broadcast([P, len(batches) * TT]), ALU.pow).then_inc(i_pool, 1)

            input_rstd(0, [0])
            ln_rstd(0)
            input_rstd(1, [1, 2, 3])

            with pool.Fori(0, LAYERS) as layer:
                base, gc, ln0 = layer * NITEM, layer * 2 * CHUNKS, layer * 2 * BATCH
                attn_chunk(base, gc, layer * CHUNKS, ln0=ln0)
                with pool.Fori(1, LAST) as c:
                    attn_chunk(base + c * BATCH, gc + c, layer * CHUNKS + c)
                attn_chunk(base + LAST * BATCH, gc + LAST, layer * CHUNKS + LAST, ln_next=ln0 + BATCH)
                ffn_chunk(base, ln0=ln0 + BATCH, attn_last=base + NITEM - 1)
                with pool.Fori(1, LAST) as c:
                    ffn_chunk(base + c * BATCH)
                ffn_chunk(base + LAST * BATCH, ln_next=ln0 + 2 * BATCH)

            def quant_diagonals(p, u, s):
                pool.wait_ge(q_dve[u], at(p, Q_DVE, f"wscale_{s}"))
                pool.tensor_tensor(q_diag[u], ident[:, :].unsqueeze(1).to_broadcast([P, TT, P]),
                                   qs[:, u, WS, :].unsqueeze(2).to_broadcast([P, TT, P]), ALU.mult).then_inc(q_pool[u], 1)

            def quant_ratio_root(p, u, s):
                K = QK[s]
                pool.wait_ge(q_dve[u], at(p, Q_DVE, f"ratio_{s}"))
                pool.tensor_tensor(qs[:, u, S_, 0:K], qs[:, u, RA, 0:K], phalf[:, 0:K], ALU.pow).then_inc(q_pool[u], 1)

            pool.wait_ge(ft_dve, LAYERS * NITEM * len(FT_DVE))
            with pool.Fori(0, BATCH // 2) as p:
                for u in range(2):
                    Xb = X[:, bass.ds((p * 2 + u) * TT, 2), :]
                    pool.wait_ge(x0_in[u], 16 * (p + 1))
                    pool.tensor_tensor(scratch[:, 8 + u:9 + u], one[:, :], one[:, :], ALU.add)
                    pool.tensor_tensor(Xb, Xb, q_x0[u][:, 0:2, :], ALU.add).then_inc(q_pool[u], 1)
                for u in range(2):
                    _, _, ve_, rstd_ = q_norm[u]
                    pool.wait_ge(q_dve[u], at(p, Q_DVE, "vareps_1"))
                    pool.tensor_tensor(rstd_, ve_, half[:, 0:TT], ALU.pow).then_inc(q_pool[u], 1)
                for u in range(2):
                    quant_ratio_root(p, u, 1)
                for u in range(2):
                    quant_diagonals(p, u, 1)
                for u in range(2):
                    pool.wait_ge(q_act[u], at(p, Q_ACT, "silu_1"))
                    a = q_x[u][:, :, 0:QI]
                    pool.tensor_tensor(a, a, q_h[u][:, :, QI:QO], ALU.mult).then_inc(q_pool[u], 1)
                for u in range(2):
                    quant_ratio_root(p, u, 2)
                for u in range(2):
                    quant_diagonals(p, u, 2)
                for u in range(2):
                    Xb = X[:, bass.ds((p * 2 + u) * TT, 2), :]
                    pool.wait_ge(q_dve[u], at(p, Q_DVE, "o3_2"))
                    pool.tensor_tensor(scratch[:, 2 + u:3 + u], one[:, :], one[:, :], ALU.add)
                    pool.tensor_tensor(Xb, Xb, q_h[u][:, 0:2, :], ALU.add).then_inc(q_pool[u], 1)

            def mlp_chunk(base, chunk0):
                for b in range(BATCH):
                    i = base + b
                    if chunk0 and b + 1 < BATCH:
                        ln_rstd(LN_LAST + b + 1)
                    for ft in range(2):
                        pool.wait_ge(g_dve, at(i, G_DVE, f"p{ft}"))
                        if ft == 0 and not (chunk0 and b < 2):
                            pool.wait_ge(gt_pe, at(i - 2, GT_PE, "o3"))
                        round_high(G[:, b % 2, 0, ft, :], hid[:, ft, :]).then_inc(g_pool, 1)

            ln_rstd(LN_LAST)
            mlp_chunk(0, True)
            with pool.Fori(1, SHARED) as j:
                mlp_chunk(j * BATCH, False)
            mlp_chunk(SHARED * BATCH, False)


def kernel(**inputs):
    import numpy as np
    import concourse.bacc as bacc
    from concourse.bass_utils import run_bass_kernel_spmd as run

    I = {k: np.asarray(v) for k, v in inputs.items()}

    def column_blocks(w, n):
        K, N = w.shape
        return w.reshape(K // P, P, N // n, n).transpose(2, 1, 0, 3).reshape(N // n, P, K // P * n)

    def row_blocks(w, k):
        K, N = w.shape
        return w.reshape(K // k, k // P, P, N).transpose(0, 2, 1, 3).reshape(K // k, P, k // P * N)

    def columns(v):
        return v.reshape(-1, P).T

    L = range(LAYERS)
    arrays = {
        "x_rows": I["x"].reshape(BATCH * SEQ, DIM),
        "wa_attn": np.concatenate([np.stack([column_blocks(I["L0_attn_W" + r][l], P) for r in "qkvg"], 2)
                                   .reshape(CHUNKS, P, -1) for l in L]),
        "wb_attn": np.concatenate([row_blocks(I["L0_attn_Wo"][l], P) for l in L]),
        "wa_ffn": np.concatenate([column_blocks(I["L0_attn_W1"][l], FF // CHUNKS) for l in L]),
        "wb_ffn": np.concatenate([row_blocks(I["L0_attn_W2"][l], FF // CHUNKS) for l in L]),
        "param_columns": np.concatenate([columns(I["L0_attn_" + n]) for n in
                                         ("ln_gamma", "ln_beta", "gn_gamma", "gn_beta", "b1")], 1),
        "b2": I["L0_attn_b2"],
    }
    gammas = (1.0 - np.exp(np.linspace(np.log(1.0 / 32), np.log(1.0 / 128), HEADS))).astype(np.float32)
    steps = np.arange(SEQ) - SEQ // 2
    decay = np.stack([gammas.astype(np.float64)[:, None] ** -steps, EPS * gammas.astype(np.float64)[:, None] ** (-2 * steps)])
    arrays["consts"] = np.concatenate([np.eye(P), np.triu(np.ones((P, P)))], 1).astype(np.float32)
    arrays["decays"] = (decay.reshape(2, CHUNKS, 2, TT, P).transpose(4, 1, 0, 3, 2)
                        .reshape(P, -1).astype(np.float32))
    arrays["quant_w"] = np.stack([row_blocks(w, QO)[0] for w in I["fside_BxS2xS2_0"]])
    arrays["quant_ctx"] = np.stack([row_blocks(w, DIM)[0] for w in I["ctx_1024"]])
    gate, up = (np.concatenate([column_blocks(I["L0_ffn_" + p + n].T, GW) for p in ("sh_", "r_")]) for n in ("gate", "up"))
    arrays["wa_mlp"] = np.concatenate([gate, up], 2)
    arrays["wb_mlp"] = np.concatenate([row_blocks(I["L0_ffn_" + p + "down"].T, GW) for p in ("sh_", "r_")])
    arrays["router_w"] = column_blocks(I["L0_ffn_router_weight"].T, EXPERTS)[0]

    nc = bacc.Bacc("TRN2", target_bir_lowering=False, num_devices=1)
    arrays = {k + "_dram": np.ascontiguousarray(v) for k, v in arrays.items()}
    args = [nc.dram_tensor(k, v.shape, mybir.dt.from_np(v.dtype), kind="ExternalInput").ap() for k, v in arrays.items()]
    out = nc.dram_tensor("out_dram", (BATCH * SEQ, DIM), mybir.dt.float32, kind="ExternalOutput").ap()
    decoder_kernel(nc, *args, out)
    r = run(nc, [arrays], core_ids=[0])
    return r.results[0]["out_dram"].reshape(BATCH, SEQ, DIM)
```
